# Optimizing a Trainium2 kernel written in Bass

```python
import numpy as np
import jax
import jax.numpy as jnp

def _softmax(x, axis=-1):
    return jax.nn.softmax(x, axis=axis)

def _gelu(x):
    return jax.nn.gelu(x, approximate=True)

def _silu(x):
    return jax.nn.silu(x)

def _sigmoid(x):
    return jax.nn.sigmoid(x)

def _layernorm(x, axis=-1, eps=1e-05):
    m = jnp.mean(x, axis=axis, keepdims=True)
    v = jnp.var(x, axis=axis, keepdims=True)
    return (x - m) / jnp.sqrt(v + eps)

def _scatter_add(tgt, idx, src, axis=0):
    return tgt.at[idx].add(src)

def _segment_sum(src, seg, n):
    return jax.ops.segment_sum(src, seg, n)
kernel_name = 'mk_pixart_seq_d1_seqx_r4_340e06'

def setup_inputs(seed: int=0):
    np.random.seed(seed)
    _w = jnp.asarray

    def _rec_inputs():
        import jax
        import jax.numpy as jnp
        _rk = jax.random.key(seed)
        x = 7.22e-05 + 1 * jax.random.normal(jax.random.fold_in(_rk, 1), (4, 1024, 256), jnp.float32)
        _lenS = 1024 - jax.random.randint(jax.random.fold_in(_rk, 7), (4,), 0, max(1, 1024 // 4) + 1, jnp.int32)
        _lenS2 = 77 - jax.random.randint(jax.random.fold_in(_rk, 8), (4,), 0, max(1, 77 // 4) + 1, jnp.int32)
        cond_1024 = 0.00782532 + 1.00527 * jax.random.normal(jax.random.fold_in(_rk, 11), (4, 256), jnp.float32)
        _ctx_1024P = jax.random.normal(jax.random.fold_in(_rk, 12), (4, 16, 256), jnp.float32)
        _ctx_1024c = jax.random.dirichlet(jax.random.fold_in(_rk, 512), 0.3 * jnp.ones((16,), jnp.float32), (4, 77))
        _ctx_1024t = jnp.einsum('bsk,bkd->bsd', _ctx_1024c, _ctx_1024P)
        _ctx_1024t = _ctx_1024t * jax.lax.rsqrt(jnp.mean(jnp.square(_ctx_1024t)) + 1e-12) * 0.953939
        ctx_1024 = 0.000376506 + 0.999991 * (_ctx_1024t + 0.3 * jax.random.normal(jax.random.fold_in(_rk, 612), (4, 77, 256), jnp.float32))
        _validS = jnp.arange(1024)[None, :] < _lenS[:, None]
        _validS2 = jnp.arange(77)[None, :] < _lenS2[:, None]
        _causal = jnp.tril(jnp.ones((1024, 1024), dtype=bool))
        mask_BxS2_ik0 = jnp.where(jnp.broadcast_to(_validS2[:, :], (4, 77)), 0, 1).astype(jnp.int32)
        return (x, cond_1024, ctx_1024, mask_BxS2_ik0)
    x, cond_1024, ctx_1024, mask_BxS2_ik0 = _rec_inputs()

    def _L0_xcond_setup():
        import jax, jax.numpy as jnp
        import numpy as np
        D = 256
        H = 16
        HD = D // H
        FF = 4 * D
        B, NQ, NK = (8, 256, 128)
        EPS = 1e-05

        def layernorm(x, g, b):
            m = jnp.mean(x, axis=-1, keepdims=True)
            v = jnp.mean(jnp.square(x - m), axis=-1, keepdims=True)
            return (x - m) * jax.lax.rsqrt(v + EPS) * g + b

        def mha(x, ctx, wq, bq, wk, bk, wv, bv, wo, bo, mask=None):
            Bq, Nq, _ = x.shape
            Nk = ctx.shape[1]
            q = (x @ wq + bq).reshape(Bq, Nq, H, HD)
            k = (ctx @ wk + bk).reshape(Bq, Nk, H, HD)
            v = (ctx @ wv + bv).reshape(Bq, Nk, H, HD)
            scores = jnp.einsum('bqhd,bkhd->bhqk', q, k) / np.sqrt(HD)
            if mask is not None:
                scores = jnp.where(mask[:, None, None, :].astype(bool), scores, -jnp.inf)
            attn = jax.nn.softmax(scores.astype(jnp.float32), axis=-1).astype(scores.dtype)
            out = jnp.einsum('bhqk,bkhd->bqhd', attn, v).reshape(Bq, Nq, D)
            return out @ wo + bo
        key = jax.random.key(seed)
        ks = jax.random.split(key, 40)
        rn = lambda k, shape, s=0.02: jax.random.normal(k, shape, jnp.float32) * s
        inp = {'x': jax.random.normal(ks[0], (B, NQ, D), jnp.float32), 't_emb': jax.random.normal(ks[1], (B, D), jnp.float32), 'context_emb': jax.random.normal(ks[2], (B, NK, D), jnp.float32), 'mask': jax.random.randint(ks[3], (B, NK), 0, 2, jnp.int32), 'ln1_g': jnp.ones((D,), jnp.float32), 'ln1_b': jnp.zeros((D,), jnp.float32), 'ln3_g': jnp.ones((D,), jnp.float32), 'ln3_b': jnp.zeros((D,), jnp.float32), 'ln2_g': jnp.ones((D,), jnp.float32), 'ln2_b': jnp.zeros((D,), jnp.float32), 'sa_wq': rn(ks[4], (D, D)), 'sa_bq': jnp.zeros((D,), jnp.float32), 'sa_wk': rn(ks[5], (D, D)), 'sa_bk': jnp.zeros((D,), jnp.float32), 'sa_wv': rn(ks[6], (D, D)), 'sa_bv': jnp.zeros((D,), jnp.float32), 'sa_wo': rn(ks[7], (D, D)), 'sa_bo': jnp.zeros((D,), jnp.float32), 'ca_wq': rn(ks[8], (D, D)), 'ca_bq': jnp.zeros((D,), jnp.float32), 'ca_wk': rn(ks[9], (D, D)), 'ca_bk': jnp.zeros((D,), jnp.float32), 'ca_wv': rn(ks[10], (D, D)), 'ca_bv': jnp.zeros((D,), jnp.float32), 'ca_wo': rn(ks[11], (D, D)), 'ca_bo': jnp.zeros((D,), jnp.float32), 'tp_w': rn(ks[12], (D, 3 * D)), 'tp_b': jnp.zeros((3 * D,), jnp.float32), 'w1': rn(ks[13], (D, FF)), 'b1': jnp.zeros((FF,), jnp.float32), 'w2': rn(ks[14], (FF, D)), 'b2': jnp.zeros((D,), jnp.float32)}
        return inp
    _L0_xcond_all = _L0_xcond_setup()
    _L0_xcond_in = {k: v for k, v in _L0_xcond_all.items() if k in ('ln1_g', 'ln1_b', 'ln3_g', 'ln3_b', 'ln2_g', 'ln2_b', 'sa_wq', 'sa_bq', 'sa_wk', 'sa_bk', 'sa_wv', 'sa_bv', 'sa_wo', 'sa_bo', 'ca_wq', 'ca_bq', 'ca_wk', 'ca_bk', 'ca_wv', 'ca_bv', 'ca_wo', 'ca_bo', 'tp_w', 'tp_b', 'w1', 'b1', 'w2', 'b2')}
    del _L0_xcond_all
    return {'x': x, 'cond_1024': cond_1024, 'ctx_1024': ctx_1024, 'mask_BxS2_ik0': mask_BxS2_ik0, 'L0_xcond_ln1_g': _L0_xcond_in['ln1_g'], 'L0_xcond_ln1_b': _L0_xcond_in['ln1_b'], 'L0_xcond_ln3_g': _L0_xcond_in['ln3_g'], 'L0_xcond_ln3_b': _L0_xcond_in['ln3_b'], 'L0_xcond_ln2_g': _L0_xcond_in['ln2_g'], 'L0_xcond_ln2_b': _L0_xcond_in['ln2_b'], 'L0_xcond_sa_wq': _L0_xcond_in['sa_wq'], 'L0_xcond_sa_bq': _L0_xcond_in['sa_bq'], 'L0_xcond_sa_wk': _L0_xcond_in['sa_wk'], 'L0_xcond_sa_bk': _L0_xcond_in['sa_bk'], 'L0_xcond_sa_wv': _L0_xcond_in['sa_wv'], 'L0_xcond_sa_bv': _L0_xcond_in['sa_bv'], 'L0_xcond_sa_wo': _L0_xcond_in['sa_wo'], 'L0_xcond_sa_bo': _L0_xcond_in['sa_bo'], 'L0_xcond_ca_wq': _L0_xcond_in['ca_wq'], 'L0_xcond_ca_bq': _L0_xcond_in['ca_bq'], 'L0_xcond_ca_wk': _L0_xcond_in['ca_wk'], 'L0_xcond_ca_bk': _L0_xcond_in['ca_bk'], 'L0_xcond_ca_wv': _L0_xcond_in['ca_wv'], 'L0_xcond_ca_bv': _L0_xcond_in['ca_bv'], 'L0_xcond_ca_wo': _L0_xcond_in['ca_wo'], 'L0_xcond_ca_bo': _L0_xcond_in['ca_bo'], 'L0_xcond_tp_w': _L0_xcond_in['tp_w'], 'L0_xcond_tp_b': _L0_xcond_in['tp_b'], 'L0_xcond_w1': _L0_xcond_in['w1'], 'L0_xcond_b1': _L0_xcond_in['b1'], 'L0_xcond_w2': _L0_xcond_in['w2'], 'L0_xcond_b2': _L0_xcond_in['b2']}

def reference(x, cond_1024, ctx_1024, mask_BxS2_ik0, L0_xcond_ln1_g, L0_xcond_ln1_b, L0_xcond_ln3_g, L0_xcond_ln3_b, L0_xcond_ln2_g, L0_xcond_ln2_b, L0_xcond_sa_wq, L0_xcond_sa_bq, L0_xcond_sa_wk, L0_xcond_sa_bk, L0_xcond_sa_wv, L0_xcond_sa_bv, L0_xcond_sa_wo, L0_xcond_sa_bo, L0_xcond_ca_wq, L0_xcond_ca_bq, L0_xcond_ca_wk, L0_xcond_ca_bk, L0_xcond_ca_wv, L0_xcond_ca_bv, L0_xcond_ca_wo, L0_xcond_ca_bo, L0_xcond_tp_w, L0_xcond_tp_b, L0_xcond_w1, L0_xcond_b1, L0_xcond_w2, L0_xcond_b2):
    import jax
    import jax.numpy as jnp

    def _L0_xcond_ref(x, t_emb, context_emb, mask, ln1_g, ln1_b, ln3_g, ln3_b, ln2_g, ln2_b, sa_wq, sa_bq, sa_wk, sa_bk, sa_wv, sa_bv, sa_wo, sa_bo, ca_wq, ca_bq, ca_wk, ca_bk, ca_wv, ca_bv, ca_wo, ca_bo, tp_w, tp_b, w1, b1, w2, b2):
        import jax, jax.numpy as jnp
        import numpy as np
        D = 256
        H = 16
        HD = D // H
        FF = 4 * D
        B, NQ, NK = (8, 256, 128)
        EPS = 1e-05

        def layernorm(x, g, b):
            m = jnp.mean(x, axis=-1, keepdims=True)
            v = jnp.mean(jnp.square(x - m), axis=-1, keepdims=True)
            return (x - m) * jax.lax.rsqrt(v + EPS) * g + b

        def mha(x, ctx, wq, bq, wk, bk, wv, bv, wo, bo, mask=None):
            Bq, Nq, _ = x.shape
            Nk = ctx.shape[1]
            q = (x @ wq + bq).reshape(Bq, Nq, H, HD)
            k = (ctx @ wk + bk).reshape(Bq, Nk, H, HD)
            v = (ctx @ wv + bv).reshape(Bq, Nk, H, HD)
            scores = jnp.einsum('bqhd,bkhd->bhqk', q, k) / np.sqrt(HD)
            if mask is not None:
                scores = jnp.where(mask[:, None, None, :].astype(bool), scores, -jnp.inf)
            attn = jax.nn.softmax(scores.astype(jnp.float32), axis=-1).astype(scores.dtype)
            out = jnp.einsum('bhqk,bkhd->bqhd', attn, v).reshape(Bq, Nq, D)
            return out @ wo + bo
        t_biases = jax.nn.silu(t_emb) @ tp_w + tp_b
        t_sa, t_ca, t_mlp = jnp.split(t_biases, 3, axis=-1)
        h = layernorm(x, ln1_g, ln1_b)
        h = mha(h, h, sa_wq, sa_bq, sa_wk, sa_bk, sa_wv, sa_bv, sa_wo, sa_bo)
        x = x + h + t_sa[:, None, :]
        h = layernorm(x, ln3_g, ln3_b)
        h = mha(h, context_emb, ca_wq, ca_bq, ca_wk, ca_bk, ca_wv, ca_bv, ca_wo, ca_bo, mask=mask)
        x = x + h + t_ca[:, None, :]
        h = layernorm(x, ln2_g, ln2_b)
        h = jax.nn.gelu(h @ w1 + b1, approximate=False) @ w2 + b2
        x = x + h + t_mlp[:, None, :]
        return x
    x = _L0_xcond_ref(x, cond_1024, ctx_1024, mask_BxS2_ik0, L0_xcond_ln1_g, L0_xcond_ln1_b, L0_xcond_ln3_g, L0_xcond_ln3_b, L0_xcond_ln2_g, L0_xcond_ln2_b, L0_xcond_sa_wq, L0_xcond_sa_bq, L0_xcond_sa_wk, L0_xcond_sa_bk, L0_xcond_sa_wv, L0_xcond_sa_bv, L0_xcond_sa_wo, L0_xcond_sa_bo, L0_xcond_ca_wq, L0_xcond_ca_bq, L0_xcond_ca_wk, L0_xcond_ca_bk, L0_xcond_ca_wv, L0_xcond_ca_bv, L0_xcond_ca_wo, L0_xcond_ca_bo, L0_xcond_tp_w, L0_xcond_tp_b, L0_xcond_w1, L0_xcond_b1, L0_xcond_w2, L0_xcond_b2)
    return x

_drawn_inputs = setup_inputs


def setup_inputs(seed=0):
    import zlib

    import numpy as np

    out = dict(_drawn_inputs(seed))
    spreads = {'L0_xcond_ln1_g': (1.0, 0.6),
     'L0_xcond_ln1_b': (0.0, 0.8),
     'L0_xcond_ln3_g': (1.0, 0.6),
     'L0_xcond_ln3_b': (0.0, 0.8),
     'L0_xcond_ln2_g': (1.0, 0.6),
     'L0_xcond_ln2_b': (0.0, 0.725),
     'L0_xcond_sa_bq': (0.0, 0.8),
     'L0_xcond_sa_bk': (0.0, 2.0),
     'L0_xcond_sa_bv': (0.0, 0.346),
     'L0_xcond_sa_bo': (0.0, 0.1),
     'L0_xcond_ca_bq': (0.0, 2.0),
     'L0_xcond_ca_bk': (0.0, 2.0),
     'L0_xcond_ca_bv': (0.0, 0.273),
     'L0_xcond_ca_bo': (0.0, 0.1),
     'L0_xcond_tp_b': (0.0, 0.1),
     'L0_xcond_b1': (0.0, 0.317),
     'L0_xcond_b2': (0.0, 0.1)}
    factors = {'L0_xcond_sa_wq': 8.0,
     'L0_xcond_sa_wk': 8.0,
     'L0_xcond_sa_wv': 5.803,
     'L0_xcond_ca_wq': 8.0,
     'L0_xcond_ca_wk': 8.0}
    for name, (base, spread) in spreads.items():
        noise = np.random.default_rng([zlib.crc32(name.encode()), seed]).standard_normal(out[name].shape)
        drawn = base * np.exp(spread * noise) if base else spread * noise
        out[name] = jnp.asarray(drawn.astype(out[name].dtype))
    for name, factor in factors.items():
        out[name] = (out[name] * factor).astype(out[name].dtype)
    return out
```

```python
from contextlib import ExitStack

import concourse.bass as bass
from concourse import mybir

ALU = mybir.AluOpType
ACT = mybir.ActivationFunctionType
AX_X = mybir.AxisListType.X
F32 = mybir.dt.float32
F32R = mybir.dt.float32r
I32 = mybir.dt.int32

P = 128
B, T, D = 4, 1024, 256
NK = 77
NKE = NK + NK % 2
H, HD = 16, 16
FF = 4 * D
DC = D // P
FC = FF // P
HG = 4
NG = H // HG
GW = HG * HD
BG = B * NG
CH = 512
TPC = CH // P
CPB = T // CH
NCH = B * CPB
KT = T // P
NU = BG * CPB
OUT_STEP = 2
MAXT_STEP = 6
LEAD = 3
EPS = 1e-5
SCALE = HD ** -0.5
MASKED = -1e30
VW = 2 * HD

ROWS_SPLIT = 4 * HD
ROW_MASK = ROWS_SPLIT
ROWS_SCORE = 96
ROW_MAX = 96
ROWS = 98


def back(k, par, n):
    return k + (par - n) // 2, (par - n) % 2


def live(k, par, count):
    return not isinstance(k, int) or 0 <= 2 * k + par < count


def reuse(item, banks):
    return next(n for n in range(1, len(banks) + 1) if banks[item - n] == banks[item])


def need(eng, sem, value):
    if not isinstance(value, int) or value > 0:
        eng.wait_ge(sem, value)


def steps(eng, step, total, first, last):
    for n in range(first):
        step(n // 2, n % 2)
    with eng.Fori(first // 2, last // 2) as k:
        step(k, 0)
        step(k, 1)
    for n in range(last, total):
        step(n // 2, n % 2)


class Arena:

    def __init__(self, nc, stack, tag):
        self.nc, self.stack, self.tag = nc, stack, tag

    def sb(self, name, shape, dt=F32):
        return self.stack.enter_context(self.nc.sbuf_tensor(f"{self.tag}_{name}", shape, dt))

    def ps(self, name, shape):
        return self.stack.enter_context(self.nc.psum_tensor(f"{self.tag}_{name}", shape, F32))

    def sem(self, name):
        return self.stack.enter_context(self.nc.semaphore(f"{self.tag}_{name}"))

    def sems(self, name, n):
        return [self.sem(f"{name}{i}") for i in range(n)]


def words(ap):
    return ap.bitcast(F32)


def chunked(w):
    return w.rearrange("(c p) n -> p c n", p=P)


def column(v):
    return v.rearrange("(c p) -> p c", p=P)


def setup(nc, a, W, s, out):
    ident, half = W["ident"], W["half"]
    with ExitStack() as stack:
        m = Arena(nc, stack, "setup")
        with_ctx = m.sb("ctx", [NK, B, D])
        ctxT = m.sb("ctxT", [P, DC, B * NK])
        wk, wv = m.sb("ca_wk", [P, DC, D]), m.sb("ca_wv", [P, DC, D])
        kfull = m.sb("kfull", [P, DC, B * NK])
        khi, klo = (m.sb(n, [P, DC, B * NK], F32R) for n in ("khi", "klo"))
        vaug = m.sb("vaug", [NK, B, H, VW])
        mask_i, mask_f = m.sb("mask_i", [NK, B], I32), m.sb("mask_f", [NK, B])
        maskrow_i = m.sb("maskrow_i", [BG, HG * NK], I32)
        maskrow_f = m.sb("maskrow_f", [BG, HG * NK])
        maskrow = m.sb("maskrow", [BG, HG * NK], F32R)
        cond = m.sb("cond", [B, D])
        sig, silu = m.sb("sig", [B, D]), m.sb("silu", [B, D])
        siluT, bvT = m.sb("siluT", [P, DC, B]), m.sb("bvT", [P, 2, DC])
        bv4 = m.sb("bv4", [P, 2, DC, B])
        tpw = m.sb("tpw", [P, DC, 3 * D])
        tprow, brow = m.sb("tprow", [B, 3 * D]), m.sb("brow", [B, 3 * D])
        badd = m.sb("badd", [B, 3 * D])
        trans = [m.ps(f"trans{c}", [P, 512]) for c in range(DC)]
        pk = [m.ps(f"pk{c}", [P, 512]) for c in range(DC)]
        pv = [m.ps(f"pv{i}", [P, 512]) for i in range(2)]
        prow = [m.ps(f"prow{i}", [P, 512]) for i in range(2)]
        ctx_in, cw_in, cond_in, tp_in, mask_in, w_in = (
            m.sem(n) for n in ("ctx_in", "cw_in", "cond_in", "tp_in", "mask_in", "w_in"))
        const, zero, own, ctxT_ps, ctxT_sb, k_ps, khi_sb, k_sb, klo_sb, v_ps, ones_sb, v_sb = (
            m.sem(n) for n in ("const", "zero", "own", "ctxT_ps", "ctxT_sb", "k_ps", "khi_sb", "k_sb",
                               "klo_sb", "v_ps", "ones_sb", "v_sb"))
        e_sb, silu_sb, siluT_ps, siluT_sb, bv_sb, row_ps, row_sb, maskrow_sb, stored = (
            m.sem(n) for n in ("e_sb", "silu_sb", "siluT_ps", "siluT_sb", "bv_sb", "row_ps", "row_sb",
                               "maskrow_sb", "stored"))
        block = stack.enter_context(nc.Block())

        @block.sync
        def _(sp):
            sp.dma_start(with_ctx[:, :, :], a["ctx"].rearrange("b k d -> k b d")).then_inc(ctx_in, 16)
            sp.dma_start(wk[:, :, :], chunked(a["ca_wk"])).then_inc(cw_in, 16)
            sp.dma_start(wv[:, :, :], chunked(a["ca_wv"])).then_inc(cw_in, 16)
            sp.dma_start(W["col"][:, 7, :], column(a["ca_bk"])).then_inc(cw_in, 16)
            sp.dma_start(mask_i[:, :], a["mask"].rearrange("b k -> k b")).then_inc(mask_in, 16)
            for b in range(B):
                sp.dma_start(maskrow_i[b * NG:(b + 1) * NG, :].rearrange("g (h k) -> g h k", h=HG),
                             a["mask"][b:b + 1, :].rearrange("b (u k) -> b u k", u=1).to_broadcast([NG, HG, NK]))\
                    .then_inc(mask_in, 16)
            for name in ("sa_wq", "sa_wk", "sa_wv", "sa_wo", "ca_wq", "ca_wo"):
                sp.dma_start(W[name][:, :, :], chunked(a[name])).then_inc(w_in, 16)
            for n, name in enumerate(("ln1_g", "ln1_b", "ln3_g", "ln3_b", "ln2_g", "ln2_b", "sa_bq")):
                sp.dma_start(W["col"][:, n, :], column(a[name])).then_inc(w_in, 16)
            for n, name in enumerate(("sa_bk", "ca_bq")):
                sp.dma_start(W["col"][:, 8 + n, :], column(a[name])).then_inc(w_in, 16)
            sp.dma_start(W["b1"][:, :], column(a["b1"])).then_inc(w_in, 16)

            sp.wait_ge(khi_sb, DC)
            sp.wait_ge(klo_sb, DC)
            for part, src in enumerate((khi, klo)):
                for c in range(DC):
                    dst = s["ck"][part].rearrange("(b c r) k -> c r b k", b=B, c=DC)[c]
                    sp.dma_start(dst, words(src[:, c, :]).rearrange("r (b k) -> r b k", b=B)).then_inc(stored, 16)
            sp.wait_ge(v_sb, B)
            sp.dma_start(s["cv"].rearrange("n k e -> k n e"),
                         vaug.rearrange("k b (g h) e -> k (b g) (h e)", g=NG)).then_inc(stored, 16)
            sp.wait_ge(maskrow_sb, 1)
            sp.dma_start(s["cmask"].rearrange("n u k -> (n u) k"), words(maskrow[:, :])).then_inc(stored, 16)
            sp.wait_ge(row_sb, 2)
            sp.dma_start(s["badd"].rearrange("b u d -> (b u) d"), badd[:, :]).then_inc(stored, 16)
            sp.wait_ge(stored, 16 * (2 * DC + 3))
            sp.wait_ge(w_in, 16 * 16)

        @block.gpsimd
        def _(pool):
            pool.memset(ident[:, :], 0.0).then_inc(zero, 1)
            pool.memset(half[:, 0, :], EPS).then_inc(const, 1)
            pool.memset(half[:, 1, :], -0.5).then_inc(const, 1)
            pool.wait_ge(zero, 1)
            pool.affine_select(out=ident[:, :], in_=ident[:, :], compare_op=ALU.not_equal, fill=1.0,
                               base=0, pattern=[[-1, P]], channel_multiplier=1).then_inc(const, 1)
            pool.memset(vaug[:, :, :, HD:VW], 1.0).then_inc(ones_sb, 1)
            for c in range(DC):
                pool.wait_ge(khi_sb, c + 1)
                pool.tensor_tensor(klo[:, c, :], kfull[:, c, :], khi[:, c, :].bitcast(F32),
                                   ALU.subtract).then_inc(klo_sb, 1)

        @block.scalar
        def _(act):
            act.dma_start(cond[:, :], a["cond"]).then_inc(cond_in, 16)
            act.dma_start(tpw[:, :, :], chunked(a["tp_w"])).then_inc(tp_in, 16)
            act.dma_start(tprow[:, :], a["tp_b"].rearrange("(u n) -> u n", u=1).to_broadcast([B, 3 * D])).then_inc(tp_in, 16)
            for n, name in enumerate(("sa_bo", "ca_bo", "b2")):
                act.dma_start(brow[:, n * D:(n + 1) * D],
                              a[name].rearrange("(u n) -> u n", u=1).to_broadcast([B, D])).then_inc(tp_in, 16)
            for n, name in enumerate(("sa_bv", "ca_bv")):
                act.dma_start(bvT[:, n, :], column(a[name])).then_inc(tp_in, 16)
            act.wait_ge(cond_in, 16)
            act.activation(sig[:, :], cond[:, :], ACT.Exp, scale=-1.0).then_inc(e_sb, 1)
            for c in range(DC):
                act.wait_ge(k_sb, c + 1)
                act.activation(khi[:, c, :], kfull[:, c, :], ACT.Copy).then_inc(khi_sb, 1)

        @block.tensor
        def _(pe):
            pe.wait_ge(const, 3)
            pe.wait_ge(ctx_in, 16)
            for c in range(DC):
                for b in range(B):
                    last = pe.transpose(trans[c][:, b * NK:(b + 1) * NK], with_ctx[:, b, c * P:(c + 1) * P],
                                        ident[0:NK, 0:NK])
                last.then_inc(ctxT_ps, 1)
            pe.wait_ge(ctxT_sb, DC)
            pe.wait_ge(cw_in, 48)
            for m_ in range(DC):
                for c in range(DC):
                    last = pe.matmul(pk[m_][:, 0:B * NK], wk[:, c, m_ * P:(m_ + 1) * P], ctxT[:, c, :],
                                     start=(c == 0), stop=(c == DC - 1))
                last.then_inc(k_ps, 1)
            for b in range(B):
                for c in range(DC):
                    last = pe.matmul(pv[b // 2][0:NK, (b % 2) * D:(b % 2 + 1) * D],
                                     ctxT[:, c, b * NK:(b + 1) * NK], wv[:, c, :],
                                     start=(c == 0), stop=(c == DC - 1))
                last.then_inc(v_ps, 1)
            pe.wait_ge(silu_sb, 1)
            for c in range(DC):
                last = pe.transpose(trans[0][:, c * B:(c + 1) * B], silu[:, c * P:(c + 1) * P], ident[0:B, 0:B])
            last.then_inc(siluT_ps, 1)
            pe.wait_ge(siluT_sb, 1)
            pe.wait_ge(bv_sb, 1)
            pe.wait_ge(tp_in, 16 * 7)
            pe.wait_ge(w_in, 16 * 16)
            for n in range(3):
                dst = prow[n // 2][0:B, (n % 2) * D:(n % 2 + 1) * D]
                for c in range(DC):
                    last = pe.matmul(dst, siluT[:, c, :], tpw[:, c, n * D:(n + 1) * D],
                                     start=(c == 0), stop=(c == DC - 1 and n == 2))
                if n < 2:
                    wo = W["sa_wo"] if n == 0 else W["ca_wo"]
                    for c in range(DC):
                        last = pe.matmul(dst, bv4[:, n, c, :], wo[:, c, :], start=False, stop=(c == DC - 1))
            last.then_inc(row_ps, 1)

        @block.vector
        def _(dve):
            dve.wait_ge(mask_in, 16 * (B + 1))
            dve.tensor_copy(mask_f[:, :], mask_i[:, :]).then_inc(own, 1)
            dve.tensor_copy(maskrow_f[:, :], maskrow_i[:, :]).then_inc(own, 1)
            dve.wait_ge(own, 2)
            dve.tensor_scalar(mask_f[:, :], mask_f[:, :], 0.0, None, ALU.not_equal).then_inc(own, 1)
            dve.tensor_scalar(maskrow[:, :], maskrow_f[:, :], 0.0, MASKED, ALU.is_equal, ALU.mult)\
                .then_inc(maskrow_sb, 1)
            for c in range(DC):
                dve.wait_ge(ctxT_ps, c + 1)
                dve.tensor_copy(ctxT[:, c, :], trans[c][:, 0:B * NK]).then_inc(ctxT_sb, 1)
            dve.wait_ge(e_sb, 1)
            dve.tensor_scalar(sig[:, :], sig[:, :], 1.0, None, ALU.add).then_inc(own, 1)
            dve.wait_ge(own, 4)
            dve.reciprocal(sig[:, :], sig[:, :]).then_inc(own, 1)
            dve.wait_ge(own, 5)
            dve.tensor_tensor(silu[:, :], cond[:, :], sig[:, :], ALU.mult).then_inc(silu_sb, 1)
            dve.wait_ge(tp_in, 16 * 7)
            dve.tensor_copy(bv4[:, :, :, :],
                            bvT.rearrange("p n (c u) -> p n c u", u=1).to_broadcast([P, 2, DC, B])).then_inc(bv_sb, 1)
            dve.tensor_tensor(brow[:, :], brow[:, :], tprow[:, :], ALU.add).then_inc(own, 1)
            dve.wait_ge(siluT_ps, 1)
            dve.tensor_copy(siluT.rearrange("p c b -> p (c b)"), trans[0][:, 0:DC * B]).then_inc(siluT_sb, 1)
            dve.wait_ge(cw_in, 48)
            for c in range(DC):
                dve.wait_ge(k_ps, c + 1)
                dve.tensor_scalar(kfull[:, c, :], pk[c][:, 0:B * NK], W["col"][:, 7, c:c + 1], None,
                                  ALU.add).then_inc(k_sb, 1)
            dve.wait_ge(ones_sb, 1)
            for b in range(B):
                dve.wait_ge(v_ps, b + 1)
                dve.tensor_scalar(vaug[:, b, :, 0:HD],
                                  pv[b // 2][0:NK, (b % 2) * D:(b % 2 + 1) * D].rearrange("k (h e) -> k h e", h=H),
                                  mask_f[:, b:b + 1], None, ALU.mult).then_inc(own, 1)
                dve.tensor_scalar(vaug[:, b, :, HD:VW], vaug[:, b, :, HD:VW], mask_f[:, b:b + 1], None,
                                  ALU.mult).then_inc(v_sb, 1)
            dve.wait_ge(own, 6 + B)
            dve.wait_ge(row_ps, 1)
            for n in range(2):
                w = min(2, 3 - 2 * n) * D
                dve.tensor_tensor(badd[:, 2 * n * D:2 * n * D + w], prow[n][0:B, 0:w],
                                  brow[:, 2 * n * D:2 * n * D + w], ALU.add).then_inc(row_sb, 1)


def norm_stats(dve, x, stats, moments, own, count):
    for t in range(TPC):
        last = dve.bn_stats(stats[:, t, :], x[:, t, :])
    last.then_inc(own, 1)
    dve.wait_ge(own, count)
    dve.memset(stats[:, TPC, 0:1], 0.0)
    for t in range(TPC):
        last = dve.bn_aggr(moments[:, t, :], stats[:, t, :])
    return last


def rstd_of(pool, moments, rstd, half, own, count):
    pool.tensor_tensor(rstd[:, :], moments[:, :, 1], half[:, 0, :], ALU.add).then_inc(own, 1)
    pool.wait_ge(own, count)
    return pool.tensor_tensor(rstd[:, :], rstd[:, :], half[:, 1, :], ALU.pow)


def normalize(dve, xhat, x, moments, rstd):
    for t in range(TPC):
        last = dve.tensor_scalar(xhat[:, t, :], x[:, t, :], moments[:, t, 0:1], rstd[:, t:t + 1],
                                 ALU.subtract, ALU.mult)
    return last


def turn(pe, banks, tokens, ident, sem):
    for c in range(DC):
        for t in range(TPC):
            last = pe.transpose(banks[c][:, t * P:(t + 1) * P], tokens[:, t, c * P:(c + 1) * P], ident[:, :])
        last.then_inc(sem, 1)


def self_qkv(nc, a, W, s):
    ident, half, col = W["ident"], W["half"], W["col"]
    x_dram = a["x"].rearrange("b (c t p) d -> (b c) p t d", c=CPB, t=TPC)
    NQK = 2 * DC
    with ExitStack() as stack:
        m = Arena(nc, stack, "qkv")
        x = [m.sb(f"x{i}", [P, TPC, D]) for i in range(2)]
        stats, moments, rstd = m.sb("stats", [P, TPC + 1, 6]), m.sb("moments", [P, TPC, 2]), m.sb("rstd", [P, TPC])
        xhat = [m.sb(f"xhat{i}", [P, TPC, D]) for i in range(2)]
        hT = [m.sb(f"hT{i}", [P, DC, CH]) for i in range(2)]
        full = [m.sb(f"full{i}", [P, NQK, CH]) for i in range(2)]
        hi = [m.sb(f"hi{i}", [P, NQK, CH], F32R) for i in range(2)]
        lo = [m.sb(f"lo{i}", [P, NQK, CH], F32R) for i in range(2)]
        vaug = [m.sb(f"vaug{i}", [P, TPC, H, VW]) for i in range(2)]
        turned = [m.ps(f"turned{c}", [P, CH]) for c in range(DC)]
        qk_ps = [m.ps(f"qk{i}", [P, CH]) for i in range(NQK)]
        v_ps = [m.ps(f"v{i}", [P, 2 * D]) for i in range(TPC // 2)]
        x_in, stored = m.sems("x_in", 2), m.sems("stored", 2)
        own, pool_own, ones, stats_done, rstd_done, xhat_done, turned_done, hT_done = (
            m.sem(n) for n in ("own", "pool_own", "ones", "stats_done", "rstd_done", "xhat_done", "turned_done",
                               "hT_done"))
        qk_done, hi_done, full_done, lo_done, v_done, vaug_done = (
            m.sem(n) for n in ("qk_done", "hi_done", "full_done", "lo_done", "v_done", "vaug_done"))
        STORES = 2 * NQK + NG
        block = stack.enter_context(nc.Block())

        @block.sync
        def _(sp):
            def step(k, par):
                n = 2 * k + par
                if live(k, par, NCH):
                    need(sp, xhat_done, n - 1)
                    sp.dma_start(x[par][:, :, :], x_dram[n]).then_inc(x_in[par], 16)
                k2, p2 = back(k, par, 2)
                if live(k2, p2, NCH):
                    n2 = 2 * k2 + p2
                    sp.wait_ge(hi_done, NQK * (n2 + 1))
                    sp.wait_ge(lo_done, NQK * (n2 + 1))
                    for i in range(NQK):
                        which, c = i // DC, i % DC
                        for part, src in enumerate((hi, lo)):
                            dst = s["qk"][which, part].rearrange("(b c g) q r t -> b c q g r t", b=B, c=DC)
                            sp.dma_start(dst[k2, c, p2], words(src[p2][:, i, :]))\
                                .then_inc(stored[p2], 16)
                    sp.wait_ge(vaug_done, 2 * (n2 + 1))
                    for g in range(NG):
                        dst = s["v"].rearrange("(b g) p t e -> b g p t e", b=B)[k2, g, :, p2 * TPC:(p2 + 1) * TPC, :]
                        sp.dma_start(dst, vaug[p2][:, :, g * HG:(g + 1) * HG, :].rearrange("p t h e -> p t (h e)"))\
                            .then_inc(stored[p2], 16)

            steps(sp, step, NCH + 2, 4, NCH)
            for par in range(2):
                sp.wait_ge(stored[par], 16 * STORES * NCH // 2)

        @block.gpsimd
        def _(pool):
            for i in range(2):
                pool.memset(vaug[i][:, :, :, HD:VW], 1.0).then_inc(ones, 1)

            def step(k, par):
                n = 2 * k + par
                if live(k, par, NCH):
                    pool.wait_ge(stats_done, n + 1)
                    need(pool, xhat_done, n)
                    rstd_of(pool, moments, rstd, half, pool_own, n + 1).then_inc(rstd_done, 1)
                k2, p2 = back(k, par, 2)
                if live(k2, p2, NCH):
                    n2 = 2 * k2 + p2
                    need(pool, stored[p2], 16 * STORES * k2)
                    for i in range(NQK):
                        pool.wait_ge(hi_done, NQK * n2 + i + 1)
                        pool.tensor_tensor(lo[p2][:, i, :], full[p2][:, i, :], hi[p2][:, i, :].bitcast(F32),
                                           ALU.subtract).then_inc(lo_done, 1)

            steps(pool, step, NCH + 2, 4, NCH)

        @block.vector
        def _(dve):
            dve.wait_ge(ones, 2)

            def step(k, par):
                n = 2 * k + par
                if live(k, par, NCH):
                    dve.wait_ge(x_in[par], 16 * (k + 1))
                    norm_stats(dve, x[par], stats, moments, own, n + 1).then_inc(stats_done, 1)
                    dve.wait_ge(rstd_done, n + 1)
                    need(dve, turned_done, DC * (n - 1))
                    normalize(dve, xhat[par], x[par], moments, rstd).then_inc(xhat_done, 1)
                k2, p2 = back(k, par, 2)
                if live(k2, p2, NCH):
                    n2 = 2 * k2 + p2
                    need(dve, lo_done, NQK * (n2 - 1))
                    for i in range(NQK):
                        dve.wait_ge(qk_done, NQK * n2 + i + 1)
                        dve.tensor_scalar(full[p2][:, i, :], qk_ps[i][:, :], col[:, 6 + i // DC * 2, i % DC:i % DC + 1],
                                          None, ALU.add).then_inc(full_done, 1)
                    need(dve, stored[p2], 16 * STORES * k2)
                    for i in range(TPC // 2):
                        dve.wait_ge(v_done, 2 * n2 + i + 1)
                        dve.tensor_copy(vaug[p2][:, 2 * i:2 * i + 2, :, 0:HD],
                                        v_ps[i].rearrange("p (t h e) -> p t h e", t=2, h=H)).then_inc(vaug_done, 1)

            steps(dve, step, NCH + 2, 4, NCH)

        @block.scalar
        def _(act):
            def step(k, par):
                n = 2 * k + par
                if live(k, par, NCH):
                    for c in range(DC):
                        act.wait_ge(turned_done, DC * n + c + 1)
                        if c == 0:
                            need(act, v_done, 2 * (n - 1))
                        act.activation(hT[par][:, c, :], turned[c][:, :], ACT.Identity, scale=col[:, 0, c:c + 1],
                                       bias=col[:, 1, c:c + 1]).then_inc(hT_done, 1)
                k1, p1 = back(k, par, 1)
                if live(k1, p1, NCH):
                    n1 = 2 * k1 + p1
                    need(act, stored[p1], 16 * STORES * k1)
                    for i in range(NQK):
                        act.wait_ge(full_done, NQK * n1 + i + 1)
                        act.activation(hi[p1][:, i, :], full[p1][:, i, :], ACT.Copy).then_inc(hi_done, 1)

            steps(act, step, NCH + 1, 4, NCH)

        @block.tensor
        def _(pe):
            def step(k, par):
                n = 2 * k + par
                if live(k, par, NCH):
                    pe.wait_ge(xhat_done, n + 1)
                    need(pe, hT_done, DC * n)
                    turn(pe, turned, xhat[par], ident, turned_done)
                k1, p1 = back(k, par, 1)
                if live(k1, p1, NCH):
                    n1 = 2 * k1 + p1
                    pe.wait_ge(hT_done, DC * (n1 + 1))
                    for i in range(NQK):
                        w, mc = W["sa_wq" if i < DC else "sa_wk"], i % DC
                        need(pe, full_done, NQK * (n1 - 1) + i + 1)
                        for c in range(DC):
                            last = pe.matmul(qk_ps[i][:, :], w[:, c, mc * P:(mc + 1) * P], hT[p1][:, c, :],
                                             start=(c == 0), stop=(c == DC - 1))
                        last.then_inc(qk_done, 1)
                    for t in range(TPC):
                        if t % 2 == 0:
                            need(pe, vaug_done, 2 * (n1 - 1) + t // 2 + 1)
                        for c in range(DC):
                            last = pe.matmul(v_ps[t // 2][:, (t % 2) * D:(t % 2 + 1) * D],
                                             hT[p1][:, c, t * P:(t + 1) * P], W["sa_wv"][:, c, :],
                                             start=(c == 0), stop=(c == DC - 1))
                        if t % 2:
                            last.then_inc(v_done, 1)

            steps(pe, step, NCH + 1, 4, NCH)


def stack_rows(sp, dram, n, which, dst, sem):
    for block in range(4):
        lo = block // 2 if which == 0 else block % 2
        for c in range(CPB):
            src = dram[lo].rearrange("n c (h e) t -> n c e h t", h=HG)[n, c]
            sp.dma_start(words(dst[block * HD:(block + 1) * HD, c, :, :]), src).then_inc(sem, 16)


def split_max(dve, maxima, rows, own, count):
    dve.tensor_scalar(rows[:, 0, :], maxima[:, :], -1.0, None, ALU.mult).then_inc(own, 1)
    dve.wait_ge(own, count)
    return dve.scalar_tensor_tensor(rows[:, 1, :], maxima[:, :], -1.0, rows[:, 0, :].bitcast(F32),
                                    ALU.mult, ALU.subtract)


class Slots:

    def __init__(self):
        tiles = HG * TPC
        self.order = [("max", 0, j) for j in range(tiles)] + [("maxT", 0, 0)] + [("max", 1, j) for j in range(2 * LEAD)]
        for u in range(NU):
            for st in range(KT):
                self.order += [("max", *self.tile(u, st, 0))]
                if st == OUT_STEP:
                    self.order += [("out", u - 1, 0)]
                if st == MAXT_STEP:
                    self.order += [("maxT", u + 1, 0)]
                self.order += [("max", *self.tile(u, st, 1))]
        self.order = [i for i in self.order + [("out", NU - 1, 0)] if 0 <= i[1] < NU]
        self.number = {item: n for n, item in enumerate(self.order)}
        self.per_unit = self.number["max", 5, 0] - self.number["max", 4, 0]

    @staticmethod
    def tile(u, st, i):
        j = 2 * (st + LEAD) + i
        return (u + 1, j) if j < HG * TPC else (u + 2, j - HG * TPC)

    def at(self, kind, u, j):
        if isinstance(u, int):
            return self.number[kind, u, j], self.number[kind, u, j] % 2
        base = self.number[kind, 4, j] - 4 * self.per_unit
        return base + self.per_unit * u, base % 2


def self_attention(nc, a, W, s):
    ident = W["ident"]
    NMAX = HG * TPC
    NEXP = HG * KT
    NB, EXP_SHIFT = 3, HG * (KT // 2) + 2
    exp_bank = [(i + (i >= EXP_SHIFT)) % NB for i in range(NEXP)]
    with ExitStack() as stack:
        m = Arena(nc, stack, "sa")
        q = [m.sb(f"q{i}", [ROWS, CPB, HG, CH], F32R) for i in range(2)]
        kk = [m.sb(f"k{i}", [ROWS, CPB, HG, CH], F32R) for i in range(2)]
        v = [m.sb(f"v{i}", [P, KT, HG, VW]) for i in range(2)]
        NP_ = 4
        probs = [m.sb(f"probs{i}", [P, HG, CH]) for i in range(NP_)]
        maxima = [m.sb(f"maxima{i}", [P, NMAX]) for i in range(2)]
        maxrows, maxT = m.sb("maxrows", [P, 2, NMAX], F32R), m.sb("maxT", [2 * NMAX, P], F32R)
        zeros, minus = m.sb("zeros", [P, NMAX]), m.sb("minus", [P, NMAX])
        o_sb = m.sb("o_sb", [P, CH])
        inv = m.sb("inv", [P, TPC, HG])
        o_out = [m.sb(f"o_out{i}", [P, TPC, HG, HD]) for i in range(2)]
        slot = [m.ps(f"slot{i}", [P, T]) for i in range(2)]
        s_exp = [m.ps(f"s_exp{i}", [P, CH]) for i in range(NB)]
        o_ps = m.ps("o", [P, CH])
        slots = Slots()
        rows_in, out_done = m.sems("rows_in", 2), m.sems("out_done", 2)
        zero, max_in, filled, emptied, negated, own, s_done, exp_done, pv_done, o_done, inv_done, w_in = (
            m.sem(n) for n in ("zero", "max_in", "filled", "emptied", "negated", "own", "s_done", "exp_done",
                               "pv_done", "o_done", "inv_done", "w_in"))
        LOADS = 16 * (2 * 4 * CPB + 1)
        block = stack.enter_context(nc.Block())

        @block.sync
        def _(sp):
            def load(n, par):
                for which, dst in enumerate((q, kk)):
                    stack_rows(sp, s["qk"][which], n, which, dst[par], rows_in[par])
                sp.dma_start(v[par][:, :, :, :].rearrange("p t h e -> p t (h e)"), s["v"][n]).then_inc(rows_in[par], 16)

            def max_rows(u, par, qc):
                sp.wait_ge(emptied, slots.at("maxT", u, 0)[0] + 1)
                rows = words(q[par][ROW_MAX:ROWS, qc, :, :]).rearrange("r h (t p) -> r (h t) p", t=TPC)
                sp.dma_start(rows, words(maxT[:, :])).then_inc(max_in, 16)

            load(0, 0)
            max_rows(0, 0, 0)

            def step(k, par):
                n = 2 * k + par
                if live(k, par, BG - 1):
                    need(sp, pv_done, 2 * KT * n)
                    load(n + 1, 1 - par)
                for qc in range(CPB):
                    u = CPB * n + qc
                    if live(k, par, BG - 1) or qc == 0:
                        max_rows(u + 1, par if qc == 0 else 1 - par, 1 - qc)
                    if not (isinstance(k, int) and k == 0 and par == 0 and qc == 0):
                        store(back(k, par, 1) if qc == 0 else (k, par), 1 - qc)

            def store(which, qc):
                n = 2 * which[0] + which[1]
                sp.wait_ge(emptied, slots.at("out", CPB * n + qc, 0)[0] + 1)
                sp.dma_start(s["attn"][n, qc].rearrange("t p e -> p t e"),
                             o_out[qc].rearrange("p t h e -> p t (h e)")).then_inc(out_done[qc], 16)

            steps(sp, step, BG, 2, BG - 2)
            store((BG // 2 - 1, 1), 1)
            for qc in range(CPB):
                sp.wait_ge(out_done[qc], 16 * BG)
            sp.wait_ge(w_in, 32)

        @block.gpsimd
        def _(pool):
            for par in range(2):
                need(pool, zero, 3 * par)
                pool.memset(words(q[par][ROWS_SPLIT:ROWS_SCORE, :, :, :]), 0.0).then_inc(zero, 1)
                pool.wait_ge(zero, 3 * par + 1)
                pool.memset(words(kk[par][ROWS_SPLIT:ROWS_SCORE, :, :, :]), 0.0).then_inc(zero, 1)
                pool.wait_ge(zero, 3 * par + 2)
                pool.memset(words(kk[par][ROW_MAX:ROWS, :, :, :]), 1.0).then_inc(zero, 1)
            pool.wait_ge(zero, 6)
            pool.memset(zeros[:, :], 0.0).then_inc(zero, 1)

            def negate(u, qc):
                pool.wait_ge(emptied, slots.at("max", u, NMAX - 1)[0] + 1)
                if not isinstance(u, int) or u > 0:
                    pool.wait_ge(filled, slots.at("maxT", u - 1, 0)[0] + 1)
                pool.tensor_tensor(minus[:, :], zeros[:, :], maxima[qc][:, :], ALU.subtract).then_inc(own, 1)
                pool.wait_ge(own, 2 * u + 1)
                pool.tensor_tensor(maxrows[:, 0, :], minus[:, :], zeros[:, :], ALU.subtract).then_inc(own, 1)
                pool.wait_ge(own, 2 * u + 2)
                pool.tensor_tensor(maxrows[:, 1, :], minus[:, :], maxrows[:, 0, :].bitcast(F32), ALU.subtract)\
                    .then_inc(negated, 1)

            for name in ("w1", "w2"):
                pool.dma_start(W[name][:, :, :], chunked(a[name])).then_inc(w_in, 16)
            pool.wait_ge(zero, 7)
            negate(0, 0)

            def step(k, par):
                for qc in range(CPB):
                    if live(k, par, BG - 1) or qc == 0:
                        negate(CPB * (2 * k + par) + qc + 1, 1 - qc)

            steps(pool, step, BG, 2, BG - 2)

        @block.tensor
        def _(pe):
            pe.wait_ge(zero, 6)

            def take(kind, u, j):
                number, which = slots.at(kind, u, j)
                need(pe, emptied, number - 1)
                return slot[which]

            def score_max(u, par, qc, j):
                h, t = j // TPC, j % TPC
                dst = take("max", u, j)
                tile = q[par][0:ROWS_SCORE, qc, h, t * P:(t + 1) * P]
                for c in range(CPB):
                    last = pe.matmul(dst[:, c * CH:(c + 1) * CH], tile, kk[par][0:ROWS_SCORE, c, h, :],
                                     start=True, stop=True)
                last.then_inc(filled, 1)

            def turn_max(u):
                pe.wait_ge(negated, u + 1)
                pe.transpose(take("maxT", u, 0)[0:2 * NMAX, 0:P],
                             maxrows[:, :, :].bitcast(F32).rearrange("p r j -> p (r j)"), ident[:, :])\
                    .then_inc(filled, 1)

            def turn_out(u):
                pe.wait_ge(o_done, u + 1)
                dst = take("out", u, 0)
                for t in range(TPC):
                    last = pe.transpose(dst[:, t * P:(t + 1) * P], o_sb[:, t * P:(t + 1) * P], ident[:, :])
                last.then_inc(filled, 1)

            def values(u, par, st):
                if st == 0:
                    need(pe, o_done, u)
                pe.wait_ge(exp_done, HG * (KT * u + st + 1))
                for h in range(HG):
                    last = pe.matmul(o_ps[h * VW:(h + 1) * VW, :], v[par][:, st, h, :], probs[st % NP_][:, h, :],
                                     start=(st == 0), stop=(st == KT - 1), tile_position=(0, h * VW))
                last.then_inc(pv_done, 1)

            def prologue():
                pe.wait_ge(rows_in[0], LOADS)
                for j in range(NMAX):
                    score_max(0, 0, 0, j)
                turn_max(0)
                for j in range(2 * LEAD):
                    score_max(1, 0, 1, j)

            prologue()

            def step(k, par):
                n = 2 * k + par
                more = live(k, par, BG - 1)
                k1, p1 = back(k, par, -1)
                for qc in range(CPB):
                    u = CPB * n + qc
                    next_par, next_qc = (par, 1) if qc == 0 else (1 - par, 0)
                    pe.wait_ge(max_in, 16 * (u + 1))
                    for st in range(KT):
                        for h in range(HG):
                            i = HG * st + h
                            need(pe, exp_done, NEXP * u + i + 1 - reuse(i, exp_bank))
                            pe.matmul(s_exp[exp_bank[i]][:, :], kk[par][:, st // TPC, h, st % TPC * P:(st % TPC + 1) * P],
                                      q[par][:, qc, h, :], start=True, stop=True).then_inc(s_done, 1)
                            if h in (0, 3):
                                j = 2 * (st + LEAD) + h // 3
                                if j < NMAX:
                                    if more or qc == 0:
                                        score_max(u + 1, next_par, next_qc, j)
                                elif more:
                                    if qc == 0 and j == NMAX:
                                        pe.wait_ge(rows_in[1 - par], LOADS * (k1 + 1))
                                    score_max(u + 2, 1 - par, qc, j - NMAX)
                            if h == 1:
                                if st > 0:
                                    values(u, par, st - 1)
                                elif not (isinstance(u, int) and u == 0):
                                    values(u - 1, par if qc else 1 - par, KT - 1)
                                if st == MAXT_STEP and (more or qc == 0):
                                    turn_max(u + 1)
                                if st == OUT_STEP and not (isinstance(u, int) and u == 0):
                                    turn_out(u - 1)

            steps(pe, step, BG, 2, BG - 2)
            values(NU - 1, 1, KT - 1)
            turn_out(NU - 1)

        @block.scalar
        def _(act):
            def step(k, par):
                n = 2 * k + par
                for qc in range(CPB):
                    u = CPB * n + qc
                    for st in range(KT):
                        need(act, pv_done, KT * u + st - NP_ + 1)
                        for h in range(HG):
                            act.wait_ge(s_done, HG * (KT * u + st) + h + 1)
                            act.activation(probs[st % NP_][:, h, :], s_exp[exp_bank[HG * st + h]][:, :], ACT.Exp, scale=SCALE)\
                                .then_inc(exp_done, 1)

            steps(act, step, BG, 2, BG - 2)

        @block.vector
        def _(dve):
            def item(kind, u, j):
                number, which = slots.at(kind, u, j)
                dve.wait_ge(filled, number + 1)
                return slot[which]

            def reduce(u, qc, j):
                dve.tensor_reduce(maxima[qc][:, j:j + 1], item("max", u, j)[:, :], AX_X, ALU.max).then_inc(emptied, 1)

            def take_max(u):
                need(dve, max_in, 16 * u)
                dve.tensor_copy(maxT[:, :], item("maxT", u, 0)[0:2 * NMAX, 0:P]).then_inc(emptied, 1)

            def take_out(u):
                dve.wait_ge(pv_done, KT * (u + 1))
                if not isinstance(u, int) or u > 0:
                    dve.wait_ge(filled, slots.at("out", u - 1, 0)[0] + 1)
                dve.tensor_copy(o_sb[:, :], o_ps[:, :]).then_inc(o_done, 1)

            def scale_out(u, qc, k_):
                if not isinstance(u, int) or u > 0:
                    dve.wait_ge(emptied, slots.at("out", u - 1, 0)[0] + 1)
                sums = item("out", u, 0)[:, 0:CH].rearrange("p (t h e) -> p t h e", t=TPC, h=HG)
                dve.reciprocal(inv[:, :, :], sums[:, :, :, HD]).then_inc(inv_done, 1)
                dve.wait_ge(inv_done, u + 1)
                need(dve, out_done[qc], 16 * k_)
                dve.tensor_tensor(o_out[qc][:, :, :, :], sums[:, :, :, 0:HD],
                                  inv.rearrange("p t (h e) -> p t h e", e=1).to_broadcast([P, TPC, HG, HD]),
                                  ALU.mult).then_inc(emptied, 1)

            for j in range(NMAX):
                reduce(0, 0, j)
            take_max(0)
            for j in range(2 * LEAD):
                reduce(1, 1, j)

            def step(k, par):
                n = 2 * k + par
                more = live(k, par, BG - 1)
                for qc in range(CPB):
                    u = CPB * n + qc
                    for st in range(KT):
                        for i in range(2):
                            j = 2 * (st + LEAD) + i
                            if j < NMAX:
                                if more or qc == 0:
                                    reduce(u + 1, 1 - qc, j)
                            elif more:
                                reduce(u + 2, qc, j - NMAX)
                            if i == 0 and st == 0 and not (isinstance(u, int) and u == 0):
                                take_out(u - 1)
                            if i == 0 and st == OUT_STEP and not (isinstance(u, int) and u == 0):
                                scale_out(u - 1, 1 - qc, (u - 1) // 2 if isinstance(u, int) else n - (1 - qc))
                            if i == 0 and st == MAXT_STEP and (more or qc == 0):
                                take_max(u + 1)

            steps(dve, step, BG, 2, BG - 2)
            take_out(NU - 1)
            scale_out(NU - 1, 1, BG - 1)


class Residual:

    def __init__(self, m, nc, a, W, s, x_in_dram, wo, row, gain, last_row):
        self.nc, self.W, self.s, self.wo, self.row, self.gain, self.last_row = nc, W, s, wo, row, gain, last_row
        self.x_dram = x_in_dram
        self.att = [m.sb(f"att{i}", [P, TPC, D]) for i in range(2)]
        self.x = [m.sb(f"x{i}", [P, TPC, D]) for i in range(2)]
        self.badd = [m.sb(f"badd{i}", [P, D]) for i in range(2)]
        self.attT = m.sb("attT", [P, DC, CH])
        self.y = [m.sb(f"y{i}", [P, TPC, D]) for i in range(2)]
        self.stats, self.moments, self.rstd = m.sb("stats", [P, TPC + 1, 6]), m.sb("moments", [P, TPC, 2]), m.sb("rstd", [P, TPC])
        self.xhat = m.sb("xhat", [P, TPC, D])
        self.hT = [m.sb(f"hT{i}", [P, DC, CH]) for i in range(2)]
        self.turned = [m.ps(f"turned{c}", [P, CH]) for c in range(DC)]
        self.wo_ps = [m.ps(f"wo{i}", [P, 2 * D]) for i in range(TPC // 2)]
        self.loaded = m.sems("loaded", 2)
        (self.own, self.pool_own, self.attT_ps, self.attT_sb, self.wo_done, self.xb_done, self.y_done, self.stats_done,
         self.rstd_done, self.xhat_done, self.hT_ps, self.hT_sb) = (
            m.sem(n) for n in ("own", "pool_own", "attT_ps", "attT_sb", "wo_done", "xb_done", "y_done", "stats_done",
                               "rstd_done", "xhat_done", "hT_ps", "hT_sb"))
        self.LOADS = 16 * (NG + 2)

    def load(self, sp, k, par):
        n = 2 * k + par
        need(sp, self.attT_ps, DC * (n - 1))
        need(sp, self.y_done, n - 1)
        for g in range(NG):
            src = self.s["attn"].rearrange("(b g) c t p e -> b g c p t e", b=B)[k, g, par]
            sp.dma_start(self.att[par][:, :, g * GW:(g + 1) * GW], src).then_inc(self.loaded[par], 16)
        sp.dma_start(self.x[par][:, :, :], self.x_dram[n]).then_inc(self.loaded[par], 16)
        sp.dma_start(self.badd[par][:, :], self.s["badd"][k][:, self.row * D:(self.row + 1) * D]
                     .to_broadcast([P, D])).then_inc(self.loaded[par], 16)

    def pool_add(self, pool, k, par):
        pool.wait_ge(self.loaded[par], self.LOADS * (k + 1))
        pool.tensor_tensor(self.x[par][:, :, :], self.x[par][:, :, :],
                           self.badd[par].rearrange("p (t d) -> p t d", t=1).to_broadcast([P, TPC, D]), ALU.add)\
            .then_inc(self.xb_done, 1)

    def pool_rstd(self, pool, k, par):
        n = 2 * k + par
        pool.wait_ge(self.stats_done, n + 1)
        need(pool, self.xhat_done, n)
        rstd_of(pool, self.moments, self.rstd, self.W["half"], self.pool_own, n + 1).then_inc(self.rstd_done, 1)

    def turn_att(self, pe, k, par):
        n = 2 * k + par
        pe.wait_ge(self.loaded[par], self.LOADS * (k + 1))
        need(pe, self.hT_sb, DC * (n - 1))
        turn(pe, self.turned, self.att[par], self.W["ident"], self.attT_ps)

    def turn_h(self, pe, k, par):
        n = 2 * k + par
        pe.wait_ge(self.xhat_done, n + 1)
        pe.wait_ge(self.attT_sb, DC * (n + 2) if not isinstance(k, int) else DC * min(n + 2, NCH))
        turn(pe, self.turned, self.xhat, self.W["ident"], self.hT_ps)

    def project(self, pe, k, par):
        n = 2 * k + par
        pe.wait_ge(self.attT_sb, DC * (n + 1))
        for t in range(TPC):
            if t % 2 == 0:
                need(pe, self.y_done, n)
            for c in range(DC):
                last = pe.matmul(self.wo_ps[t // 2][:, (t % 2) * D:(t % 2 + 1) * D],
                                 self.attT[:, c, t * P:(t + 1) * P], self.wo[:, c, :],
                                 start=(c == 0), stop=(c == DC - 1))
            if t % 2:
                last.then_inc(self.wo_done, 1)

    def take_att(self, act, k, par):
        n = 2 * k + par
        for c in range(DC):
            act.wait_ge(self.attT_ps, DC * n + c + 1)
            if c == 0:
                need(act, self.wo_done, 2 * n)
            act.activation(self.attT[:, c, :], self.turned[c][:, :], ACT.Copy).then_inc(self.attT_sb, 1)

    def take_h(self, act, k, par, used, count):
        n = 2 * k + par
        need(act, used, count)
        for c in range(DC):
            act.wait_ge(self.hT_ps, DC * n + c + 1)
            act.activation(self.hT[par][:, c, :], self.turned[c][:, :], ACT.Identity,
                           scale=self.W["col"][:, self.gain, c:c + 1],
                           bias=self.W["col"][:, self.gain + 1, c:c + 1]).then_inc(self.hT_sb, 1)

    def add_norm(self, dve, k, par, free):
        n = 2 * k + par
        dve.wait_ge(self.xb_done, n + 1)
        free(k, par)
        for i in range(TPC // 2):
            dve.wait_ge(self.wo_done, 2 * n + i + 1)
            last = dve.tensor_tensor(self.y[par][:, 2 * i:2 * i + 2, :],
                                     self.wo_ps[i].rearrange("p (t d) -> p t d", t=2),
                                     self.x[par][:, 2 * i:2 * i + 2, :], ALU.add)
        last.then_inc(self.y_done, 1)
        dve.wait_ge(self.y_done, n + 1)
        norm_stats(dve, self.y[par], self.stats, self.moments, self.own, n + 1).then_inc(self.stats_done, 1)
        dve.wait_ge(self.rstd_done, n + 1)
        need(dve, self.hT_ps, DC * n)
        normalize(dve, self.xhat, self.y[par], self.moments, self.rstd).then_inc(self.xhat_done, 1)


def chunk_view(x):
    return x.rearrange("b (c t p) d -> (b c) p t d", c=CPB, t=TPC)


def cross_q(nc, a, W, s):
    col = W["col"]
    with ExitStack() as stack:
        m = Arena(nc, stack, "cq")
        r = Residual(m, nc, a, W, s, chunk_view(a["x"]), W["sa_wo"], 0, 2, None)
        full = [m.sb(f"full{i}", [P, DC, CH]) for i in range(2)]
        hi = [m.sb(f"hi{i}", [P, DC, CH], F32R) for i in range(2)]
        lo = [m.sb(f"lo{i}", [P, DC, CH], F32R) for i in range(2)]
        q_ps = [m.ps(f"q{i}", [P, CH]) for i in range(DC)]
        stored, q_done, hi_done, full_done, lo_done = (
            m.sems("stored", 2), m.sem("q_done"), m.sem("hi_done"), m.sem("full_done"), m.sem("lo_done"))
        y_stored = m.sems("y_stored", 2)
        STORES = 16 * 2 * DC
        block = stack.enter_context(nc.Block())

        @block.sync
        def _(sp):
            def step(k, par):
                if live(k, par, NCH):
                    r.load(sp, k, par)
                k1, p1 = back(k, par, 1)
                if live(k1, p1, NCH):
                    n1 = 2 * k1 + p1
                    sp.wait_ge(r.y_done, n1 + 1)
                    sp.dma_start(s["x1"][n1], r.y[p1][:, :, :]).then_inc(y_stored[p1], 16)
                k2, p2 = back(k, par, 3)
                if live(k2, p2, NCH):
                    n2 = 2 * k2 + p2
                    sp.wait_ge(hi_done, DC * (n2 + 1))
                    sp.wait_ge(lo_done, DC * (n2 + 1))
                    for c in range(DC):
                        for part, src in enumerate((hi, lo)):
                            dst = s["cq"][part].rearrange("(b c g) q r t -> b c q g r t", b=B, c=DC)
                            sp.dma_start(dst[k2, c, p2], words(src[p2][:, c, :]))\
                                .then_inc(stored[p2], 16)

            steps(sp, step, NCH + 3, 4, NCH)
            for par in range(2):
                sp.wait_ge(stored[par], STORES * NCH // 2)
                sp.wait_ge(y_stored[par], 16 * NCH // 2)

        @block.gpsimd
        def _(pool):
            def step(k, par):
                if live(k, par, NCH):
                    r.pool_add(pool, k, par)
                k2, p2 = back(k, par, 2)
                if live(k2, p2, NCH):
                    n2 = 2 * k2 + p2
                    need(pool, stored[p2], STORES * k2)
                    for i in range(DC):
                        pool.wait_ge(hi_done, DC * n2 + i + 1)
                        pool.tensor_tensor(lo[p2][:, i, :], full[p2][:, i, :], hi[p2][:, i, :].bitcast(F32),
                                           ALU.subtract).then_inc(lo_done, 1)
                if live(k, par, NCH):
                    r.pool_rstd(pool, k, par)

            steps(pool, step, NCH + 2, 4, NCH)

        @block.tensor
        def _(pe):
            def step(k, par):
                if live(k, par, NCH):
                    r.turn_att(pe, k, par)
                k2, p2 = back(k, par, 2)
                if live(k2, p2, NCH):
                    n2 = 2 * k2 + p2
                    pe.wait_ge(r.hT_sb, DC * (n2 + 1))
                    for i in range(DC):
                        need(pe, full_done, DC * (n2 - 1) + i + 1)
                        for c in range(DC):
                            last = pe.matmul(q_ps[i][:, :], W["ca_wq"][:, c, i * P:(i + 1) * P], r.hT[p2][:, c, :],
                                             start=(c == 0), stop=(c == DC - 1))
                        last.then_inc(q_done, 1)
                if live(k, par, NCH):
                    r.project(pe, k, par)
                k1, p1 = back(k, par, 1)
                if live(k1, p1, NCH):
                    r.turn_h(pe, k1, p1)

            steps(pe, step, NCH + 2, 4, NCH)

        @block.scalar
        def _(act):
            def step(k, par):
                if live(k, par, NCH):
                    r.take_att(act, k, par)
                k2, p2 = back(k, par, 2)
                if live(k2, p2, NCH):
                    n2 = 2 * k2 + p2
                    need(act, stored[p2], STORES * k2)
                    for i in range(DC):
                        act.wait_ge(full_done, DC * n2 + i + 1)
                        act.activation(hi[p2][:, i, :], full[p2][:, i, :], ACT.Copy).then_inc(hi_done, 1)
                k1, p1 = back(k, par, 1)
                if live(k1, p1, NCH):
                    r.take_h(act, k1, p1, q_done, DC * (2 * k1 + p1 - 1))

            steps(act, step, NCH + 2, 4, NCH)

        @block.vector
        def _(dve):
            def free(k, par):
                need(dve, y_stored[par], 16 * k)

            def step(k, par):
                k2, p2 = back(k, par, 2)
                if live(k2, p2, NCH):
                    n2 = 2 * k2 + p2
                    need(dve, lo_done, DC * (n2 - 1))
                    for i in range(DC):
                        dve.wait_ge(q_done, DC * n2 + i + 1)
                        dve.tensor_scalar(full[p2][:, i, :], q_ps[i][:, :], col[:, 9, i:i + 1], None,
                                          ALU.add).then_inc(full_done, 1)
                if live(k, par, NCH):
                    r.add_norm(dve, k, par, free)

            steps(dve, step, NCH + 2, 4, NCH)


def cross_attention(nc, a, W, s):
    ident = W["ident"]
    UB = NG * CPB
    with ExitStack() as stack:
        m = Arena(nc, stack, "ca")
        q = [m.sb(f"q{i}", [ROWS, CPB, HG, CH], F32R) for i in range(NG)]
        kk = [m.sb(f"k{i}", [ROWS, HG, NKE], F32R) for i in range(NG)]
        v = [m.sb(f"v{i}", [NK, HG, VW]) for i in range(NG)]
        mask = [m.sb(f"mask{i}", [NK, 1]) for i in range(NG)]
        probs = [m.sb(f"probs{i}", [NK, HG, CH]) for i in range(2)]
        maxima = [m.sb(f"maxima{i}", [P, HG, TPC]) for i in range(2)]
        maxrows, maxT = m.sb("maxrows", [P, 2, HG * TPC], F32R), m.sb("maxT", [2 * HG * TPC, P], F32R)
        o_sb = m.sb("o_sb", [P, CH])
        inv = m.sb("inv", [P, TPC, HG])
        o_out = [m.sb(f"o_out{i}", [P, TPC, HG, HD]) for i in range(2)]
        s_max = [m.ps(f"s_max{i}", [P, TPC, P]) for i in range(2)]
        s_exp = [m.ps(f"s_exp{i}", [P, CH]) for i in range(2)]
        o_ps = [m.ps(f"o{i}", [P, CH]) for i in range(2)]
        mT, oT = m.ps("mT", [P, CH]), m.ps("oT", [P, CH])
        rows_in, out_done = m.sems("rows_in", NG), m.sems("out_done", 2)
        zero, max_in, scored, reduced, negated, own, maxT_done, maxT_sb = (
            m.sem(n) for n in ("zero", "max_in", "scored", "reduced", "negated", "own", "maxT_done", "maxT_sb"))
        s_done, exp_done, pv_done, o_done, oT_done, inv_done, out_ready = (
            m.sem(n) for n in ("s_done", "exp_done", "pv_done", "o_done", "oT_done", "inv_done", "out_ready"))
        LOADS = 16 * (4 * CPB + 4 + 3)
        block = stack.enter_context(nc.Block())

        def batches(eng, step):
            step(0)
            with eng.Fori(1, B - 1) as b:
                step(b)
            step(B - 1)

        def there(b, unit):
            return not isinstance(b, int) or 0 <= b * UB + unit < NU

        @block.sync
        def _(sp):
            def load(b, g):
                n = NG * b + g
                stack_rows(sp, s["cq"], n, 0, q[g], rows_in[g])
                for lo in range(2):
                    for half in range(2):
                        src = s["ck"][lo].rearrange("(n h e) k -> n e h k", n=BG, h=HG)[n]
                        row = (2 * half + lo) * HD
                        sp.dma_start(words(kk[g][row:row + HD, :, 0:NK]), src).then_inc(rows_in[g], 16)
                sp.dma_start(words(kk[g][ROW_MASK:ROW_MASK + 1, :, 0:NK]),
                             s["cmask"][n].rearrange("n (h k) -> n h k", h=HG)).then_inc(rows_in[g], 16)
                sp.dma_start(mask[g][:, :], s["cmask"][n][:, 0:NK].rearrange("n k -> k n"))\
                    .then_inc(rows_in[g], 16)
                sp.dma_start(v[g].rearrange("k h e -> k (h e)"), s["cv"][n]).then_inc(rows_in[g], 16)

            def max_rows(b, unit):
                g, qc = unit // CPB % NG, unit % CPB
                sp.wait_ge(maxT_sb, UB * b + unit + 1)
                rows = words(q[g][ROW_MAX:ROWS, qc, :, :]).rearrange("r h (t p) -> r (h t) p", t=TPC)
                sp.dma_start(rows, words(maxT[:, :])).then_inc(max_in, 16)

            def store(b, unit):
                g, qc = unit // CPB % NG, unit % CPB
                sp.wait_ge(out_ready, UB * b + unit + 1)
                dst = s["attn"][NG * b + unit // CPB, qc]
                sp.dma_start(dst.rearrange("t p e -> p t e"), o_out[qc].rearrange("p t h e -> p t (h e)"))\
                    .then_inc(out_done[qc], 16)

            sp.wait_ge(zero, 4 * NG)
            load(0, 0)
            load(0, 1)
            max_rows(0, 0)

            def step(b):
                for unit in range(UB):
                    if unit % CPB == 0 and there(b, unit + 2 * CPB):
                        g = unit // CPB + 2
                        need(sp, pv_done, UB * b + unit - 2 * CPB)
                        load(b + g // NG, g % NG)
                    if there(b, unit + 1):
                        max_rows(b, unit + 1)
                    if there(b, unit - 1):
                        store(b, unit - 1)

            batches(sp, step)
            store(B - 1, UB - 1)
            for qc in range(CPB):
                sp.wait_ge(out_done[qc], 16 * BG)

        @block.gpsimd
        def _(pool):
            for g in range(NG):
                need(pool, zero, 4 * g)
                pool.memset(words(q[g][ROW_MASK:ROWS_SCORE, :, :, :]), 0.0).then_inc(zero, 1)
                pool.wait_ge(zero, 4 * g + 1)
                pool.memset(words(kk[g][:, :, :]), 0.0).then_inc(zero, 1)
                pool.wait_ge(zero, 4 * g + 2)
                pool.memset(words(kk[g][ROW_MAX:ROWS, :, :]), 1.0).then_inc(zero, 1)
                pool.wait_ge(zero, 4 * g + 3)
                pool.memset(words(q[g][ROW_MASK:ROW_MASK + 1, :, :, :]), 1.0).then_inc(zero, 1)

        @block.tensor
        def _(pe):
            pe.wait_ge(zero, 4 * NG)

            def score_max(b, unit, h):
                g, qc = unit // CPB % NG, unit % CPB
                need(pe, reduced, HG * (UB * b + unit) + h - 1)
                for t in range(TPC):
                    last = pe.matmul(s_max[h % 2][:, t, 0:NKE],
                                     q[g][0:ROWS_SCORE, qc, h, t * P:(t + 1) * P],
                                     kk[g][0:ROWS_SCORE, h, :], start=True, stop=True)
                last.then_inc(scored, 1)

            def turn_max(b, unit):
                pe.wait_ge(negated, UB * b + unit + 1)
                need(pe, maxT_sb, UB * b + unit)
                pe.transpose(mT[0:2 * HG * TPC, 0:P], maxrows[:, :, :].bitcast(F32).rearrange("p r j -> p (r j)"),
                             ident[:, :]).then_inc(maxT_done, 1)

            def values(b, unit):
                g, qc = unit // CPB % NG, unit % CPB
                u = UB * b + unit
                need(pe, o_done, u - 1)
                pe.wait_ge(exp_done, HG * (u + 1))
                for h in range(HG):
                    last = pe.matmul(o_ps[qc][h * VW:(h + 1) * VW, :], v[g][:, h, :], probs[qc][:, h, :],
                                     start=True, stop=True, tile_position=(0, h * VW))
                last.then_inc(pv_done, 1)

            def turn_out(b, unit):
                u = UB * b + unit
                pe.wait_ge(o_done, u + 1)
                need(pe, out_ready, u)
                for t in range(TPC):
                    last = pe.transpose(oT[:, t * P:(t + 1) * P], o_sb[:, t * P:(t + 1) * P], ident[:, :])
                last.then_inc(oT_done, 1)

            pe.wait_ge(rows_in[0], LOADS)
            for unit in range(2):
                for h in range(HG):
                    score_max(0, unit, h)
                if unit == 0:
                    turn_max(0, 0)

            def step(b):
                for unit in range(UB):
                    u = UB * b + unit
                    g, qc = unit // CPB, unit % CPB
                    ahead = unit + 2
                    if there(b, unit + 1):
                        turn_max(b, unit + 1)
                    pe.wait_ge(max_in, 16 * (u + 1))
                    if there(b, ahead) and qc == 0:
                        ga = ahead // CPB
                        pe.wait_ge(rows_in[ga % NG], LOADS * (b + ga // NG + 1))
                    for h in range(HG):
                        need(pe, exp_done, HG * u + h - 1)
                        pe.matmul(s_exp[h % 2][0:NK, :], kk[g][:, h, 0:NK], q[g][:, qc, h, :],
                                  start=True, stop=True).then_inc(s_done, 1)
                        if there(b, ahead):
                            score_max(b, ahead, h)
                        if h == 0 and there(b, unit - 1):
                            values(b, unit - 1)
                        if h == 2 and there(b, unit - 1):
                            turn_out(b, unit - 1)

            batches(pe, step)
            values(B - 1, UB - 1)
            turn_out(B - 1, UB - 1)

        @block.scalar
        def _(act):
            def take_max(b, unit):
                u = UB * b + unit
                act.wait_ge(maxT_done, u + 1)
                need(act, max_in, 16 * u)
                act.activation(maxT[:, :], mT[0:2 * HG * TPC, 0:P], ACT.Copy).then_inc(maxT_sb, 1)

            def take_out(b, unit):
                u = UB * b + unit
                act.wait_ge(pv_done, u + 1)
                need(act, oT_done, u)
                act.activation(o_sb[:, :], o_ps[unit % 2][:, :], ACT.Copy).then_inc(o_done, 1)

            take_max(0, 0)

            def step(b):
                for unit in range(UB):
                    u = UB * b + unit
                    g, qc = unit // CPB, unit % CPB
                    if there(b, unit + 1):
                        take_max(b, unit + 1)
                    need(act, pv_done, u - 1)
                    if qc == 0:
                        act.wait_ge(rows_in[g], LOADS * (b + 1))
                    for h in range(HG):
                        act.wait_ge(s_done, HG * u + h + 1)
                        act.activation(probs[qc][:, h, :], s_exp[h % 2][0:NK, :], ACT.Exp, scale=SCALE,
                                       bias=mask[g][:, 0:1]).then_inc(exp_done, 1)
                        if h == 1 and there(b, unit - 1):
                            take_out(b, unit - 1)

            batches(act, step)
            take_out(B - 1, UB - 1)

        @block.vector
        def _(dve):
            def reduce(b, unit, h):
                dve.wait_ge(scored, HG * (UB * b + unit) + h + 1)
                dve.tensor_reduce(maxima[unit % 2][:, h, :], s_max[h % 2][:, :, 0:NK], AX_X, ALU.max).then_inc(reduced, 1)

            def negate(b, unit):
                u = UB * b + unit
                dve.wait_ge(reduced, HG * (u + 1))
                need(dve, maxT_done, u)
                split_max(dve, maxima[unit % 2].rearrange("p h t -> p (h t)"), maxrows, own, u + 1).then_inc(negated, 1)

            def scale_out(b, unit):
                u = UB * b + unit
                dve.wait_ge(oT_done, u + 1)
                sums = oT.rearrange("p (t h e) -> p t h e", t=TPC, h=HG)
                dve.reciprocal(inv[:, :, :], sums[:, :, :, HD]).then_inc(inv_done, 1)
                dve.wait_ge(inv_done, u + 1)
                need(dve, out_done[unit % 2], 16 * (NG * b + unit // CPB))
                dve.tensor_tensor(o_out[unit % 2][:, :, :, :], sums[:, :, :, 0:HD],
                                  inv.rearrange("p t (h e) -> p t h e", e=1).to_broadcast([P, TPC, HG, HD]),
                                  ALU.mult).then_inc(out_ready, 1)

            for unit in range(2):
                for h in range(HG):
                    reduce(0, unit, h)
                negate(0, unit)

            def step(b):
                for unit in range(UB):
                    for h in range(HG):
                        if there(b, unit + 2):
                            reduce(b, unit + 2, h)
                        if h == 3 and there(b, unit - 1):
                            scale_out(b, unit - 1)
                    if there(b, unit + 2):
                        negate(b, unit + 2)

            batches(dve, step)
            scale_out(B - 1, UB - 1)


def mlp(nc, a, W, s, out):
    with ExitStack() as stack:
        m = Arena(nc, stack, "mlp")
        r = Residual(m, nc, a, W, s, s["x1"], W["ca_wo"], 1, 4, 2)
        row2 = [m.sb(f"row2_{i}", [P, D]) for i in range(2)]
        yb = [m.sb(f"yb{i}", [P, TPC, D]) for i in range(2)]
        hidden = [m.sb(f"hidden{i}", [P, FC, CH]) for i in range(2)]
        res = [m.sb(f"res{i}", [P, TPC, D]) for i in range(2)]
        w1_ps = [m.ps(f"w1_{i}", [P, CH]) for i in range(2)]
        w2_ps = [m.ps(f"w2_{i}", [P, 2 * D]) for i in range(2)]
        row_in, stored = m.sems("row_in", 2), m.sems("stored", 2)
        w1_done, hidden_done, w2_done, yb_done, res_done = (
            m.sem(n) for n in ("w1_done", "hidden_done", "w2_done", "yb_done", "res_done"))
        out_dram = chunk_view(out)
        block = stack.enter_context(nc.Block())

        @block.sync
        def _(sp):
            def step(k, par):
                if live(k, par, NCH):
                    need(sp, yb_done, 2 * k + par - 1)
                    sp.dma_start(row2[par][:, :], s["badd"][k][:, 2 * D:3 * D].to_broadcast([P, D]))\
                        .then_inc(row_in[par], 16)
                    r.load(sp, k, par)
                k2, p2 = back(k, par, 3)
                if live(k2, p2, NCH):
                    n2 = 2 * k2 + p2
                    sp.wait_ge(res_done, 2 * (n2 + 1))
                    sp.dma_start(out_dram[n2], res[p2][:, :, :]).then_inc(stored[p2], 16)

            steps(sp, step, NCH + 3, 4, NCH)
            for par in range(2):
                sp.wait_ge(stored[par], 16 * NCH // 2)

        @block.gpsimd
        def _(pool):
            def step(k, par):
                n = 2 * k + par
                r.pool_add(pool, k, par)
                r.pool_rstd(pool, k, par)
                pool.wait_ge(row_in[par], 16 * (k + 1))
                need(pool, res_done, 2 * (n - 1))
                pool.tensor_tensor(yb[par][:, :, :], r.y[par][:, :, :],
                                   row2[par].rearrange("p (t d) -> p t d", t=1).to_broadcast([P, TPC, D]),
                                   ALU.add).then_inc(yb_done, 1)

            steps(pool, step, NCH, 2, NCH)

        @block.tensor
        def _(pe):
            def step(k, par):
                if live(k, par, NCH):
                    r.turn_att(pe, k, par)
                k2, p2 = back(k, par, 2)
                if live(k2, p2, NCH):
                    up(2 * k2 + p2, p2)
                if live(k, par, NCH):
                    r.project(pe, k, par)
                if live(k2, p2, NCH):
                    down(2 * k2 + p2, p2)
                k1, p1 = back(k, par, 1)
                if live(k1, p1, NCH):
                    r.turn_h(pe, k1, p1)

            def up(n, par):
                pe.wait_ge(r.hT_sb, DC * (n + 1))
                for f in range(FC):
                    need(pe, hidden_done, FC * n + f - 1)
                    for c in range(DC):
                        last = pe.matmul(w1_ps[f % 2][:, :], W["w1"][:, c, f * P:(f + 1) * P], r.hT[par][:, c, :],
                                         start=(c == 0), stop=(c == DC - 1))
                    last.then_inc(w1_done, 1)

            def down(n, par):
                pe.wait_ge(hidden_done, FC * (n + 1))
                for t in range(TPC):
                    if t % 2 == 0:
                        need(pe, res_done, 2 * (n - 1) + t // 2 + 1)
                    for f in range(FC):
                        last = pe.matmul(w2_ps[t // 2][:, (t % 2) * D:(t % 2 + 1) * D],
                                         hidden[par][:, f, t * P:(t + 1) * P], W["w2"][:, f, :],
                                         start=(f == 0), stop=(f == FC - 1))
                    if t % 2:
                        last.then_inc(w2_done, 1)

            steps(pe, step, NCH + 2, 4, NCH)

        @block.scalar
        def _(act):
            def step(k, par):
                if live(k, par, NCH):
                    r.take_att(act, k, par)
                k1, p1 = back(k, par, 2)
                if live(k1, p1, NCH):
                    n1 = 2 * k1 + p1
                    need(act, w2_done, 2 * (n1 - 1))
                    for f in range(FC):
                        act.wait_ge(w1_done, FC * n1 + f + 1)
                        act.activation(hidden[p1][:, f, :], w1_ps[f % 2][:, :], ACT.Gelu,
                                       bias=W["b1"][:, f:f + 1]).then_inc(hidden_done, 1)
                kh, ph = back(k, par, 1)
                if live(kh, ph, NCH):
                    r.take_h(act, kh, ph, w1_done, FC * (2 * kh + ph - 1))

            steps(act, step, NCH + 2, 4, NCH)

        @block.vector
        def _(dve):
            def free(k, par):
                need(dve, yb_done, 2 * k + par - 1)

            def step(k, par):
                if live(k, par, NCH):
                    r.add_norm(dve, k, par, free)
                k1, p1 = back(k, par, 2)
                if live(k1, p1, NCH):
                    n1 = 2 * k1 + p1
                    dve.wait_ge(yb_done, n1 + 1)
                    need(dve, stored[p1], 16 * k1)
                    for i in range(TPC // 2):
                        dve.wait_ge(w2_done, 2 * n1 + i + 1)
                        dve.tensor_tensor(res[p1][:, 2 * i:2 * i + 2, :],
                                          w2_ps[i].rearrange("p (t d) -> p t d", t=2),
                                          yb[p1][:, 2 * i:2 * i + 2, :], ALU.add).then_inc(res_done, 1)

            steps(dve, step, NCH + 2, 4, NCH)


def build(nc, a, out):
    def scratch(name, shape, dt=F32):
        return nc.dram_tensor(name, shape, dt, kind="Internal").ap()

    qk = scratch("qk_parts", [2, 2, BG, CPB, GW, CH])
    s = {
        "qk": qk,
        "v": scratch("v_ones", [BG, P, KT, HG * VW]),
        "ck": scratch("ctx_k_parts", [2, BG * GW, NK]),
        "cv": scratch("ctx_v", [BG, NK, HG * VW]),
        "cmask": scratch("ctx_mask", [BG, 1, HG * NK]),
        "cq": scratch("cross_q_parts", [2, BG, CPB, GW, CH]),
        "badd": scratch("rows", [B, 1, 3 * D]),
        "attn": scratch("attn", [BG, CPB, TPC, P, GW]),
        "x1": scratch("x1", [NCH, P, TPC, D]),
    }
    with ExitStack() as stack:
        def sb(name, shape):
            return stack.enter_context(nc.sbuf_tensor(name, shape, F32))

        W = {n: sb(n, [P, DC, D]) for n in ("sa_wq", "sa_wk", "sa_wv", "sa_wo", "ca_wq", "ca_wo")}
        W |= {"w1": sb("w1", [P, DC, FF]), "w2": sb("w2", [P, FC, D]), "b1": sb("b1", [P, FC]),
              "col": sb("col", [P, 10, DC]), "ident": sb("ident", [P, P]), "half": sb("half", [P, 2, TPC])}
        setup(nc, a, W, s, out)
        self_qkv(nc, a, W, s)
        self_attention(nc, a, W, s)
        cross_q(nc, a, W, s)
        cross_attention(nc, a, W, s)
        mlp(nc, a, W, s, out)


_INS = {"x": "x", "cond_1024": "cond", "ctx_1024": "ctx", "mask_BxS2_ik0": "mask"}
_WEIGHTS = ["ln1_g", "ln1_b", "ln3_g", "ln3_b", "ln2_g", "ln2_b", "sa_wq", "sa_bq", "sa_wk", "sa_bk", "sa_wv", "sa_bv",
            "sa_wo", "sa_bo", "ca_wq", "ca_bq", "ca_wk", "ca_bk", "ca_wv", "ca_bv", "ca_wo", "ca_bo", "tp_w", "tp_b",
            "w1", "b1", "w2", "b2"]


def kernel(**inputs):
    import numpy as np
    import concourse.bacc as bacc
    from concourse.bass_utils import run_bass_kernel_spmd

    nc = bacc.Bacc("TRN2", target_bir_lowering=False, num_devices=1)
    arrays, args = {}, {}
    for name, short in (_INS | {f"L0_xcond_{w}": w for w in _WEIGHTS}).items():
        v = np.ascontiguousarray(inputs[name])
        arrays[f"in_{short}"] = v
        args[short] = nc.dram_tensor(f"in_{short}", v.shape, mybir.dt.from_np(v.dtype), kind="ExternalInput").ap()
    out = nc.dram_tensor("out", (B, T, D), F32, kind="ExternalOutput").ap()
    with nc.allow_non_contiguous_dma(reason="a few short vectors are loaded as columns"):
        build(nc, args, out)
    r = run_bass_kernel_spmd(nc, [arrays], core_ids=[0])
    return r.results[0]["out"]
```

```python
from contextlib import ExitStack

import concourse.bass as bass
from concourse import mybir

ALU = mybir.AluOpType
ACT = mybir.ActivationFunctionType
AX_X = mybir.AxisListType.X
F32 = mybir.dt.float32
F32R = mybir.dt.float32r
I32 = mybir.dt.int32

P = 128
B, T, D = 4, 1024, 256
NK = 77
NKE = NK + NK % 2
H, HD = 16, 16
FF = 4 * D
DC = D // P
FC = FF // P
HG = 4
NG = H // HG
GW = HG * HD
BG = B * NG
CH = 512
TPC = CH // P
CPB = T // CH
NCH = B * CPB
KT = T // P
NU = BG * CPB
OUT_STEP = 2
MAXT_STEP = 6
LEAD = 3
EPS = 1e-5
SCALE = HD ** -0.5
MASKED = -1e30
VW = 2 * HD

ROWS_SPLIT = 4 * HD
ROW_MASK = ROWS_SPLIT
ROWS_SCORE = 96
ROW_MAX = 96
ROWS = 98


def back(k, par, n):
    return k + (par - n) // 2, (par - n) % 2


def live(k, par, count):
    return not isinstance(k, int) or 0 <= 2 * k + par < count


def reuse(item, banks):
    return next(n for n in range(1, len(banks) + 1) if banks[item - n] == banks[item])


def need(eng, sem, value):
    if not isinstance(value, int) or value > 0:
        eng.wait_ge(sem, value)


def steps(eng, step, total, first, last):
    for n in range(first):
        step(n // 2, n % 2)
    with eng.Fori(first // 2, last // 2) as k:
        step(k, 0)
        step(k, 1)
    for n in range(last, total):
        step(n // 2, n % 2)


class Arena:

    def __init__(self, nc, stack, tag):
        self.nc, self.stack, self.tag = nc, stack, tag

    def sb(self, name, shape, dt=F32):
        return self.stack.enter_context(self.nc.sbuf_tensor(f"{self.tag}_{name}", shape, dt))

    def ps(self, name, shape):
        return self.stack.enter_context(self.nc.psum_tensor(f"{self.tag}_{name}", shape, F32))

    def sem(self, name):
        return self.stack.enter_context(self.nc.semaphore(f"{self.tag}_{name}"))

    def sems(self, name, n):
        return [self.sem(f"{name}{i}") for i in range(n)]


def words(ap):
    return ap.bitcast(F32)


def chunked(w):
    return w.rearrange("(c p) n -> p c n", p=P)


def column(v):
    return v.rearrange("(c p) -> p c", p=P)


class Shared:

    def __init__(self, m):
        self.rows = [m.sb(f"rows{i}", [ROWS, CPB, HG, CH], F32R) for i in range(4)]
        self.v = [m.sb(f"v{i}", [P, KT, HG, VW]) for i in range(2)]
        self.self_in, self.qkv_stored = m.sems("self_in", 2), m.sems("qkv_stored", 2)
        self.ck = [m.sb(f"ck{i}", [ROWS, HG, NKE], F32R) for i in range(NG)]
        self.cv = [m.sb(f"cv{i}", [P, HG, VW]) for i in range(NG)]
        self.mask = [m.sb(f"mask{i}", [NK, 1]) for i in range(NG)]
        self.cross_in = [m.sems(f"cross_in{i}_", CPB) for i in range(NG)]
        self.context_in, self.cq_stored = m.sems("context_in", NG), m.sems("cq_stored", 2)
        self.att = [m.sb(f"att{i}", [P, TPC, D]) for i in range(2)]
        self.x, self.x_in = [m.sb(f"x{i}", [P, TPC, D]) for i in range(2)], m.sems("x_in", 2)
        self.badd = [m.sb(f"badd{i}", [P, D]) for i in range(2)]
        self.residual_in = [m.sems(f"residual_in{i}_", 2) for i in range(2)]

    def constant_q(self, eng, zero, base, i):
        need(eng, zero, base)
        eng.memset(words(self.rows[i][ROWS_SPLIT:ROWS_SCORE, :, :, :]), 0.0).then_inc(zero, 1)
        eng.wait_ge(zero, base + 1)
        eng.memset(words(self.rows[i][ROW_MASK:ROW_MASK + 1, :, :, :]), 1.0).then_inc(zero, 1)

    def constant_k(self, eng, zero, base, i):
        need(eng, zero, base)
        eng.memset(words(self.rows[i][ROWS_SPLIT:ROWS_SCORE, :, :, :]), 0.0).then_inc(zero, 1)
        eng.wait_ge(zero, base + 1)
        eng.memset(words(self.rows[i][ROW_MAX:ROWS, :, :, :]), 1.0).then_inc(zero, 1)

    def load_self(self, sp, s, n, par):
        for which in range(2):
            stack_rows(sp, s["qk"][which], n, which, self.rows[2 * which + par], self.self_in[par])
        sp.dma_start(self.v[par][:, :, :, :].rearrange("p t h e -> p t (h e)"), s["v"][n])\
            .then_inc(self.self_in[par], 16)

    def load_cross_q(self, sp, s, b, g, qc):
        stack_rows(sp, s["cq"], NG * b + g, 0, self.rows[g], self.cross_in[g][qc], range(qc, qc + 1))

    def load_cross_kv(self, pool, s, b, g):
        n, sem = NG * b + g, self.context_in[g]
        for lo in range(2):
            for half in range(2):
                src = s["ck"][lo].rearrange("(n h e) k -> n e h k", n=BG, h=HG)[n]
                row = (2 * half + lo) * HD
                pool.dma_start(words(self.ck[g][row:row + HD, :, 0:NK]), src).then_inc(sem, 16)
        pool.dma_start(words(self.ck[g][ROW_MASK:ROW_MASK + 1, :, 0:NK]),
                       s["cmask"][n].rearrange("n (h k) -> n h k", h=HG)).then_inc(sem, 16)
        pool.dma_start(self.mask[g][:, :], s["cmask"][n][:, 0:NK].rearrange("n k -> k n")).then_inc(sem, 16)
        pool.dma_start(self.cv[g][0:NK, :, :].rearrange("k h e -> k (h e)"), s["cv"][n]).then_inc(sem, 16)

    def load_residual(self, sp, s, x_dram, row, k, par):
        sem = self.residual_in[row][par]
        for g in range(NG):
            src = s["attn"].rearrange("(b g) c t p e -> b g c p t e", b=B)[k, g, par]
            sp.dma_start(self.att[par][:, :, g * GW:(g + 1) * GW], src).then_inc(sem, 16)
        sp.dma_start(self.x[par][:, :, :], x_dram[2 * k + par]).then_inc(sem, 16)
        sp.dma_start(self.badd[par][:, :], s["badd"][k][:, row * D:(row + 1) * D].to_broadcast([P, D]))\
            .then_inc(sem, 16)


CQ_STORES = 16 * 2 * DC
QKV_STORES = 2 * 2 * DC + NG
SELF_LOADS = 16 * (2 * 4 * CPB + 1)
CROSS_Q_LOADS = 16 * 4
CROSS_KV_LOADS = 16 * 7
RESIDUAL_LOADS = 16 * (NG + 2)


def setup(nc, a, W, s, shared):
    ident, half = W["ident"], W["half"]
    with ExitStack() as stack:
        m = Arena(nc, stack, "setup")
        ctx = m.sb("ctx", [NK, B, D])
        ctxT = m.sb("ctxT", [P, DC, B * NK])
        wk, wv = m.sb("ca_wk", [P, DC, D]), m.sb("ca_wv", [P, DC, D])
        kfull = m.sb("kfull", [P, DC, B * NK])
        khi, klo = (m.sb(n, [P, DC, B * NK], F32R) for n in ("khi", "klo"))
        vaug = m.sb("vaug", [NK, B, H, VW])
        mask_i, mask_f = m.sb("mask_i", [NK, B], I32), m.sb("mask_f", [NK, B])
        maskrow_i = m.sb("maskrow_i", [BG, HG * NK], I32)
        maskrow_f = m.sb("maskrow_f", [BG, HG * NK])
        maskrow = m.sb("maskrow", [BG, HG * NK], F32R)
        cond = m.sb("cond", [B, D])
        sig, silu = m.sb("sig", [B, D]), m.sb("silu", [B, D])
        siluT, bvT = m.sb("siluT", [P, DC, B]), m.sb("bvT", [P, 2, DC])
        bv4 = m.sb("bv4", [P, 2, DC, B])
        tpw = m.sb("tpw", [P, DC, 3 * D])
        tprow, brow = m.sb("tprow", [B, 3 * D]), m.sb("brow", [B, 3 * D])
        badd = m.sb("badd", [B, 3 * D])
        trans = [m.ps(f"trans{c}", [P, 512]) for c in range(DC)]
        pk = [m.ps(f"pk{c}", [P, 512]) for c in range(DC)]
        pv = [m.ps(f"pv{i}", [P, 512]) for i in range(2)]
        prow = [m.ps(f"prow{i}", [P, 512]) for i in range(2)]
        ctx_in, cw_in, cond_in, tp_in, mask_in, w_in = (
            m.sem(n) for n in ("ctx_in", "cw_in", "cond_in", "tp_in", "mask_in", "w_in"))
        const, zero, own, ctxT_ps, ctxT_sb, k_ps, khi_sb, k_sb, klo_sb, v_ps, ones_sb, v_sb = (
            m.sem(n) for n in ("const", "zero", "own", "ctxT_ps", "ctxT_sb", "k_ps", "khi_sb", "k_sb",
                               "klo_sb", "v_ps", "ones_sb", "v_sb"))
        e_sb, silu_sb, siluT_ps, siluT_sb, bv_sb, row_ps, row_sb, maskrow_sb, stored = (
            m.sem(n) for n in ("e_sb", "silu_sb", "siluT_ps", "siluT_sb", "bv_sb", "row_ps", "row_sb",
                               "maskrow_sb", "stored"))
        dve_rows, pool_rows = m.sem("dve_rows"), m.sem("pool_rows")
        block = stack.enter_context(nc.Block())

        @block.sync
        def _(sp):
            sp.dma_start(ctx[:, :, :], a["ctx"].rearrange("b k d -> k b d")).then_inc(ctx_in, 16)
            sp.dma_start(wk[:, :, :], chunked(a["ca_wk"])).then_inc(cw_in, 16)
            sp.dma_start(wv[:, :, :], chunked(a["ca_wv"])).then_inc(cw_in, 16)
            sp.dma_start(W["col"][:, 7, :], column(a["ca_bk"])).then_inc(cw_in, 16)
            sp.dma_start(mask_i[:, :], a["mask"].rearrange("b k -> k b")).then_inc(mask_in, 16)
            for b in range(B):
                sp.dma_start(maskrow_i[b * NG:(b + 1) * NG, :].rearrange("g (h k) -> g h k", h=HG),
                             a["mask"][b:b + 1, :].rearrange("b (u k) -> b u k", u=1).to_broadcast([NG, HG, NK]))\
                    .then_inc(mask_in, 16)
            for par in range(2):
                sp.dma_start(shared.x[par][:, :, :], chunk_view(a["x"])[par]).then_inc(shared.x_in[par], 16)
            for name in ("sa_wq", "sa_wk", "sa_wv", "sa_wo", "ca_wq", "ca_wo"):
                sp.dma_start(W[name][:, :, :], chunked(a[name])).then_inc(w_in, 16)
            for n, name in enumerate(("ln1_g", "ln1_b", "ln3_g", "ln3_b", "ln2_g", "ln2_b", "sa_bq")):
                sp.dma_start(W["col"][:, n, :], column(a[name])).then_inc(w_in, 16)
            for n, name in enumerate(("sa_bk", "ca_bq")):
                sp.dma_start(W["col"][:, 8 + n, :], column(a[name])).then_inc(w_in, 16)
            sp.dma_start(W["b1"][:, :], column(a["b1"])).then_inc(w_in, 16)

            sp.wait_ge(khi_sb, DC)
            sp.wait_ge(klo_sb, DC)
            for part, src in enumerate((khi, klo)):
                for c in range(DC):
                    dst = s["ck"][part].rearrange("(b c r) k -> c r b k", b=B, c=DC)[c]
                    sp.dma_start(dst, words(src[:, c, :]).rearrange("r (b k) -> r b k", b=B)).then_inc(stored, 16)
            sp.wait_ge(v_sb, B)
            sp.dma_start(s["cv"].rearrange("n k e -> k n e"),
                         vaug.rearrange("k b (g h) e -> k (b g) (h e)", g=NG)).then_inc(stored, 16)
            sp.wait_ge(maskrow_sb, 1)
            sp.dma_start(s["cmask"].rearrange("n u k -> (n u) k"), words(maskrow[:, :])).then_inc(stored, 16)
            sp.wait_ge(row_sb, 2)
            sp.dma_start(s["badd"].rearrange("b u d -> (b u) d"), badd[:, :]).then_inc(stored, 16)
            sp.wait_ge(stored, 16 * (2 * DC + 3))
            sp.wait_ge(w_in, 16 * 16)

        @block.gpsimd
        def _(pool):
            pool.memset(ident[:, :], 0.0).then_inc(zero, 1)
            pool.memset(half[:, 0, :], EPS).then_inc(const, 1)
            pool.memset(half[:, 1, :], -0.5).then_inc(const, 1)
            pool.wait_ge(zero, 1)
            pool.affine_select(out=ident[:, :], in_=ident[:, :], compare_op=ALU.not_equal, fill=1.0,
                               base=0, pattern=[[-1, P]], channel_multiplier=1).then_inc(const, 1)
            pool.memset(vaug[:, :, :, HD:VW], 1.0).then_inc(ones_sb, 1)
            pool.wait_ge(ones_sb, 1)
            for i in range(2):
                shared.constant_k(pool, pool_rows, 2 * i, 2 + i)
            shared.constant_q(pool, pool_rows, 4, 1)
            pool.wait_ge(pool_rows, 6)
            for c in range(DC):
                pool.wait_ge(khi_sb, c + 1)
                pool.tensor_tensor(klo[:, c, :], kfull[:, c, :], khi[:, c, :].bitcast(F32),
                                   ALU.subtract).then_inc(klo_sb, 1)

        @block.scalar
        def _(act):
            act.dma_start(cond[:, :], a["cond"]).then_inc(cond_in, 16)
            act.dma_start(tpw[:, :, :], chunked(a["tp_w"])).then_inc(tp_in, 16)
            act.dma_start(tprow[:, :], a["tp_b"].rearrange("(u n) -> u n", u=1).to_broadcast([B, 3 * D])).then_inc(tp_in, 16)
            for n, name in enumerate(("sa_bo", "ca_bo", "b2")):
                act.dma_start(brow[:, n * D:(n + 1) * D],
                              a[name].rearrange("(u n) -> u n", u=1).to_broadcast([B, D])).then_inc(tp_in, 16)
            for n, name in enumerate(("sa_bv", "ca_bv")):
                act.dma_start(bvT[:, n, :], column(a[name])).then_inc(tp_in, 16)
            act.wait_ge(cond_in, 16)
            act.activation(sig[:, :], cond[:, :], ACT.Exp, scale=-1.0).then_inc(e_sb, 1)
            for c in range(DC):
                act.wait_ge(k_sb, c + 1)
                act.activation(khi[:, c, :], kfull[:, c, :], ACT.Copy).then_inc(khi_sb, 1)

        @block.tensor
        def _(pe):
            pe.wait_ge(const, 3)
            pe.wait_ge(ctx_in, 16)
            for c in range(DC):
                for b in range(B):
                    last = pe.transpose(trans[c][:, b * NK:(b + 1) * NK], ctx[:, b, c * P:(c + 1) * P],
                                        ident[0:NK, 0:NK])
                last.then_inc(ctxT_ps, 1)
            pe.wait_ge(ctxT_sb, DC)
            pe.wait_ge(cw_in, 48)
            for m_ in range(DC):
                for c in range(DC):
                    last = pe.matmul(pk[m_][:, 0:B * NK], wk[:, c, m_ * P:(m_ + 1) * P], ctxT[:, c, :],
                                     start=(c == 0), stop=(c == DC - 1))
                last.then_inc(k_ps, 1)
            for b in range(B):
                for c in range(DC):
                    last = pe.matmul(pv[b // 2][0:NK, (b % 2) * D:(b % 2 + 1) * D],
                                     ctxT[:, c, b * NK:(b + 1) * NK], wv[:, c, :],
                                     start=(c == 0), stop=(c == DC - 1))
                last.then_inc(v_ps, 1)
            pe.wait_ge(silu_sb, 1)
            for c in range(DC):
                last = pe.transpose(trans[0][:, c * B:(c + 1) * B], silu[:, c * P:(c + 1) * P], ident[0:B, 0:B])
            last.then_inc(siluT_ps, 1)
            pe.wait_ge(siluT_sb, 1)
            pe.wait_ge(bv_sb, 1)
            pe.wait_ge(tp_in, 16 * 7)
            pe.wait_ge(w_in, 16 * 16)
            for n in range(3):
                dst = prow[n // 2][0:B, (n % 2) * D:(n % 2 + 1) * D]
                for c in range(DC):
                    last = pe.matmul(dst, siluT[:, c, :], tpw[:, c, n * D:(n + 1) * D],
                                     start=(c == 0), stop=(c == DC - 1 and n == 2))
                if n < 2:
                    wo = W["sa_wo"] if n == 0 else W["ca_wo"]
                    for c in range(DC):
                        last = pe.matmul(dst, bv4[:, n, c, :], wo[:, c, :], start=False, stop=(c == DC - 1))
            last.then_inc(row_ps, 1)

        @block.vector
        def _(dve):
            shared.constant_q(dve, dve_rows, 0, 0)
            dve.wait_ge(mask_in, 16 * (B + 1))
            dve.tensor_copy(mask_f[:, :], mask_i[:, :]).then_inc(own, 1)
            dve.tensor_copy(maskrow_f[:, :], maskrow_i[:, :]).then_inc(own, 1)
            dve.wait_ge(own, 2)
            dve.tensor_scalar(mask_f[:, :], mask_f[:, :], 0.0, None, ALU.not_equal).then_inc(own, 1)
            dve.tensor_scalar(maskrow[:, :], maskrow_f[:, :], 0.0, MASKED, ALU.is_equal, ALU.mult)\
                .then_inc(maskrow_sb, 1)
            for c in range(DC):
                dve.wait_ge(ctxT_ps, c + 1)
                dve.tensor_copy(ctxT[:, c, :], trans[c][:, 0:B * NK]).then_inc(ctxT_sb, 1)
            dve.wait_ge(e_sb, 1)
            dve.tensor_scalar(sig[:, :], sig[:, :], 1.0, None, ALU.add).then_inc(own, 1)
            dve.wait_ge(own, 4)
            dve.reciprocal(sig[:, :], sig[:, :]).then_inc(own, 1)
            dve.wait_ge(own, 5)
            dve.tensor_tensor(silu[:, :], cond[:, :], sig[:, :], ALU.mult).then_inc(silu_sb, 1)
            dve.wait_ge(tp_in, 16 * 7)
            dve.tensor_copy(bv4[:, :, :, :],
                            bvT.rearrange("p n (c u) -> p n c u", u=1).to_broadcast([P, 2, DC, B])).then_inc(bv_sb, 1)
            dve.tensor_tensor(brow[:, :], brow[:, :], tprow[:, :], ALU.add).then_inc(own, 1)
            dve.wait_ge(siluT_ps, 1)
            dve.tensor_copy(siluT.rearrange("p c b -> p (c b)"), trans[0][:, 0:DC * B]).then_inc(siluT_sb, 1)
            dve.wait_ge(cw_in, 48)
            for c in range(DC):
                dve.wait_ge(k_ps, c + 1)
                dve.tensor_scalar(kfull[:, c, :], pk[c][:, 0:B * NK], W["col"][:, 7, c:c + 1], None,
                                  ALU.add).then_inc(k_sb, 1)
            dve.wait_ge(ones_sb, 1)
            for b in range(B):
                dve.wait_ge(v_ps, b + 1)
                dve.tensor_scalar(vaug[:, b, :, 0:HD],
                                  pv[b // 2][0:NK, (b % 2) * D:(b % 2 + 1) * D].rearrange("k (h e) -> k h e", h=H),
                                  mask_f[:, b:b + 1], None, ALU.mult).then_inc(own, 1)
                dve.tensor_scalar(vaug[:, b, :, HD:VW], vaug[:, b, :, HD:VW], mask_f[:, b:b + 1], None,
                                  ALU.mult).then_inc(v_sb, 1)
            dve.wait_ge(own, 6 + B)
            dve.wait_ge(row_ps, 1)
            for n in range(2):
                w = min(2, 3 - 2 * n) * D
                dve.tensor_tensor(badd[:, 2 * n * D:2 * n * D + w], prow[n][0:B, 0:w],
                                  brow[:, 2 * n * D:2 * n * D + w], ALU.add).then_inc(row_sb, 1)


def norm_stats(dve, x, stats, moments, own, count):
    for t in range(TPC):
        last = dve.bn_stats(stats[:, t, :], x[:, t, :])
    last.then_inc(own, 1)
    dve.wait_ge(own, count)
    dve.memset(stats[:, TPC, 0:1], 0.0)
    for t in range(TPC):
        last = dve.bn_aggr(moments[:, t, :], stats[:, t, :])
    return last


def rstd_of(pool, moments, rstd, half, own, count):
    pool.tensor_tensor(rstd[:, :], moments[:, :, 1], half[:, 0, :], ALU.add).then_inc(own, 1)
    pool.wait_ge(own, count)
    return pool.tensor_tensor(rstd[:, :], rstd[:, :], half[:, 1, :], ALU.pow)


def normalize(dve, xhat, x, moments, rstd):
    for t in range(TPC):
        last = dve.tensor_scalar(xhat[:, t, :], x[:, t, :], moments[:, t, 0:1], rstd[:, t:t + 1],
                                 ALU.subtract, ALU.mult)
    return last


def turn(pe, banks, tokens, ident, sem):
    for c in range(DC):
        for t in range(TPC):
            last = pe.transpose(banks[c][:, t * P:(t + 1) * P], tokens[:, t, c * P:(c + 1) * P], ident[:, :])
        last.then_inc(sem, 1)


def self_qkv(nc, a, W, s, shared):
    ident, half, col = W["ident"], W["half"], W["col"]
    x_dram = chunk_view(a["x"])
    NQK = 2 * DC
    with ExitStack() as stack:
        m = Arena(nc, stack, "qkv")
        x, xhat = shared.x, shared.att
        stats, moments, rstd = m.sb("stats", [P, TPC + 1, 6]), m.sb("moments", [P, TPC, 2]), m.sb("rstd", [P, TPC])
        hT = [m.sb(f"hT{i}", [P, DC, CH]) for i in range(2)]
        full = [m.sb(f"full{i}", [P, NQK, CH]) for i in range(2)]
        hi = [m.sb(f"hi{i}", [P, NQK, CH], F32R) for i in range(2)]
        lo = [m.sb(f"lo{i}", [P, NQK, CH], F32R) for i in range(2)]
        vaug = [m.sb(f"vaug{i}", [P, TPC, H, VW]) for i in range(2)]
        turned = [m.ps(f"turned{c}", [P, CH]) for c in range(DC)]
        qk_ps = [m.ps(f"qk{i}", [P, CH]) for i in range(NQK)]
        v_ps = [m.ps(f"v{i}", [P, 2 * D]) for i in range(TPC // 2)]
        x_in, stored = shared.x_in, shared.qkv_stored
        own, pool_own, ones, stats_done, rstd_done, xhat_done, turned_done, hT_done = (
            m.sem(n) for n in ("own", "pool_own", "ones", "stats_done", "rstd_done", "xhat_done", "turned_done",
                               "hT_done"))
        qk_done, hi_done, full_done, lo_done, v_done, vaug_done = (
            m.sem(n) for n in ("qk_done", "hi_done", "full_done", "lo_done", "v_done", "vaug_done"))
        zero = m.sem("zero")
        block = stack.enter_context(nc.Block())

        @block.sync
        def _(sp):
            def step(k, par):
                n = 2 * k + par
                if live(k, par, NCH) and not (isinstance(k, int) and k == 0):
                    sp.wait_ge(xhat_done, n - 1)
                    sp.dma_start(x[par][:, :, :], x_dram[n]).then_inc(x_in[par], 16)
                if isinstance(k, int) and n == NCH + 1:
                    for first in range(2):
                        sp.wait_ge(stored[first], 16 * QKV_STORES)
                    shared.load_self(sp, s, 0, 0)
                k2, p2 = back(k, par, 3)
                if live(k2, p2, NCH):
                    n2 = 2 * k2 + p2
                    sp.wait_ge(hi_done, NQK * (n2 + 1))
                    sp.wait_ge(lo_done, NQK * (n2 + 1))
                    for i in range(NQK):
                        which, c = i // DC, i % DC
                        for part, src in enumerate((hi, lo)):
                            dst = s["qk"][which, part].rearrange("(b c g) q r t -> b c q g r t", b=B, c=DC)
                            sp.dma_start(dst[k2, c, p2], words(src[p2][:, i, :]))\
                                .then_inc(stored[p2], 16)
                    sp.wait_ge(vaug_done, 2 * (n2 + 1))
                    for g in range(NG):
                        dst = s["v"].rearrange("(b g) p t e -> b g p t e", b=B)[k2, g, :, p2 * TPC:(p2 + 1) * TPC, :]
                        sp.dma_start(dst, vaug[p2][:, :, g * HG:(g + 1) * HG, :].rearrange("p t h e -> p t (h e)"))\
                            .then_inc(stored[p2], 16)

            steps(sp, step, NCH + 3, 4, NCH)

        @block.gpsimd
        def _(pool):
            for i in range(2):
                pool.memset(vaug[i][:, :, :, HD:VW], 1.0).then_inc(ones, 1)
            pool.wait_ge(ones, 2)
            for g in range(NG):
                need(pool, zero, 3 * g)
                pool.memset(words(shared.ck[g][:, :, :]), 0.0).then_inc(zero, 1)
                pool.wait_ge(zero, 3 * g + 1)
                pool.memset(words(shared.ck[g][ROW_MAX:ROWS, :, :]), 1.0).then_inc(zero, 1)
                pool.wait_ge(zero, 3 * g + 2)
                pool.memset(shared.cv[g][:, :, :], 0.0).then_inc(zero, 1)
            pool.wait_ge(zero, 3 * NG)

            def step(k, par):
                n = 2 * k + par
                if live(k, par, NCH):
                    pool.wait_ge(stats_done, n + 1)
                    need(pool, xhat_done, n)
                    rstd_of(pool, moments, rstd, half, pool_own, n + 1).then_inc(rstd_done, 1)
                k2, p2 = back(k, par, 2)
                if live(k2, p2, NCH):
                    n2 = 2 * k2 + p2
                    need(pool, stored[p2], 16 * QKV_STORES * k2)
                    for i in range(NQK):
                        pool.wait_ge(hi_done, NQK * n2 + i + 1)
                        pool.tensor_tensor(lo[p2][:, i, :], full[p2][:, i, :], hi[p2][:, i, :].bitcast(F32),
                                           ALU.subtract).then_inc(lo_done, 1)

            steps(pool, step, NCH + 2, 4, NCH)

        @block.vector
        def _(dve):
            dve.wait_ge(ones, 2)

            def step(k, par):
                n = 2 * k + par
                if live(k, par, NCH):
                    dve.wait_ge(x_in[par], 16 * (k + 1))
                    norm_stats(dve, x[par], stats, moments, own, n + 1).then_inc(stats_done, 1)
                    dve.wait_ge(rstd_done, n + 1)
                    need(dve, turned_done, DC * (n - 1))
                    normalize(dve, xhat[par], x[par], moments, rstd).then_inc(xhat_done, 1)
                k2, p2 = back(k, par, 2)
                if live(k2, p2, NCH):
                    n2 = 2 * k2 + p2
                    need(dve, lo_done, NQK * (n2 - 1))
                    for i in range(NQK):
                        dve.wait_ge(qk_done, NQK * n2 + i + 1)
                        dve.tensor_scalar(full[p2][:, i, :], qk_ps[i][:, :], col[:, 6 + i // DC * 2, i % DC:i % DC + 1],
                                          None, ALU.add).then_inc(full_done, 1)
                    need(dve, stored[p2], 16 * QKV_STORES * k2)
                    for i in range(TPC // 2):
                        dve.wait_ge(v_done, 2 * n2 + i + 1)
                        dve.tensor_copy(vaug[p2][:, 2 * i:2 * i + 2, :, 0:HD],
                                        v_ps[i].rearrange("p (t h e) -> p t h e", t=2, h=H)).then_inc(vaug_done, 1)

            steps(dve, step, NCH + 2, 4, NCH)

        @block.scalar
        def _(act):
            def step(k, par):
                n = 2 * k + par
                if live(k, par, NCH):
                    for c in range(DC):
                        act.wait_ge(turned_done, DC * n + c + 1)
                        if c == 0:
                            need(act, v_done, 2 * (n - 1))
                        act.activation(hT[par][:, c, :], turned[c][:, :], ACT.Identity, scale=col[:, 0, c:c + 1],
                                       bias=col[:, 1, c:c + 1]).then_inc(hT_done, 1)
                k1, p1 = back(k, par, 1)
                if live(k1, p1, NCH):
                    n1 = 2 * k1 + p1
                    need(act, stored[p1], 16 * QKV_STORES * k1)
                    for i in range(NQK):
                        act.wait_ge(full_done, NQK * n1 + i + 1)
                        act.activation(hi[p1][:, i, :], full[p1][:, i, :], ACT.Copy).then_inc(hi_done, 1)

            steps(act, step, NCH + 1, 4, NCH)

        @block.tensor
        def _(pe):
            def step(k, par):
                n = 2 * k + par
                if live(k, par, NCH):
                    pe.wait_ge(xhat_done, n + 1)
                    need(pe, hT_done, DC * n)
                    turn(pe, turned, xhat[par], ident, turned_done)
                k1, p1 = back(k, par, 1)
                if live(k1, p1, NCH):
                    n1 = 2 * k1 + p1
                    pe.wait_ge(hT_done, DC * (n1 + 1))
                    for i in range(NQK):
                        w, mc = W["sa_wq" if i < DC else "sa_wk"], i % DC
                        need(pe, full_done, NQK * (n1 - 1) + i + 1)
                        for c in range(DC):
                            last = pe.matmul(qk_ps[i][:, :], w[:, c, mc * P:(mc + 1) * P], hT[p1][:, c, :],
                                             start=(c == 0), stop=(c == DC - 1))
                        last.then_inc(qk_done, 1)
                    for t in range(TPC):
                        if t % 2 == 0:
                            need(pe, vaug_done, 2 * (n1 - 1) + t // 2 + 1)
                        for c in range(DC):
                            last = pe.matmul(v_ps[t // 2][:, (t % 2) * D:(t % 2 + 1) * D],
                                             hT[p1][:, c, t * P:(t + 1) * P], W["sa_wv"][:, c, :],
                                             start=(c == 0), stop=(c == DC - 1))
                        if t % 2:
                            last.then_inc(v_done, 1)

            steps(pe, step, NCH + 1, 4, NCH)


def stack_rows(sp, dram, n, which, dst, sem, chunks=range(CPB)):
    for block in range(4):
        lo = block // 2 if which == 0 else block % 2
        for c in chunks:
            src = dram[lo].rearrange("n c (h e) t -> n c e h t", h=HG)[n, c]
            sp.dma_start(words(dst[block * HD:(block + 1) * HD, c, :, :]), src).then_inc(sem, 16)


def split_max(dve, maxima, rows, own, count):
    dve.tensor_scalar(rows[:, 0, :], maxima[:, :], -1.0, None, ALU.mult).then_inc(own, 1)
    dve.wait_ge(own, count)
    return dve.scalar_tensor_tensor(rows[:, 1, :], maxima[:, :], -1.0, rows[:, 0, :].bitcast(F32),
                                    ALU.mult, ALU.subtract)


class Slots:

    def __init__(self):
        tiles = HG * TPC
        self.order = [("max", 0, j) for j in range(tiles)] + [("maxT", 0, 0)] + [("max", 1, j) for j in range(2 * LEAD)]
        for u in range(NU):
            for st in range(KT):
                self.order += [("max", *self.tile(u, st, 0))]
                if st == OUT_STEP:
                    self.order += [("out", u - 1, 0)]
                if st == MAXT_STEP:
                    self.order += [("maxT", u + 1, 0)]
                self.order += [("max", *self.tile(u, st, 1))]
        self.order = [i for i in self.order + [("out", NU - 1, 0)] if 0 <= i[1] < NU]
        self.number = {item: n for n, item in enumerate(self.order)}
        self.per_unit = self.number["max", 5, 0] - self.number["max", 4, 0]

    @staticmethod
    def tile(u, st, i):
        j = 2 * (st + LEAD) + i
        return (u + 1, j) if j < HG * TPC else (u + 2, j - HG * TPC)

    def at(self, kind, u, j):
        if isinstance(u, int):
            return self.number[kind, u, j], self.number[kind, u, j] % 2
        base = self.number[kind, 4, j] - 4 * self.per_unit
        return base + self.per_unit * u, base % 2


def self_attention(nc, a, W, s, shared):
    ident = W["ident"]
    NMAX = HG * TPC
    NEXP = HG * KT
    NB, EXP_SHIFT = 3, HG * (KT // 2) + 2
    exp_bank = [(i + (i >= EXP_SHIFT)) % NB for i in range(NEXP)]
    with ExitStack() as stack:
        m = Arena(nc, stack, "sa")
        q, kk, v = shared.rows[0:2], shared.rows[2:4], shared.v
        maxima = [m.sb(f"maxima{i}", [P, NMAX]) for i in range(2)]
        maxrows, maxT = m.sb("maxrows", [P, 2, NMAX], F32R), m.sb("maxT", [2 * NMAX, P], F32R)
        zeros, minus = m.sb("zeros", [P, NMAX]), m.sb("minus", [P, NMAX])
        o_sb = m.sb("o_sb", [P, CH])
        inv = m.sb("inv", [P, TPC, HG])
        o_out = [m.sb(f"o_out{i}", [P, TPC, HG, HD]) for i in range(2)]
        NP_ = 4
        probs = [m.sb(f"probs{i}", [P, HG, CH]) for i in range(NP_)]
        slot = [m.ps(f"slot{i}", [P, T]) for i in range(2)]
        s_exp = [m.ps(f"s_exp{i}", [P, CH]) for i in range(NB)]
        o_ps = m.ps("o", [P, CH])
        slots = Slots()
        rows_in, out_done = shared.self_in, m.sems("out_done", 2)
        zero, max_in, filled, emptied, negated, own, s_done, exp_done, pv_done, o_done, inv_done, w_in = (
            m.sem(n) for n in ("zero", "max_in", "filled", "emptied", "negated", "own", "s_done", "exp_done",
                               "pv_done", "o_done", "inv_done", "w_in"))
        block = stack.enter_context(nc.Block())

        @block.sync
        def _(sp):
            def max_rows(u, par, qc):
                sp.wait_ge(emptied, slots.at("maxT", u, 0)[0] + 1)
                rows = words(q[par][ROW_MAX:ROWS, qc, :, :]).rearrange("r h (t p) -> r (h t) p", t=TPC)
                sp.dma_start(rows, words(maxT[:, :])).then_inc(max_in, 16)

            max_rows(0, 0, 0)
            for par in range(2):
                sp.wait_ge(shared.qkv_stored[par], 16 * QKV_STORES * NCH // 2)

            def step(k, par):
                n = 2 * k + par
                if live(k, par, BG - 1):
                    need(sp, pv_done, 2 * KT * n)
                    shared.load_self(sp, s, n + 1, 1 - par)
                for qc in range(CPB):
                    u = CPB * n + qc
                    if live(k, par, BG - 1) or qc == 0:
                        max_rows(u + 1, par if qc == 0 else 1 - par, 1 - qc)
                    if not (isinstance(k, int) and k == 0 and par == 0 and qc == 0):
                        store(back(k, par, 1) if qc == 0 else (k, par), 1 - qc)
                    if isinstance(n, int) and n == BG - 2:
                        sp.wait_ge(out_done[qc], 16 * NG)
                        shared.load_residual(sp, s, chunk_view(a["x"]), 0, 0, qc)

            def store(which, qc):
                n = 2 * which[0] + which[1]
                sp.wait_ge(emptied, slots.at("out", CPB * n + qc, 0)[0] + 1)
                sp.dma_start(s["attn"][n, qc].rearrange("t p e -> p t e"),
                             o_out[qc].rearrange("p t h e -> p t (h e)")).then_inc(out_done[qc], 16)

            steps(sp, step, BG, 2, BG - 2)
            store((BG // 2 - 1, 1), 1)
            for qc in range(CPB):
                sp.wait_ge(out_done[qc], 16 * BG)
            sp.wait_ge(w_in, 32)

        @block.gpsimd
        def _(pool):
            pool.memset(zeros[:, :], 0.0).then_inc(zero, 1)
            pool.wait_ge(zero, 1)
            def negate(u, qc):
                pool.wait_ge(emptied, slots.at("max", u, NMAX - 1)[0] + 1)
                if not isinstance(u, int) or u > 0:
                    pool.wait_ge(filled, slots.at("maxT", u - 1, 0)[0] + 1)
                pool.tensor_tensor(minus[:, :], zeros[:, :], maxima[qc][:, :], ALU.subtract).then_inc(own, 1)
                pool.wait_ge(own, 2 * u + 1)
                pool.tensor_tensor(maxrows[:, 0, :], minus[:, :], zeros[:, :], ALU.subtract).then_inc(own, 1)
                pool.wait_ge(own, 2 * u + 2)
                pool.tensor_tensor(maxrows[:, 1, :], minus[:, :], maxrows[:, 0, :].bitcast(F32), ALU.subtract)\
                    .then_inc(negated, 1)

            negate(0, 0)
            for name in ("w1", "w2"):
                pool.dma_start(W[name][:, :, :], chunked(a[name])).then_inc(w_in, 16)

            def step(k, par):
                for qc in range(CPB):
                    if isinstance(k, int) and k == 0:
                        shared.load_cross_kv(pool, s, 0, CPB * par + qc)
                    if live(k, par, BG - 1) or qc == 0:
                        negate(CPB * (2 * k + par) + qc + 1, 1 - qc)

            steps(pool, step, BG, 2, BG - 2)

        @block.tensor
        def _(pe):
            def take(kind, u, j):
                number, which = slots.at(kind, u, j)
                need(pe, emptied, number - 1)
                return slot[which]

            def score_max(u, par, qc, j):
                h, t = j // TPC, j % TPC
                dst = take("max", u, j)
                tile = q[par][0:ROWS_SCORE, qc, h, t * P:(t + 1) * P]
                for c in range(CPB):
                    last = pe.matmul(dst[:, c * CH:(c + 1) * CH], tile, kk[par][0:ROWS_SCORE, c, h, :],
                                     start=True, stop=True)
                last.then_inc(filled, 1)

            def turn_max(u):
                pe.wait_ge(negated, u + 1)
                pe.transpose(take("maxT", u, 0)[0:2 * NMAX, 0:P],
                             maxrows[:, :, :].bitcast(F32).rearrange("p r j -> p (r j)"), ident[:, :])\
                    .then_inc(filled, 1)

            def turn_out(u):
                pe.wait_ge(o_done, u + 1)
                dst = take("out", u, 0)
                for t in range(TPC):
                    last = pe.transpose(dst[:, t * P:(t + 1) * P], o_sb[:, t * P:(t + 1) * P], ident[:, :])
                last.then_inc(filled, 1)

            def values(u, par, st):
                if st == 0:
                    need(pe, o_done, u)
                pe.wait_ge(exp_done, HG * (KT * u + st + 1))
                for h in range(HG):
                    last = pe.matmul(o_ps[h * VW:(h + 1) * VW, :], v[par][:, st, h, :], probs[st % NP_][:, h, :],
                                     start=(st == 0), stop=(st == KT - 1), tile_position=(0, h * VW))
                last.then_inc(pv_done, 1)

            def prologue():
                pe.wait_ge(rows_in[0], SELF_LOADS)
                for j in range(NMAX):
                    score_max(0, 0, 0, j)
                turn_max(0)
                for j in range(2 * LEAD):
                    score_max(1, 0, 1, j)

            prologue()

            def step(k, par):
                n = 2 * k + par
                more = live(k, par, BG - 1)
                k1, p1 = back(k, par, -1)
                for qc in range(CPB):
                    u = CPB * n + qc
                    next_par, next_qc = (par, 1) if qc == 0 else (1 - par, 0)
                    pe.wait_ge(max_in, 16 * (u + 1))
                    for st in range(KT):
                        for h in range(HG):
                            i = HG * st + h
                            need(pe, exp_done, NEXP * u + i + 1 - reuse(i, exp_bank))
                            pe.matmul(s_exp[exp_bank[i]][:, :], kk[par][:, st // TPC, h, st % TPC * P:(st % TPC + 1) * P],
                                      q[par][:, qc, h, :], start=True, stop=True).then_inc(s_done, 1)
                            if h in (0, 3):
                                j = 2 * (st + LEAD) + h // 3
                                if j < NMAX:
                                    if more or qc == 0:
                                        score_max(u + 1, next_par, next_qc, j)
                                elif more:
                                    if qc == 0 and j == NMAX:
                                        pe.wait_ge(rows_in[1 - par], SELF_LOADS * (k1 + 1))
                                    score_max(u + 2, 1 - par, qc, j - NMAX)
                            if h == 1:
                                if st > 0:
                                    values(u, par, st - 1)
                                elif not (isinstance(u, int) and u == 0):
                                    values(u - 1, par if qc else 1 - par, KT - 1)
                                if st == MAXT_STEP and (more or qc == 0):
                                    turn_max(u + 1)
                                if st == OUT_STEP and not (isinstance(u, int) and u == 0):
                                    turn_out(u - 1)

            steps(pe, step, BG, 2, BG - 2)
            values(NU - 1, 1, KT - 1)
            turn_out(NU - 1)

        @block.scalar
        def _(act):
            for par in range(2):
                act.wait_ge(shared.qkv_stored[par], 16 * QKV_STORES * NCH // 2)

            def step(k, par):
                n = 2 * k + par
                for qc in range(CPB):
                    u = CPB * n + qc
                    for st in range(KT):
                        need(act, pv_done, KT * u + st - NP_ + 1)
                        for h in range(HG):
                            act.wait_ge(s_done, HG * (KT * u + st) + h + 1)
                            act.activation(probs[st % NP_][:, h, :], s_exp[exp_bank[HG * st + h]][:, :], ACT.Exp, scale=SCALE)\
                                .then_inc(exp_done, 1)

            steps(act, step, BG, 2, BG - 2)

        @block.vector
        def _(dve):
            def item(kind, u, j):
                number, which = slots.at(kind, u, j)
                dve.wait_ge(filled, number + 1)
                return slot[which]

            def reduce(u, qc, j):
                dve.tensor_reduce(maxima[qc][:, j:j + 1], item("max", u, j)[:, :], AX_X, ALU.max).then_inc(emptied, 1)

            def take_max(u):
                need(dve, max_in, 16 * u)
                dve.tensor_copy(maxT[:, :], item("maxT", u, 0)[0:2 * NMAX, 0:P]).then_inc(emptied, 1)

            def take_out(u):
                dve.wait_ge(pv_done, KT * (u + 1))
                if not isinstance(u, int) or u > 0:
                    dve.wait_ge(filled, slots.at("out", u - 1, 0)[0] + 1)
                dve.tensor_copy(o_sb[:, :], o_ps[:, :]).then_inc(o_done, 1)

            def scale_out(u, qc, k_):
                if not isinstance(u, int) or u > 0:
                    dve.wait_ge(emptied, slots.at("out", u - 1, 0)[0] + 1)
                sums = item("out", u, 0)[:, 0:CH].rearrange("p (t h e) -> p t h e", t=TPC, h=HG)
                dve.reciprocal(inv[:, :, :], sums[:, :, :, HD]).then_inc(inv_done, 1)
                dve.wait_ge(inv_done, u + 1)
                need(dve, out_done[qc], 16 * k_)
                dve.tensor_tensor(o_out[qc][:, :, :, :], sums[:, :, :, 0:HD],
                                  inv.rearrange("p t (h e) -> p t h e", e=1).to_broadcast([P, TPC, HG, HD]),
                                  ALU.mult).then_inc(emptied, 1)

            for j in range(NMAX):
                reduce(0, 0, j)
            take_max(0)
            for j in range(2 * LEAD):
                reduce(1, 1, j)

            def step(k, par):
                n = 2 * k + par
                more = live(k, par, BG - 1)
                for qc in range(CPB):
                    u = CPB * n + qc
                    for st in range(KT):
                        for i in range(2):
                            j = 2 * (st + LEAD) + i
                            if j < NMAX:
                                if more or qc == 0:
                                    reduce(u + 1, 1 - qc, j)
                            elif more:
                                reduce(u + 2, qc, j - NMAX)
                            if i == 0 and st == 0 and not (isinstance(u, int) and u == 0):
                                take_out(u - 1)
                            if i == 0 and st == OUT_STEP and not (isinstance(u, int) and u == 0):
                                scale_out(u - 1, 1 - qc, (u - 1) // 2 if isinstance(u, int) else n - (1 - qc))
                            if i == 0 and st == MAXT_STEP and (more or qc == 0):
                                take_max(u + 1)

            steps(dve, step, BG, 2, BG - 2)
            take_out(NU - 1)
            scale_out(NU - 1, 1, BG - 1)


class Residual:

    def __init__(self, m, W, s, shared, x_dram, wo, row, gain):
        self.W, self.s, self.shared, self.x_dram, self.wo, self.row, self.gain = W, s, shared, x_dram, wo, row, gain
        self.att, self.x, self.badd, self.loaded = shared.att, shared.x, shared.badd, shared.residual_in[row]
        self.attT = m.sb("attT", [P, DC, CH])
        self.y = [m.sb(f"y{i}", [P, TPC, D]) for i in range(2)]
        self.stats, self.moments, self.rstd = m.sb("stats", [P, TPC + 1, 6]), m.sb("moments", [P, TPC, 2]), m.sb("rstd", [P, TPC])
        self.xhat = m.sb("xhat", [P, TPC, D])
        self.hT = [m.sb(f"hT{i}", [P, DC, CH]) for i in range(2)]
        self.turned = [m.ps(f"turned{c}", [P, CH]) for c in range(DC)]
        self.wo_ps = [m.ps(f"wo{i}", [P, 2 * D]) for i in range(TPC // 2)]
        (self.own, self.pool_own, self.attT_ps, self.attT_sb, self.wo_done, self.xb_done, self.y_done, self.stats_done,
         self.rstd_done, self.xhat_done, self.hT_ps, self.hT_sb) = (
            m.sem(n) for n in ("own", "pool_own", "attT_ps", "attT_sb", "wo_done", "xb_done", "y_done", "stats_done",
                               "rstd_done", "xhat_done", "hT_ps", "hT_sb"))

    def load(self, sp, k, par):
        n = 2 * k + par
        if isinstance(n, int) and n < 2:
            return
        sp.wait_ge(self.attT_ps, DC * (n - 1))
        sp.wait_ge(self.y_done, n - 1)
        self.shared.load_residual(sp, self.s, self.x_dram, self.row, k, par)

    def pool_add(self, pool, k, par):
        pool.wait_ge(self.loaded[par], RESIDUAL_LOADS * (k + 1))
        pool.tensor_tensor(self.x[par][:, :, :], self.x[par][:, :, :],
                           self.badd[par].rearrange("p (t d) -> p t d", t=1).to_broadcast([P, TPC, D]), ALU.add)\
            .then_inc(self.xb_done, 1)

    def pool_rstd(self, pool, k, par):
        n = 2 * k + par
        pool.wait_ge(self.stats_done, n + 1)
        need(pool, self.xhat_done, n)
        rstd_of(pool, self.moments, self.rstd, self.W["half"], self.pool_own, n + 1).then_inc(self.rstd_done, 1)

    def turn_att(self, pe, k, par):
        n = 2 * k + par
        pe.wait_ge(self.loaded[par], RESIDUAL_LOADS * (k + 1))
        need(pe, self.hT_sb, DC * (n - 1))
        turn(pe, self.turned, self.att[par], self.W["ident"], self.attT_ps)

    def turn_h(self, pe, k, par):
        n = 2 * k + par
        pe.wait_ge(self.xhat_done, n + 1)
        pe.wait_ge(self.attT_sb, DC * (n + 2) if not isinstance(k, int) else DC * min(n + 2, NCH))
        turn(pe, self.turned, self.xhat, self.W["ident"], self.hT_ps)

    def project(self, pe, k, par):
        n = 2 * k + par
        pe.wait_ge(self.attT_sb, DC * (n + 1))
        for t in range(TPC):
            if t % 2 == 0:
                need(pe, self.y_done, n)
            for c in range(DC):
                last = pe.matmul(self.wo_ps[t // 2][:, (t % 2) * D:(t % 2 + 1) * D],
                                 self.attT[:, c, t * P:(t + 1) * P], self.wo[:, c, :],
                                 start=(c == 0), stop=(c == DC - 1))
            if t % 2:
                last.then_inc(self.wo_done, 1)

    def take_att(self, act, k, par):
        n = 2 * k + par
        for c in range(DC):
            act.wait_ge(self.attT_ps, DC * n + c + 1)
            if c == 0:
                need(act, self.wo_done, 2 * n)
            act.activation(self.attT[:, c, :], self.turned[c][:, :], ACT.Copy).then_inc(self.attT_sb, 1)

    def take_h(self, act, k, par, used, count):
        n = 2 * k + par
        need(act, used, count)
        for c in range(DC):
            act.wait_ge(self.hT_ps, DC * n + c + 1)
            act.activation(self.hT[par][:, c, :], self.turned[c][:, :], ACT.Identity,
                           scale=self.W["col"][:, self.gain, c:c + 1],
                           bias=self.W["col"][:, self.gain + 1, c:c + 1]).then_inc(self.hT_sb, 1)

    def add_norm(self, dve, k, par, free):
        n = 2 * k + par
        dve.wait_ge(self.xb_done, n + 1)
        free(k, par)
        for i in range(TPC // 2):
            dve.wait_ge(self.wo_done, 2 * n + i + 1)
            last = dve.tensor_tensor(self.y[par][:, 2 * i:2 * i + 2, :],
                                     self.wo_ps[i].rearrange("p (t d) -> p t d", t=2),
                                     self.x[par][:, 2 * i:2 * i + 2, :], ALU.add)
        last.then_inc(self.y_done, 1)
        dve.wait_ge(self.y_done, n + 1)
        norm_stats(dve, self.y[par], self.stats, self.moments, self.own, n + 1).then_inc(self.stats_done, 1)
        dve.wait_ge(self.rstd_done, n + 1)
        need(dve, self.hT_ps, DC * n)
        normalize(dve, self.xhat, self.y[par], self.moments, self.rstd).then_inc(self.xhat_done, 1)


def chunk_view(x):
    return x.rearrange("b (c t p) d -> (b c) p t d", c=CPB, t=TPC)


def cross_q(nc, a, W, s, shared):
    col = W["col"]
    with ExitStack() as stack:
        m = Arena(nc, stack, "cq")
        r = Residual(m, W, s, shared, chunk_view(a["x"]), W["sa_wo"], 0, 2)
        full = [m.sb(f"full{i}", [P, DC, CH]) for i in range(2)]
        hi = [m.sb(f"hi{i}", [P, DC, CH], F32R) for i in range(2)]
        lo = [m.sb(f"lo{i}", [P, DC, CH], F32R) for i in range(2)]
        q_ps = [m.ps(f"q{i}", [P, CH]) for i in range(DC)]
        stored, q_done, hi_done, full_done, lo_done = (
            shared.cq_stored, m.sem("q_done"), m.sem("hi_done"), m.sem("full_done"), m.sem("lo_done"))
        y_stored, mask_rows = m.sems("y_stored", 2), m.sem("mask_rows")
        block = stack.enter_context(nc.Block())

        @block.sync
        def _(sp):
            def step(k, par):
                n = 2 * k + par
                if live(k, par, NCH):
                    r.load(sp, k, par)
                k1, p1 = back(k, par, 1)
                if live(k1, p1, NCH):
                    n1 = 2 * k1 + p1
                    sp.wait_ge(r.y_done, n1 + 1)
                    sp.dma_start(s["x1"][n1], r.y[p1][:, :, :]).then_inc(y_stored[p1], 16)
                if isinstance(k, int) and n == NCH + 1:
                    for first in range(2):
                        sp.wait_ge(stored[first], CQ_STORES)
                    for qc in range(CPB):
                        shared.load_cross_q(sp, s, 0, 0, qc)
                k2, p2 = back(k, par, 3)
                if live(k2, p2, NCH):
                    n2 = 2 * k2 + p2
                    sp.wait_ge(hi_done, DC * (n2 + 1))
                    sp.wait_ge(lo_done, DC * (n2 + 1))
                    for c in range(DC):
                        for part, src in enumerate((hi, lo)):
                            dst = s["cq"][part].rearrange("(b c g) q r t -> b c q g r t", b=B, c=DC)
                            sp.dma_start(dst[k2, c, p2], words(src[p2][:, c, :]))\
                                .then_inc(stored[p2], 16)

            steps(sp, step, NCH + 3, 4, NCH)
            for par in range(2):
                sp.wait_ge(y_stored[par], 16 * NCH // 2)

        @block.gpsimd
        def _(pool):
            for i in range(2):
                need(pool, mask_rows, i)
                pool.memset(words(shared.rows[2 + i][ROW_MASK:ROW_MASK + 1, :, :, :]), 1.0).then_inc(mask_rows, 1)
            pool.wait_ge(mask_rows, 2)

            def step(k, par):
                if live(k, par, NCH):
                    r.pool_add(pool, k, par)
                k2, p2 = back(k, par, 2)
                if live(k2, p2, NCH):
                    n2 = 2 * k2 + p2
                    need(pool, stored[p2], CQ_STORES * k2)
                    for i in range(DC):
                        pool.wait_ge(hi_done, DC * n2 + i + 1)
                        pool.tensor_tensor(lo[p2][:, i, :], full[p2][:, i, :], hi[p2][:, i, :].bitcast(F32),
                                           ALU.subtract).then_inc(lo_done, 1)
                if live(k, par, NCH):
                    r.pool_rstd(pool, k, par)

            steps(pool, step, NCH + 2, 4, NCH)

        @block.tensor
        def _(pe):
            def step(k, par):
                if live(k, par, NCH):
                    r.turn_att(pe, k, par)
                k2, p2 = back(k, par, 2)
                if live(k2, p2, NCH):
                    n2 = 2 * k2 + p2
                    pe.wait_ge(r.hT_sb, DC * (n2 + 1))
                    for i in range(DC):
                        need(pe, full_done, DC * (n2 - 1) + i + 1)
                        for c in range(DC):
                            last = pe.matmul(q_ps[i][:, :], W["ca_wq"][:, c, i * P:(i + 1) * P], r.hT[p2][:, c, :],
                                             start=(c == 0), stop=(c == DC - 1))
                        last.then_inc(q_done, 1)
                if live(k, par, NCH):
                    r.project(pe, k, par)
                k1, p1 = back(k, par, 1)
                if live(k1, p1, NCH):
                    r.turn_h(pe, k1, p1)

            steps(pe, step, NCH + 2, 4, NCH)

        @block.scalar
        def _(act):
            def step(k, par):
                if live(k, par, NCH):
                    r.take_att(act, k, par)
                k2, p2 = back(k, par, 2)
                if live(k2, p2, NCH):
                    n2 = 2 * k2 + p2
                    need(act, stored[p2], CQ_STORES * k2)
                    for i in range(DC):
                        act.wait_ge(full_done, DC * n2 + i + 1)
                        act.activation(hi[p2][:, i, :], full[p2][:, i, :], ACT.Copy).then_inc(hi_done, 1)
                k1, p1 = back(k, par, 1)
                if live(k1, p1, NCH):
                    r.take_h(act, k1, p1, q_done, DC * (2 * k1 + p1 - 1))

            steps(act, step, NCH + 2, 4, NCH)

        @block.vector
        def _(dve):
            def free(k, par):
                need(dve, y_stored[par], 16 * k)

            def step(k, par):
                k2, p2 = back(k, par, 2)
                if live(k2, p2, NCH):
                    n2 = 2 * k2 + p2
                    need(dve, lo_done, DC * (n2 - 1))
                    for i in range(DC):
                        dve.wait_ge(q_done, DC * n2 + i + 1)
                        dve.tensor_scalar(full[p2][:, i, :], q_ps[i][:, :], col[:, 9, i:i + 1], None,
                                          ALU.add).then_inc(full_done, 1)
                if live(k, par, NCH):
                    r.add_norm(dve, k, par, free)

            steps(dve, step, NCH + 2, 4, NCH)


def cross_attention(nc, a, W, s, shared):
    ident = W["ident"]
    UB = NG * CPB
    with ExitStack() as stack:
        m = Arena(nc, stack, "ca")
        q, kk, v, mask = shared.rows, shared.ck, shared.cv, shared.mask
        maxima = [m.sb(f"maxima{i}", [P, HG, TPC]) for i in range(2)]
        maxrows, maxT = m.sb("maxrows", [P, 2, HG * TPC], F32R), m.sb("maxT", [2 * HG * TPC, P], F32R)
        o_sb = m.sb("o_sb", [P, CH])
        inv = m.sb("inv", [P, TPC, HG])
        o_out = [m.sb(f"o_out{i}", [P, TPC, HG, HD]) for i in range(2)]
        probs = [m.sb(f"probs{i}", [P, HG, CH]) for i in range(2)]
        s_max = [m.ps(f"s_max{i}", [P, TPC, P]) for i in range(2)]
        s_exp = [m.ps(f"s_exp{i}", [P, CH]) for i in range(2)]
        o_ps = [m.ps(f"o{i}", [P, CH]) for i in range(2)]
        mT, oT = m.ps("mT", [P, CH]), m.ps("oT", [P, CH])
        rows_in, context_in, out_done = shared.cross_in, shared.context_in, m.sems("out_done", 2)
        zero, max_in, scored, reduced, negated, own, maxT_done, maxT_sb = (
            m.sem(n) for n in ("zero", "max_in", "scored", "reduced", "negated", "own", "maxT_done", "maxT_sb"))
        s_done, exp_done, pv_done, o_done, oT_done, inv_done, out_ready = (
            m.sem(n) for n in ("s_done", "exp_done", "pv_done", "o_done", "oT_done", "inv_done", "out_ready"))
        block = stack.enter_context(nc.Block())

        def batches(eng, step):
            step(0)
            with eng.Fori(1, B - 1) as b:
                step(b)
            step(B - 1)

        def there(b, unit):
            return not isinstance(b, int) or 0 <= b * UB + unit < NU

        @block.sync
        def _(sp):
            def max_rows(b, unit):
                g, qc = unit // CPB % NG, unit % CPB
                sp.wait_ge(maxT_sb, UB * b + unit + 1)
                rows = words(q[g][ROW_MAX:ROWS, qc, :, :]).rearrange("r h (t p) -> r (h t) p", t=TPC)
                sp.dma_start(rows, words(maxT[:, :])).then_inc(max_in, 16)

            def store(b, unit):
                g, qc = unit // CPB % NG, unit % CPB
                sp.wait_ge(out_ready, UB * b + unit + 1)
                dst = s["attn"][NG * b + unit // CPB, qc]
                sp.dma_start(dst.rearrange("t p e -> p t e"), o_out[qc].rearrange("p t h e -> p t (h e)"))\
                    .then_inc(out_done[qc], 16)

            for qc in range(CPB):
                shared.load_cross_q(sp, s, 0, 1, qc)
            max_rows(0, 0)
            for par in range(2):
                sp.wait_ge(shared.cq_stored[par], CQ_STORES * NCH // 2)

            def step(b):
                for unit in range(UB):
                    qc = unit % CPB
                    if there(b, unit + 1):
                        max_rows(b, unit + 1)
                    if there(b, unit + 2 * CPB):
                        g = unit // CPB + 2
                        need(sp, pv_done, UB * b + unit - 2 * CPB + 1)
                        shared.load_cross_q(sp, s, b + g // NG, g % NG, qc)
                    if there(b, unit - 1):
                        store(b, unit - 1)
                    if isinstance(b, int) and b == B - 1 and unit // CPB == 2:
                        sp.wait_ge(out_done[qc], 16 * NG)
                        shared.load_residual(sp, s, s["x1"], 1, 0, qc)

            batches(sp, step)
            store(B - 1, UB - 1)
            for qc in range(CPB):
                sp.wait_ge(out_done[qc], 16 * BG)

        @block.gpsimd
        def _(pool):
            for i in range(2):
                need(pool, zero, i)
                pool.memset(probs[i][:, :, :], 0.0).then_inc(zero, 1)

            def step(b):
                if there(b, UB):
                    for g in range(NG):
                        pool.wait_ge(pv_done, UB * b + CPB * (g + 1))
                        shared.load_cross_kv(pool, s, b + 1, g)

            batches(pool, step)

        @block.tensor
        def _(pe):
            def score_max(b, unit, h):
                g, qc = unit // CPB % NG, unit % CPB
                need(pe, reduced, HG * (UB * b + unit) + h - 1)
                for t in range(TPC):
                    last = pe.matmul(s_max[h % 2][:, t, 0:NKE],
                                     q[g][0:ROWS_SCORE, qc, h, t * P:(t + 1) * P],
                                     kk[g][0:ROWS_SCORE, h, :], start=True, stop=True)
                last.then_inc(scored, 1)

            def turn_max(b, unit):
                pe.wait_ge(negated, UB * b + unit + 1)
                need(pe, maxT_sb, UB * b + unit)
                pe.transpose(mT[0:2 * HG * TPC, 0:P], maxrows[:, :, :].bitcast(F32).rearrange("p r j -> p (r j)"),
                             ident[:, :]).then_inc(maxT_done, 1)

            def values(b, unit):
                g, qc = unit // CPB % NG, unit % CPB
                u = UB * b + unit
                need(pe, o_done, u - 1)
                pe.wait_ge(exp_done, HG * (u + 1))
                for h in range(HG):
                    last = pe.matmul(o_ps[qc][h * VW:(h + 1) * VW, :], v[g][:, h, :], probs[qc][:, h, :],
                                     start=True, stop=True, tile_position=(0, h * VW))
                last.then_inc(pv_done, 1)

            def turn_out(b, unit):
                u = UB * b + unit
                pe.wait_ge(o_done, u + 1)
                need(pe, out_ready, u)
                for t in range(TPC):
                    last = pe.transpose(oT[:, t * P:(t + 1) * P], o_sb[:, t * P:(t + 1) * P], ident[:, :])
                last.then_inc(oT_done, 1)

            pe.wait_ge(context_in[0], CROSS_KV_LOADS)
            for unit in range(2):
                pe.wait_ge(rows_in[0][unit], CROSS_Q_LOADS)
                for h in range(HG):
                    score_max(0, unit, h)
                if unit == 0:
                    turn_max(0, 0)

            def step(b):
                for unit in range(UB):
                    u = UB * b + unit
                    g, qc = unit // CPB, unit % CPB
                    ahead = unit + 2
                    pe.wait_ge(max_in, 16 * (u + 1))
                    if there(b, ahead):
                        ga = ahead // CPB
                        pe.wait_ge(rows_in[ga % NG][qc], CROSS_Q_LOADS * (b + ga // NG + 1))
                        if qc == 0:
                            pe.wait_ge(context_in[ga % NG], CROSS_KV_LOADS * (b + ga // NG + 1))
                    for h in range(HG):
                        need(pe, exp_done, HG * u + h - 1)
                        pe.matmul(s_exp[h % 2][0:NK, :], kk[g][:, h, 0:NK], q[g][:, qc, h, :],
                                  start=True, stop=True).then_inc(s_done, 1)
                        if there(b, ahead):
                            score_max(b, ahead, h)
                        if h == 0 and there(b, unit - 1):
                            values(b, unit - 1)
                        if h == 1 and there(b, unit + 1):
                            turn_max(b, unit + 1)
                        if h == 2 and there(b, unit - 1):
                            turn_out(b, unit - 1)

            batches(pe, step)
            values(B - 1, UB - 1)
            turn_out(B - 1, UB - 1)

        @block.scalar
        def _(act):
            def take_max(b, unit):
                u = UB * b + unit
                act.wait_ge(maxT_done, u + 1)
                need(act, max_in, 16 * u)
                act.activation(maxT[:, :], mT[0:2 * HG * TPC, 0:P], ACT.Copy).then_inc(maxT_sb, 1)

            def take_out(b, unit):
                u = UB * b + unit
                act.wait_ge(pv_done, u + 1)
                need(act, oT_done, u)
                act.activation(o_sb[:, :], o_ps[unit % 2][:, :], ACT.Copy).then_inc(o_done, 1)

            take_max(0, 0)
            act.wait_ge(zero, 2)

            def step(b):
                for unit in range(UB):
                    u = UB * b + unit
                    g, qc = unit // CPB, unit % CPB
                    need(act, pv_done, u - 1)
                    if qc == 0:
                        act.wait_ge(context_in[g], CROSS_KV_LOADS * (b + 1))
                    for h in range(HG):
                        act.wait_ge(s_done, HG * u + h + 1)
                        act.activation(probs[qc][0:NK, h, :], s_exp[h % 2][0:NK, :], ACT.Exp, scale=SCALE,
                                       bias=mask[g][:, 0:1]).then_inc(exp_done, 1)
                        if h == 1 and there(b, unit - 1):
                            take_out(b, unit - 1)
                        if h == 1 and there(b, unit + 1):
                            take_max(b, unit + 1)

            batches(act, step)
            take_out(B - 1, UB - 1)

        @block.vector
        def _(dve):
            def reduce(b, unit, h):
                dve.wait_ge(scored, HG * (UB * b + unit) + h + 1)
                dve.tensor_reduce(maxima[unit % 2][:, h, :], s_max[h % 2][:, :, 0:NK], AX_X, ALU.max).then_inc(reduced, 1)

            def negate(b, unit):
                u = UB * b + unit
                dve.wait_ge(reduced, HG * (u + 1))
                need(dve, maxT_done, u)
                split_max(dve, maxima[unit % 2].rearrange("p h t -> p (h t)"), maxrows, own, u + 1).then_inc(negated, 1)

            def scale_out(b, unit):
                u = UB * b + unit
                dve.wait_ge(oT_done, u + 1)
                sums = oT.rearrange("p (t h e) -> p t h e", t=TPC, h=HG)
                dve.reciprocal(inv[:, :, :], sums[:, :, :, HD]).then_inc(inv_done, 1)
                dve.wait_ge(inv_done, u + 1)
                need(dve, out_done[unit % 2], 16 * (NG * b + unit // CPB))
                dve.tensor_tensor(o_out[unit % 2][:, :, :, :], sums[:, :, :, 0:HD],
                                  inv.rearrange("p t (h e) -> p t h e", e=1).to_broadcast([P, TPC, HG, HD]),
                                  ALU.mult).then_inc(out_ready, 1)

            for unit in range(2):
                for h in range(HG):
                    reduce(0, unit, h)
                negate(0, unit)

            def step(b):
                for unit in range(UB):
                    for h in range(HG):
                        if there(b, unit + 2):
                            reduce(b, unit + 2, h)
                        if h == 3 and there(b, unit - 1):
                            scale_out(b, unit - 1)
                    if there(b, unit + 2):
                        negate(b, unit + 2)

            batches(dve, step)
            scale_out(B - 1, UB - 1)


def mlp(nc, a, W, s, shared, out):
    with ExitStack() as stack:
        m = Arena(nc, stack, "mlp")
        r = Residual(m, W, s, shared, s["x1"], W["ca_wo"], 1, 4)
        row2 = [m.sb(f"row2_{i}", [P, D]) for i in range(2)]
        yb = [m.sb(f"yb{i}", [P, TPC, D]) for i in range(2)]
        hidden = [m.sb(f"hidden{i}", [P, FC, CH]) for i in range(2)]
        res = [m.sb(f"res{i}", [P, TPC, D]) for i in range(2)]
        w1_ps = [m.ps(f"w1_{i}", [P, CH]) for i in range(2)]
        w2_ps = [m.ps(f"w2_{i}", [P, 2 * D]) for i in range(2)]
        row_in, stored = m.sems("row_in", 2), m.sems("stored", 2)
        w1_done, hidden_done, w2_done, yb_done, res_done = (
            m.sem(n) for n in ("w1_done", "hidden_done", "w2_done", "yb_done", "res_done"))
        out_dram = chunk_view(out)
        block = stack.enter_context(nc.Block())

        @block.sync
        def _(sp):
            def step(k, par):
                if live(k, par, NCH):
                    need(sp, yb_done, 2 * k + par - 1)
                    sp.dma_start(row2[par][:, :], s["badd"][k][:, 2 * D:3 * D].to_broadcast([P, D]))\
                        .then_inc(row_in[par], 16)
                    r.load(sp, k, par)
                k2, p2 = back(k, par, 3)
                if live(k2, p2, NCH):
                    n2 = 2 * k2 + p2
                    sp.wait_ge(res_done, 2 * (n2 + 1))
                    sp.dma_start(out_dram[n2], res[p2][:, :, :]).then_inc(stored[p2], 16)

            steps(sp, step, NCH + 3, 4, NCH)
            for par in range(2):
                sp.wait_ge(stored[par], 16 * NCH // 2)

        @block.gpsimd
        def _(pool):
            def step(k, par):
                n = 2 * k + par
                r.pool_add(pool, k, par)
                r.pool_rstd(pool, k, par)
                pool.wait_ge(row_in[par], 16 * (k + 1))
                need(pool, res_done, 2 * (n - 1))
                pool.tensor_tensor(yb[par][:, :, :], r.y[par][:, :, :],
                                   row2[par].rearrange("p (t d) -> p t d", t=1).to_broadcast([P, TPC, D]),
                                   ALU.add).then_inc(yb_done, 1)

            steps(pool, step, NCH, 2, NCH)

        @block.tensor
        def _(pe):
            def step(k, par):
                if live(k, par, NCH):
                    r.turn_att(pe, k, par)
                k2, p2 = back(k, par, 2)
                if live(k2, p2, NCH):
                    up(2 * k2 + p2, p2)
                if live(k, par, NCH):
                    r.project(pe, k, par)
                if live(k2, p2, NCH):
                    down(2 * k2 + p2, p2)
                k1, p1 = back(k, par, 1)
                if live(k1, p1, NCH):
                    r.turn_h(pe, k1, p1)

            def up(n, par):
                pe.wait_ge(r.hT_sb, DC * (n + 1))
                for f in range(FC):
                    need(pe, hidden_done, FC * n + f - 1)
                    for c in range(DC):
                        last = pe.matmul(w1_ps[f % 2][:, :], W["w1"][:, c, f * P:(f + 1) * P], r.hT[par][:, c, :],
                                         start=(c == 0), stop=(c == DC - 1))
                    last.then_inc(w1_done, 1)

            def down(n, par):
                pe.wait_ge(hidden_done, FC * (n + 1))
                for t in range(TPC):
                    if t % 2 == 0:
                        need(pe, res_done, 2 * (n - 1) + t // 2 + 1)
                    for f in range(FC):
                        last = pe.matmul(w2_ps[t // 2][:, (t % 2) * D:(t % 2 + 1) * D],
                                         hidden[par][:, f, t * P:(t + 1) * P], W["w2"][:, f, :],
                                         start=(f == 0), stop=(f == FC - 1))
                    if t % 2:
                        last.then_inc(w2_done, 1)

            steps(pe, step, NCH + 2, 4, NCH)

        @block.scalar
        def _(act):
            def step(k, par):
                if live(k, par, NCH):
                    r.take_att(act, k, par)
                k1, p1 = back(k, par, 2)
                if live(k1, p1, NCH):
                    n1 = 2 * k1 + p1
                    need(act, w2_done, 2 * (n1 - 1))
                    for f in range(FC):
                        act.wait_ge(w1_done, FC * n1 + f + 1)
                        act.activation(hidden[p1][:, f, :], w1_ps[f % 2][:, :], ACT.Gelu,
                                       bias=W["b1"][:, f:f + 1]).then_inc(hidden_done, 1)
                kh, ph = back(k, par, 1)
                if live(kh, ph, NCH):
                    r.take_h(act, kh, ph, w1_done, FC * (2 * kh + ph - 1))

            steps(act, step, NCH + 2, 4, NCH)

        @block.vector
        def _(dve):
            def free(k, par):
                need(dve, yb_done, 2 * k + par - 1)

            def step(k, par):
                if live(k, par, NCH):
                    r.add_norm(dve, k, par, free)
                k1, p1 = back(k, par, 2)
                if live(k1, p1, NCH):
                    n1 = 2 * k1 + p1
                    dve.wait_ge(yb_done, n1 + 1)
                    need(dve, stored[p1], 16 * k1)
                    for i in range(TPC // 2):
                        dve.wait_ge(w2_done, 2 * n1 + i + 1)
                        dve.tensor_tensor(res[p1][:, 2 * i:2 * i + 2, :],
                                          w2_ps[i].rearrange("p (t d) -> p t d", t=2),
                                          yb[p1][:, 2 * i:2 * i + 2, :], ALU.add).then_inc(res_done, 1)

            steps(dve, step, NCH + 2, 4, NCH)


def build(nc, a, out):
    def scratch(name, shape, dt=F32):
        return nc.dram_tensor(name, shape, dt, kind="Internal").ap()

    qk = scratch("qk_parts", [2, 2, BG, CPB, GW, CH])
    s = {
        "qk": qk,
        "v": scratch("v_ones", [BG, P, KT, HG * VW]),
        "ck": scratch("ctx_k_parts", [2, BG * GW, NK]),
        "cv": scratch("ctx_v", [BG, NK, HG * VW]),
        "cmask": scratch("ctx_mask", [BG, 1, HG * NK]),
        "cq": scratch("cross_q_parts", [2, BG, CPB, GW, CH]),
        "badd": scratch("rows", [B, 1, 3 * D]),
        "attn": scratch("attn", [BG, CPB, TPC, P, GW]),
        "x1": scratch("x1", [NCH, P, TPC, D]),
    }
    with ExitStack() as stack:
        def sb(name, shape):
            return stack.enter_context(nc.sbuf_tensor(name, shape, F32))

        W = {n: sb(n, [P, DC, D]) for n in ("sa_wq", "sa_wk", "sa_wv", "sa_wo", "ca_wq", "ca_wo")}
        W |= {"w1": sb("w1", [P, DC, FF]), "w2": sb("w2", [P, FC, D]), "b1": sb("b1", [P, FC]),
              "col": sb("col", [P, 10, DC]), "ident": sb("ident", [P, P]), "half": sb("half", [P, 2, TPC])}
        shared = Shared(Arena(nc, stack, "shared"))
        setup(nc, a, W, s, shared)
        self_qkv(nc, a, W, s, shared)
        self_attention(nc, a, W, s, shared)
        cross_q(nc, a, W, s, shared)
        cross_attention(nc, a, W, s, shared)
        mlp(nc, a, W, s, shared, out)


_INS = {"x": "x", "cond_1024": "cond", "ctx_1024": "ctx", "mask_BxS2_ik0": "mask"}
_WEIGHTS = ["ln1_g", "ln1_b", "ln3_g", "ln3_b", "ln2_g", "ln2_b", "sa_wq", "sa_bq", "sa_wk", "sa_bk", "sa_wv", "sa_bv",
            "sa_wo", "sa_bo", "ca_wq", "ca_bq", "ca_wk", "ca_bk", "ca_wv", "ca_bv", "ca_wo", "ca_bo", "tp_w", "tp_b",
            "w1", "b1", "w2", "b2"]


def kernel(**inputs):
    import numpy as np
    import concourse.bacc as bacc
    from concourse.bass_utils import run_bass_kernel_spmd

    nc = bacc.Bacc("TRN2", target_bir_lowering=False, num_devices=1)
    arrays, args = {}, {}
    for name, short in (_INS | {f"L0_xcond_{w}": w for w in _WEIGHTS}).items():
        v = np.ascontiguousarray(inputs[name])
        arrays[f"in_{short}"] = v
        args[short] = nc.dram_tensor(f"in_{short}", v.shape, mybir.dt.from_np(v.dtype), kind="ExternalInput").ap()
    out = nc.dram_tensor("out", (B, T, D), F32, kind="ExternalOutput").ap()
    with nc.allow_non_contiguous_dma(reason="a few short vectors are loaded as columns"):
        build(nc, args, out)
    r = run_bass_kernel_spmd(nc, [arrays], core_ids=[0])
    return r.results[0]["out"]
```

```python
from contextlib import ExitStack

import concourse.bass as bass
from concourse import mybir

ALU = mybir.AluOpType
ACT = mybir.ActivationFunctionType
AX_X = mybir.AxisListType.X
F32 = mybir.dt.float32
F32R = mybir.dt.float32r
I32 = mybir.dt.int32

P = 128
B, T, D = 4, 1024, 256
NK = 77
NKE = NK + NK % 2
H, HD = 16, 16
FF = 4 * D
DC = D // P
FC = FF // P
HG = 4
NG = H // HG
GW = HG * HD
BG = B * NG
CH = 512
TPC = CH // P
CPB = T // CH
NCH = B * CPB
KT = T // P
NU = BG * CPB
OUT_STEP = 2
MAXT_STEP = 6
LEAD = 3
EPS = 1e-5
SCALE = HD ** -0.5
MASKED = -1e30
VW = 2 * HD

ROWS_SPLIT = 4 * HD
ROWS_SCORE = 96
ROW_MAX = 96
ROWS = 98


def back(k, par, n):
    return k + (par - n) // 2, (par - n) % 2


def live(k, par, count):
    return not isinstance(k, int) or 0 <= 2 * k + par < count


def reuse(item, banks):
    return next(n for n in range(1, len(banks) + 1) if banks[item - n] == banks[item])


def need(eng, sem, value):
    if not isinstance(value, int) or value > 0:
        eng.wait_ge(sem, value)


def steps(eng, step, total, first, last):
    for n in range(first):
        step(n // 2, n % 2)
    with eng.Fori(first // 2, last // 2) as k:
        step(k, 0)
        step(k, 1)
    for n in range(last, total):
        step(n // 2, n % 2)


class Arena:

    def __init__(self, nc, stack, tag):
        self.nc, self.stack, self.tag = nc, stack, tag

    def sb(self, name, shape, dt=F32):
        return self.stack.enter_context(self.nc.sbuf_tensor(f"{self.tag}_{name}", shape, dt))

    def ps(self, name, shape):
        return self.stack.enter_context(self.nc.psum_tensor(f"{self.tag}_{name}", shape, F32))

    def sem(self, name):
        return self.stack.enter_context(self.nc.semaphore(f"{self.tag}_{name}"))

    def sems(self, name, n):
        return [self.sem(f"{name}{i}") for i in range(n)]


def words(ap):
    return ap.bitcast(F32)


def chunked(w):
    return w.rearrange("(c p) n -> p c n", p=P)


def column(v):
    return v.rearrange("(c p) -> p c", p=P)


class Shared:

    def __init__(self, m):
        self.rows = [m.sb(f"rows{i}", [P, CPB, HG, CH], F32R) for i in range(4)]
        self.v = [m.sb(f"v{i}", [P, KT, HG, VW]) for i in range(2)]
        self.self_in, self.qkv_stored = m.sems("self_in", 2), m.sems("qkv_stored", 2)
        self.cq = [r[:, :, 0, :] for r in self.rows]
        self.ck = [m.sb(f"ck{i}", [P, 2, NK], F32R) for i in range(NG)]
        self.cv = [m.sb(f"cv{i}", [P, HG, VW]) for i in range(NG)]
        self.mask = [m.sb(f"mask{i}", [P, NK]) for i in range(NG)]
        self.cross_in = m.sems("cross_in", NG)
        self.cq_stored = m.sems("cq_stored", 2)
        self.att = [m.sb(f"att{i}", [P, TPC, D]) for i in range(2)]
        self.x, self.x_in = [m.sb(f"x{i}", [P, TPC, D]) for i in range(2)], m.sems("x_in", 2)
        self.badd = [m.sb(f"badd{i}", [P, D]) for i in range(2)]
        self.residual_in = [m.sems(f"residual_in{i}_", 2) for i in range(2)]

    def constant_q(self, eng, zero, base, i):
        need(eng, zero, base)
        eng.memset(words(self.rows[i][ROWS_SPLIT:ROWS_SCORE, :, :, :]), 0.0).then_inc(zero, 1)

    def constant_k(self, eng, zero, base, i):
        need(eng, zero, base)
        eng.memset(words(self.rows[i][ROWS_SPLIT:ROWS_SCORE, :, :, :]), 0.0).then_inc(zero, 1)
        eng.wait_ge(zero, base + 1)
        eng.memset(words(self.rows[i][ROW_MAX:ROWS, :, :, :]), 1.0).then_inc(zero, 1)

    def load_self(self, sp, s, n, par):
        for which in range(2):
            stack_rows(sp, s["qk"][which], n, which, self.rows[2 * which + par], self.self_in[par])
        sp.dma_start(self.v[par][:, :, :, :].rearrange("p t h e -> p t (h e)"), s["v"][n])\
            .then_inc(self.self_in[par], 16)

    def load_cross(self, sp, s, b, g):
        n, sem = NG * b + g, self.cross_in[g]
        for copy in range(2):
            at = slice(copy * GW, (copy + 1) * GW)
            sp.dma_start(words(self.cq[g][at, :, :]), s["cq"][copy][n]).then_inc(sem, 16)
            for part in range(2):
                src = s["ck"][part].rearrange("(n r) k -> n r k", r=GW)[n]
                sp.dma_start(words(self.ck[g][at, part, :]), src).then_inc(sem, 16)
        sp.dma_start(self.mask[g][:, :], s["cmask"][n][:, 0:NK].to_broadcast([P, NK])).then_inc(sem, 16)
        sp.dma_start(self.cv[g][0:NK, :, :].rearrange("k h e -> k (h e)"), s["cv"][n]).then_inc(sem, 16)

    def load_residual(self, sp, s, x_dram, row, k, par):
        sem = self.residual_in[row][par]
        for g in range(NG):
            src = s["attn"].rearrange("(b g) c t p e -> b g c p t e", b=B)[k, g, par]
            sp.dma_start(self.att[par][:, :, g * GW:(g + 1) * GW], src).then_inc(sem, 16)
        sp.dma_start(self.x[par][:, :, :], x_dram[2 * k + par]).then_inc(sem, 16)
        sp.dma_start(self.badd[par][:, :], s["badd"][k][:, row * D:(row + 1) * D].to_broadcast([P, D]))\
            .then_inc(sem, 16)


CQ_STORES = 16 * 2
QKV_STORES = 2 * 2 + NG
SELF_LOADS = 16 * (2 * 4 * CPB + 1)
CROSS_LOADS = 16 * 8
RESIDUAL_LOADS = 16 * (NG + 2)


def setup(nc, a, W, s, shared):
    ident, half = W["ident"], W["half"]
    with ExitStack() as stack:
        m = Arena(nc, stack, "setup")
        ctx = m.sb("ctx", [NK, B, D])
        ctxT = m.sb("ctxT", [P, DC, B * NK])
        wk, wv = m.sb("ca_wk", [P, DC, D]), m.sb("ca_wv", [P, DC, D])
        kfull = m.sb("kfull", [P, DC, B * NK])
        khi, klo = (m.sb(n, [P, DC, B * NK], F32R) for n in ("khi", "klo"))
        vaug = m.sb("vaug", [NK, B, H, VW])
        mask_i, mask_f = m.sb("mask_i", [NK, B], I32), m.sb("mask_f", [NK, B])
        maskrow_i = m.sb("maskrow_i", [BG, HG * NK], I32)
        maskrow_f = m.sb("maskrow_f", [BG, HG * NK])
        maskrow = m.sb("maskrow", [BG, HG * NK], F32R)
        cond = m.sb("cond", [B, D])
        sig, silu = m.sb("sig", [B, D]), m.sb("silu", [B, D])
        siluT, bvT = m.sb("siluT", [P, DC, B]), m.sb("bvT", [P, 2, DC])
        bv4 = m.sb("bv4", [P, 2, DC, B])
        tpw = m.sb("tpw", [P, DC, 3 * D])
        tprow, brow = m.sb("tprow", [B, 3 * D]), m.sb("brow", [B, 3 * D])
        badd = m.sb("badd", [B, 3 * D])
        trans = [m.ps(f"trans{c}", [P, 512]) for c in range(DC)]
        pk = [m.ps(f"pk{c}", [P, 512]) for c in range(DC)]
        pv = [m.ps(f"pv{i}", [P, 512]) for i in range(2)]
        prow = [m.ps(f"prow{i}", [P, 512]) for i in range(2)]
        ctx_in, cw_in, cond_in, tp_in, mask_in, w_in = (
            m.sem(n) for n in ("ctx_in", "cw_in", "cond_in", "tp_in", "mask_in", "w_in"))
        const, zero, own, ctxT_ps, ctxT_sb, k_ps, khi_sb, k_sb, klo_sb, v_ps, ones_sb, v_sb = (
            m.sem(n) for n in ("const", "zero", "own", "ctxT_ps", "ctxT_sb", "k_ps", "khi_sb", "k_sb",
                               "klo_sb", "v_ps", "ones_sb", "v_sb"))
        e_sb, silu_sb, siluT_ps, siluT_sb, bv_sb, row_ps, row_sb, maskrow_sb, stored = (
            m.sem(n) for n in ("e_sb", "silu_sb", "siluT_ps", "siluT_sb", "bv_sb", "row_ps", "row_sb",
                               "maskrow_sb", "stored"))
        dve_rows, pool_rows = m.sem("dve_rows"), m.sem("pool_rows")
        block = stack.enter_context(nc.Block())

        @block.sync
        def _(sp):
            sp.dma_start(ctx[:, :, :], a["ctx"].rearrange("b k d -> k b d")).then_inc(ctx_in, 16)
            sp.dma_start(wk[:, :, :], chunked(a["ca_wk"])).then_inc(cw_in, 16)
            sp.dma_start(wv[:, :, :], chunked(a["ca_wv"])).then_inc(cw_in, 16)
            sp.dma_start(W["col"][:, 7, :], column(a["ca_bk"])).then_inc(cw_in, 16)
            sp.dma_start(mask_i[:, :], a["mask"].rearrange("b k -> k b")).then_inc(mask_in, 16)
            for b in range(B):
                sp.dma_start(maskrow_i[b * NG:(b + 1) * NG, :].rearrange("g (h k) -> g h k", h=HG),
                             a["mask"][b:b + 1, :].rearrange("b (u k) -> b u k", u=1).to_broadcast([NG, HG, NK]))\
                    .then_inc(mask_in, 16)
            for par in range(2):
                sp.dma_start(shared.x[par][:, :, :], chunk_view(a["x"])[par]).then_inc(shared.x_in[par], 16)
            for name in ("sa_wq", "sa_wk", "sa_wv", "sa_wo", "ca_wq", "ca_wo"):
                sp.dma_start(W[name][:, :, :], chunked(a[name])).then_inc(w_in, 16)
            for n, name in enumerate(("ln1_g", "ln1_b", "ln3_g", "ln3_b", "ln2_g", "ln2_b", "sa_bq")):
                sp.dma_start(W["col"][:, n, :], column(a[name])).then_inc(w_in, 16)
            for n, name in enumerate(("sa_bk", "ca_bq")):
                sp.dma_start(W["col"][:, 8 + n, :], column(a[name])).then_inc(w_in, 16)
            sp.dma_start(W["b1"][:, :], column(a["b1"])).then_inc(w_in, 16)

            sp.wait_ge(khi_sb, DC)
            sp.wait_ge(klo_sb, DC)
            for part, src in enumerate((khi, klo)):
                for c in range(DC):
                    dst = s["ck"][part].rearrange("(b c r) k -> c r b k", b=B, c=DC)[c]
                    sp.dma_start(dst, words(src[:, c, :]).rearrange("r (b k) -> r b k", b=B)).then_inc(stored, 16)
            sp.wait_ge(v_sb, B)
            sp.dma_start(s["cv"].rearrange("n k e -> k n e"),
                         vaug.rearrange("k b (g h) e -> k (b g) (h e)", g=NG)).then_inc(stored, 16)
            sp.wait_ge(maskrow_sb, 1)
            sp.dma_start(s["cmask"].rearrange("n u k -> (n u) k"), words(maskrow[:, :])).then_inc(stored, 16)
            sp.wait_ge(row_sb, 2)
            sp.dma_start(s["badd"].rearrange("b u d -> (b u) d"), badd[:, :]).then_inc(stored, 16)
            sp.wait_ge(stored, 16 * (2 * DC + 3))
            sp.wait_ge(w_in, 16 * 16)

        @block.gpsimd
        def _(pool):
            pool.memset(ident[:, :], 0.0).then_inc(zero, 1)
            pool.memset(half[:, 0, :], EPS).then_inc(const, 1)
            pool.memset(half[:, 1, :], -0.5).then_inc(const, 1)
            pool.wait_ge(zero, 1)
            pool.affine_select(out=ident[:, :], in_=ident[:, :], compare_op=ALU.not_equal, fill=1.0,
                               base=0, pattern=[[-1, P]], channel_multiplier=1).then_inc(const, 1)
            pool.memset(vaug[:, :, :, HD:VW], 1.0).then_inc(ones_sb, 1)
            pool.wait_ge(ones_sb, 1)
            for i in range(2):
                shared.constant_k(pool, pool_rows, 2 * i, 2 + i)
            shared.constant_q(pool, pool_rows, 4, 1)
            pool.wait_ge(pool_rows, 5)
            for c in range(DC):
                pool.wait_ge(khi_sb, c + 1)
                pool.tensor_tensor(klo[:, c, :], kfull[:, c, :], khi[:, c, :].bitcast(F32),
                                   ALU.subtract).then_inc(klo_sb, 1)

        @block.scalar
        def _(act):
            act.dma_start(cond[:, :], a["cond"]).then_inc(cond_in, 16)
            act.dma_start(tpw[:, :, :], chunked(a["tp_w"])).then_inc(tp_in, 16)
            act.dma_start(tprow[:, :], a["tp_b"].rearrange("(u n) -> u n", u=1).to_broadcast([B, 3 * D])).then_inc(tp_in, 16)
            for n, name in enumerate(("sa_bo", "ca_bo", "b2")):
                act.dma_start(brow[:, n * D:(n + 1) * D],
                              a[name].rearrange("(u n) -> u n", u=1).to_broadcast([B, D])).then_inc(tp_in, 16)
            for n, name in enumerate(("sa_bv", "ca_bv")):
                act.dma_start(bvT[:, n, :], column(a[name])).then_inc(tp_in, 16)
            act.wait_ge(cond_in, 16)
            act.activation(sig[:, :], cond[:, :], ACT.Exp, scale=-1.0).then_inc(e_sb, 1)
            for c in range(DC):
                act.wait_ge(k_sb, c + 1)
                act.activation(khi[:, c, :], kfull[:, c, :], ACT.Copy).then_inc(khi_sb, 1)

        @block.tensor
        def _(pe):
            pe.wait_ge(const, 3)
            pe.wait_ge(ctx_in, 16)
            for c in range(DC):
                for b in range(B):
                    last = pe.transpose(trans[c][:, b * NK:(b + 1) * NK], ctx[:, b, c * P:(c + 1) * P],
                                        ident[0:NK, 0:NK])
                last.then_inc(ctxT_ps, 1)
            pe.wait_ge(ctxT_sb, DC)
            pe.wait_ge(cw_in, 48)
            for m_ in range(DC):
                for c in range(DC):
                    last = pe.matmul(pk[m_][:, 0:B * NK], wk[:, c, m_ * P:(m_ + 1) * P], ctxT[:, c, :],
                                     start=(c == 0), stop=(c == DC - 1))
                last.then_inc(k_ps, 1)
            for b in range(B):
                for c in range(DC):
                    last = pe.matmul(pv[b // 2][0:NK, (b % 2) * D:(b % 2 + 1) * D],
                                     ctxT[:, c, b * NK:(b + 1) * NK], wv[:, c, :],
                                     start=(c == 0), stop=(c == DC - 1))
                last.then_inc(v_ps, 1)
            pe.wait_ge(silu_sb, 1)
            for c in range(DC):
                last = pe.transpose(trans[0][:, c * B:(c + 1) * B], silu[:, c * P:(c + 1) * P], ident[0:B, 0:B])
            last.then_inc(siluT_ps, 1)
            pe.wait_ge(siluT_sb, 1)
            pe.wait_ge(bv_sb, 1)
            pe.wait_ge(tp_in, 16 * 7)
            pe.wait_ge(w_in, 16 * 16)
            for n in range(3):
                dst = prow[n // 2][0:B, (n % 2) * D:(n % 2 + 1) * D]
                for c in range(DC):
                    last = pe.matmul(dst, siluT[:, c, :], tpw[:, c, n * D:(n + 1) * D],
                                     start=(c == 0), stop=(c == DC - 1 and n == 2))
                if n < 2:
                    wo = W["sa_wo"] if n == 0 else W["ca_wo"]
                    for c in range(DC):
                        last = pe.matmul(dst, bv4[:, n, c, :], wo[:, c, :], start=False, stop=(c == DC - 1))
            last.then_inc(row_ps, 1)

        @block.vector
        def _(dve):
            shared.constant_q(dve, dve_rows, 0, 0)
            dve.wait_ge(mask_in, 16 * (B + 1))
            dve.tensor_copy(mask_f[:, :], mask_i[:, :]).then_inc(own, 1)
            dve.tensor_copy(maskrow_f[:, :], maskrow_i[:, :]).then_inc(own, 1)
            dve.wait_ge(own, 2)
            dve.tensor_scalar(mask_f[:, :], mask_f[:, :], 0.0, None, ALU.not_equal).then_inc(own, 1)
            dve.tensor_scalar(maskrow[:, :], maskrow_f[:, :], 0.0, MASKED, ALU.is_equal, ALU.mult)\
                .then_inc(maskrow_sb, 1)
            for c in range(DC):
                dve.wait_ge(ctxT_ps, c + 1)
                dve.tensor_copy(ctxT[:, c, :], trans[c][:, 0:B * NK]).then_inc(ctxT_sb, 1)
            dve.wait_ge(e_sb, 1)
            dve.tensor_scalar(sig[:, :], sig[:, :], 1.0, None, ALU.add).then_inc(own, 1)
            dve.wait_ge(own, 4)
            dve.reciprocal(sig[:, :], sig[:, :]).then_inc(own, 1)
            dve.wait_ge(own, 5)
            dve.tensor_tensor(silu[:, :], cond[:, :], sig[:, :], ALU.mult).then_inc(silu_sb, 1)
            dve.wait_ge(tp_in, 16 * 7)
            dve.tensor_copy(bv4[:, :, :, :],
                            bvT.rearrange("p n (c u) -> p n c u", u=1).to_broadcast([P, 2, DC, B])).then_inc(bv_sb, 1)
            dve.tensor_tensor(brow[:, :], brow[:, :], tprow[:, :], ALU.add).then_inc(own, 1)
            dve.wait_ge(siluT_ps, 1)
            dve.tensor_copy(siluT.rearrange("p c b -> p (c b)"), trans[0][:, 0:DC * B]).then_inc(siluT_sb, 1)
            dve.wait_ge(cw_in, 48)
            for c in range(DC):
                dve.wait_ge(k_ps, c + 1)
                dve.tensor_scalar(kfull[:, c, :], pk[c][:, 0:B * NK], W["col"][:, 7, c:c + 1], None,
                                  ALU.add).then_inc(k_sb, 1)
            dve.wait_ge(ones_sb, 1)
            for b in range(B):
                dve.wait_ge(v_ps, b + 1)
                dve.tensor_scalar(vaug[:, b, :, 0:HD],
                                  pv[b // 2][0:NK, (b % 2) * D:(b % 2 + 1) * D].rearrange("k (h e) -> k h e", h=H),
                                  mask_f[:, b:b + 1], None, ALU.mult).then_inc(own, 1)
                dve.tensor_scalar(vaug[:, b, :, HD:VW], vaug[:, b, :, HD:VW], mask_f[:, b:b + 1], None,
                                  ALU.mult).then_inc(v_sb, 1)
            dve.wait_ge(own, 6 + B)
            dve.wait_ge(row_ps, 1)
            for n in range(2):
                w = min(2, 3 - 2 * n) * D
                dve.tensor_tensor(badd[:, 2 * n * D:2 * n * D + w], prow[n][0:B, 0:w],
                                  brow[:, 2 * n * D:2 * n * D + w], ALU.add).then_inc(row_sb, 1)


def norm_stats(dve, x, stats, moments, own, count):
    for t in range(TPC):
        last = dve.bn_stats(stats[:, t, :], x[:, t, :])
    last.then_inc(own, 1)
    dve.wait_ge(own, count)
    dve.memset(stats[:, TPC, 0:1], 0.0)
    for t in range(TPC):
        last = dve.bn_aggr(moments[:, t, :], stats[:, t, :])
    return last


def rstd_of(pool, moments, rstd, half, own, count):
    pool.tensor_tensor(rstd[:, :], moments[:, :, 1], half[:, 0, :], ALU.add).then_inc(own, 1)
    pool.wait_ge(own, count)
    return pool.tensor_tensor(rstd[:, :], rstd[:, :], half[:, 1, :], ALU.pow)


def normalize(dve, xhat, x, moments, rstd):
    for t in range(TPC):
        last = dve.tensor_scalar(xhat[:, t, :], x[:, t, :], moments[:, t, 0:1], rstd[:, t:t + 1],
                                 ALU.subtract, ALU.mult)
    return last


def turn(pe, banks, tokens, ident, sem):
    for c in range(DC):
        for t in range(TPC):
            last = pe.transpose(banks[c][:, t * P:(t + 1) * P], tokens[:, t, c * P:(c + 1) * P], ident[:, :])
        last.then_inc(sem, 1)


def self_qkv(nc, a, W, s, shared):
    ident, half, col = W["ident"], W["half"], W["col"]
    x_dram = chunk_view(a["x"])
    NQK = 2 * DC
    with ExitStack() as stack:
        m = Arena(nc, stack, "qkv")
        x, xhat = shared.x, shared.att
        stats, moments, rstd = m.sb("stats", [P, TPC + 1, 6]), m.sb("moments", [P, TPC, 2]), m.sb("rstd", [P, TPC])
        hT = [m.sb(f"hT{i}", [P, DC, CH]) for i in range(2)]
        full = [m.sb(f"full{i}", [P, NQK, CH]) for i in range(2)]
        hi = [m.sb(f"hi{i}", [P, NQK, CH], F32R) for i in range(2)]
        lo = [m.sb(f"lo{i}", [P, NQK, CH], F32R) for i in range(2)]
        vaug = [m.sb(f"vaug{i}", [P, TPC, H, VW]) for i in range(2)]
        turned = [m.ps(f"turned{c}", [P, CH]) for c in range(DC)]
        qk_ps = [m.ps(f"qk{i}", [P, CH]) for i in range(NQK)]
        v_ps = [m.ps(f"v{i}", [P, 2 * D]) for i in range(TPC // 2)]
        x_in, stored = shared.x_in, shared.qkv_stored
        own, pool_own, ones, stats_done, rstd_done, xhat_done, turned_done, hT_done = (
            m.sem(n) for n in ("own", "pool_own", "ones", "stats_done", "rstd_done", "xhat_done", "turned_done",
                               "hT_done"))
        qk_done, hi_done, full_done, lo_done, v_done, vaug_done = (
            m.sem(n) for n in ("qk_done", "hi_done", "full_done", "lo_done", "v_done", "vaug_done"))
        block = stack.enter_context(nc.Block())

        @block.sync
        def _(sp):
            def step(k, par):
                n = 2 * k + par
                if live(k, par, NCH) and not (isinstance(k, int) and k == 0):
                    sp.wait_ge(xhat_done, n - 1)
                    sp.dma_start(x[par][:, :, :], x_dram[n]).then_inc(x_in[par], 16)
                if isinstance(k, int) and n == NCH + 1:
                    for first in range(2):
                        sp.wait_ge(stored[first], 16 * QKV_STORES)
                    shared.load_self(sp, s, 0, 0)
                k2, p2 = back(k, par, 3)
                if live(k2, p2, NCH):
                    n2 = 2 * k2 + p2
                    sp.wait_ge(hi_done, NQK * (n2 + 1))
                    sp.wait_ge(lo_done, NQK * (n2 + 1))
                    for which in range(2):
                        for part, src in enumerate((hi, lo)):
                            dst = s["qk"][which, part].rearrange("(b c g) r q t -> b q (g r) c t", b=B, c=DC)
                            sp.dma_start(dst[k2, p2], words(src[p2][:, which * DC:(which + 1) * DC, :]))\
                                .then_inc(stored[p2], 16)
                    sp.wait_ge(vaug_done, 2 * (n2 + 1))
                    for g in range(NG):
                        dst = s["v"].rearrange("(b g) p t e -> b g p t e", b=B)[k2, g, :, p2 * TPC:(p2 + 1) * TPC, :]
                        sp.dma_start(dst, vaug[p2][:, :, g * HG:(g + 1) * HG, :].rearrange("p t h e -> p t (h e)"))\
                            .then_inc(stored[p2], 16)

            steps(sp, step, NCH + 3, 4, NCH)

        @block.gpsimd
        def _(pool):
            for i in range(2):
                pool.memset(vaug[i][:, :, :, HD:VW], 1.0).then_inc(ones, 1)
            for g in range(NG):
                pool.wait_ge(ones, 2 + g)
                pool.memset(shared.cv[g][:, :, :], 0.0).then_inc(ones, 1)
            pool.wait_ge(ones, 2 + NG)

            def step(k, par):
                n = 2 * k + par
                if live(k, par, NCH):
                    pool.wait_ge(stats_done, n + 1)
                    need(pool, xhat_done, n)
                    rstd_of(pool, moments, rstd, half, pool_own, n + 1).then_inc(rstd_done, 1)
                k2, p2 = back(k, par, 2)
                if live(k2, p2, NCH):
                    n2 = 2 * k2 + p2
                    need(pool, stored[p2], 16 * QKV_STORES * k2)
                    for i in range(NQK):
                        pool.wait_ge(hi_done, NQK * n2 + i + 1)
                        pool.tensor_tensor(lo[p2][:, i, :], full[p2][:, i, :], hi[p2][:, i, :].bitcast(F32),
                                           ALU.subtract).then_inc(lo_done, 1)

            steps(pool, step, NCH + 2, 4, NCH)

        @block.vector
        def _(dve):
            dve.wait_ge(ones, 2)

            def step(k, par):
                n = 2 * k + par
                if live(k, par, NCH):
                    dve.wait_ge(x_in[par], 16 * (k + 1))
                    norm_stats(dve, x[par], stats, moments, own, n + 1).then_inc(stats_done, 1)
                    dve.wait_ge(rstd_done, n + 1)
                    need(dve, turned_done, DC * (n - 1))
                    normalize(dve, xhat[par], x[par], moments, rstd).then_inc(xhat_done, 1)
                k2, p2 = back(k, par, 2)
                if live(k2, p2, NCH):
                    n2 = 2 * k2 + p2
                    need(dve, lo_done, NQK * (n2 - 1))
                    for i in range(NQK):
                        dve.wait_ge(qk_done, NQK * n2 + i + 1)
                        dve.tensor_scalar(full[p2][:, i, :], qk_ps[i][:, :], col[:, 6 + i // DC * 2, i % DC:i % DC + 1],
                                          None, ALU.add).then_inc(full_done, 1)
                    need(dve, stored[p2], 16 * QKV_STORES * k2)
                    for i in range(TPC // 2):
                        dve.wait_ge(v_done, 2 * n2 + i + 1)
                        dve.tensor_copy(vaug[p2][:, 2 * i:2 * i + 2, :, 0:HD],
                                        v_ps[i].rearrange("p (t h e) -> p t h e", t=2, h=H)).then_inc(vaug_done, 1)

            steps(dve, step, NCH + 2, 4, NCH)

        @block.scalar
        def _(act):
            def step(k, par):
                n = 2 * k + par
                if live(k, par, NCH):
                    for c in range(DC):
                        act.wait_ge(turned_done, DC * n + c + 1)
                        if c == 0:
                            need(act, v_done, 2 * (n - 1))
                        act.activation(hT[par][:, c, :], turned[c][:, :], ACT.Identity, scale=col[:, 0, c:c + 1],
                                       bias=col[:, 1, c:c + 1]).then_inc(hT_done, 1)
                k1, p1 = back(k, par, 1)
                if live(k1, p1, NCH):
                    n1 = 2 * k1 + p1
                    need(act, stored[p1], 16 * QKV_STORES * k1)
                    for i in range(NQK):
                        act.wait_ge(full_done, NQK * n1 + i + 1)
                        act.activation(hi[p1][:, i, :], full[p1][:, i, :], ACT.Copy).then_inc(hi_done, 1)

            steps(act, step, NCH + 1, 4, NCH)

        @block.tensor
        def _(pe):
            def step(k, par):
                n = 2 * k + par
                if live(k, par, NCH):
                    pe.wait_ge(xhat_done, n + 1)
                    need(pe, hT_done, DC * n)
                    turn(pe, turned, xhat[par], ident, turned_done)
                k1, p1 = back(k, par, 1)
                if live(k1, p1, NCH):
                    n1 = 2 * k1 + p1
                    pe.wait_ge(hT_done, DC * (n1 + 1))
                    for i in range(NQK):
                        w, mc = W["sa_wq" if i < DC else "sa_wk"], i % DC
                        need(pe, full_done, NQK * (n1 - 1) + i + 1)
                        for c in range(DC):
                            last = pe.matmul(qk_ps[i][:, :], w[:, c, mc * P:(mc + 1) * P], hT[p1][:, c, :],
                                             start=(c == 0), stop=(c == DC - 1))
                        last.then_inc(qk_done, 1)
                    for t in range(TPC):
                        if t % 2 == 0:
                            need(pe, vaug_done, 2 * (n1 - 1) + t // 2 + 1)
                        for c in range(DC):
                            last = pe.matmul(v_ps[t // 2][:, (t % 2) * D:(t % 2 + 1) * D],
                                             hT[p1][:, c, t * P:(t + 1) * P], W["sa_wv"][:, c, :],
                                             start=(c == 0), stop=(c == DC - 1))
                        if t % 2:
                            last.then_inc(v_done, 1)

            steps(pe, step, NCH + 1, 4, NCH)


def stack_rows(sp, dram, n, which, dst, sem):
    for block in range(4):
        lo = block // 2 if which == 0 else block % 2
        for c in range(CPB):
            src = dram[lo].rearrange("n (h e) c t -> n c e h t", h=HG)[n, c]
            sp.dma_start(words(dst[block * HD:(block + 1) * HD, c, :, :]), src).then_inc(sem, 16)


class Slots:

    def __init__(self):
        tiles = HG * TPC
        self.order = [("max", 0, j) for j in range(tiles)] + [("maxT", 0, 0)] + [("max", 1, j) for j in range(2 * LEAD)]
        for u in range(NU):
            for st in range(KT):
                self.order += [("max", *self.tile(u, st, 0))]
                if st == OUT_STEP:
                    self.order += [("out", u - 1, 0)]
                if st == MAXT_STEP:
                    self.order += [("maxT", u + 1, 0)]
                self.order += [("max", *self.tile(u, st, 1))]
        self.order = [i for i in self.order + [("out", NU - 1, 0)] if 0 <= i[1] < NU]
        self.number = {item: n for n, item in enumerate(self.order)}
        self.per_unit = self.number["max", 5, 0] - self.number["max", 4, 0]

    @staticmethod
    def tile(u, st, i):
        j = 2 * (st + LEAD) + i
        return (u + 1, j) if j < HG * TPC else (u + 2, j - HG * TPC)

    def at(self, kind, u, j):
        if isinstance(u, int):
            return self.number[kind, u, j], self.number[kind, u, j] % 2
        base = self.number[kind, 4, j] - 4 * self.per_unit
        return base + self.per_unit * u, base % 2


def self_attention(nc, a, W, s, shared):
    ident = W["ident"]
    NMAX = HG * TPC
    NEXP = HG * KT
    NB, EXP_SHIFT = 3, HG * (KT // 2) + 2
    exp_bank = [(i + (i >= EXP_SHIFT)) % NB for i in range(NEXP)]
    with ExitStack() as stack:
        m = Arena(nc, stack, "sa")
        q, kk, v = shared.rows[0:2], shared.rows[2:4], shared.v
        maxima = [m.sb(f"maxima{i}", [P, NMAX]) for i in range(2)]
        maxrows, maxT = m.sb("maxrows", [P, 2, NMAX], F32R), m.sb("maxT", [2 * NMAX, P], F32R)
        zeros, minus = m.sb("zeros", [P, NMAX]), m.sb("minus", [P, NMAX])
        o_sb = m.sb("o_sb", [P, CH])
        inv = m.sb("inv", [P, TPC, HG])
        o_out = [m.sb(f"o_out{i}", [P, TPC, HG, HD]) for i in range(2)]
        NP_ = 4
        probs = [m.sb(f"probs{i}", [P, HG, CH]) for i in range(NP_)]
        slot = [m.ps(f"slot{i}", [P, T]) for i in range(2)]
        s_exp = [m.ps(f"s_exp{i}", [P, CH]) for i in range(NB)]
        o_ps = m.ps("o", [P, CH])
        slots = Slots()
        rows_in, out_done = shared.self_in, m.sems("out_done", 2)
        zero, max_in, filled, emptied, negated, own, s_done, exp_done, pv_done, o_done, inv_done, w_in = (
            m.sem(n) for n in ("zero", "max_in", "filled", "emptied", "negated", "own", "s_done", "exp_done",
                               "pv_done", "o_done", "inv_done", "w_in"))
        block = stack.enter_context(nc.Block())

        @block.sync
        def _(sp):
            def max_rows(u, par, qc):
                sp.wait_ge(emptied, slots.at("maxT", u, 0)[0] + 1)
                rows = words(q[par][ROW_MAX:ROWS, qc, :, :]).rearrange("r h (t p) -> r (h t) p", t=TPC)
                sp.dma_start(rows, words(maxT[:, :])).then_inc(max_in, 16)

            max_rows(0, 0, 0)
            for par in range(2):
                sp.wait_ge(shared.qkv_stored[par], 16 * QKV_STORES * NCH // 2)

            def step(k, par):
                n = 2 * k + par
                if live(k, par, BG - 1):
                    need(sp, pv_done, 2 * KT * n)
                    shared.load_self(sp, s, n + 1, 1 - par)
                for qc in range(CPB):
                    u = CPB * n + qc
                    if live(k, par, BG - 1) or qc == 0:
                        max_rows(u + 1, par if qc == 0 else 1 - par, 1 - qc)
                    if not (isinstance(k, int) and k == 0 and par == 0 and qc == 0):
                        store(back(k, par, 1) if qc == 0 else (k, par), 1 - qc)
                    if isinstance(n, int) and n == BG - 2:
                        sp.wait_ge(out_done[qc], 16 * NG)
                        shared.load_residual(sp, s, chunk_view(a["x"]), 0, 0, qc)

            def store(which, qc):
                n = 2 * which[0] + which[1]
                sp.wait_ge(emptied, slots.at("out", CPB * n + qc, 0)[0] + 1)
                sp.dma_start(s["attn"][n, qc].rearrange("t p e -> p t e"),
                             o_out[qc].rearrange("p t h e -> p t (h e)")).then_inc(out_done[qc], 16)

            steps(sp, step, BG, 2, BG - 2)
            store((BG // 2 - 1, 1), 1)
            for qc in range(CPB):
                sp.wait_ge(out_done[qc], 16 * BG)
            sp.wait_ge(w_in, 32)

        @block.gpsimd
        def _(pool):
            pool.memset(zeros[:, :], 0.0).then_inc(zero, 1)
            pool.wait_ge(zero, 1)
            def negate(u, qc):
                pool.wait_ge(emptied, slots.at("max", u, NMAX - 1)[0] + 1)
                if not isinstance(u, int) or u > 0:
                    pool.wait_ge(filled, slots.at("maxT", u - 1, 0)[0] + 1)
                pool.tensor_tensor(minus[:, :], zeros[:, :], maxima[qc][:, :], ALU.subtract).then_inc(own, 1)
                pool.wait_ge(own, 2 * u + 1)
                pool.tensor_tensor(maxrows[:, 0, :], minus[:, :], zeros[:, :], ALU.subtract).then_inc(own, 1)
                pool.wait_ge(own, 2 * u + 2)
                pool.tensor_tensor(maxrows[:, 1, :], minus[:, :], maxrows[:, 0, :].bitcast(F32), ALU.subtract)\
                    .then_inc(negated, 1)

            negate(0, 0)
            for name in ("w1", "w2"):
                pool.dma_start(W[name][:, :, :], chunked(a[name])).then_inc(w_in, 16)

            def step(k, par):
                for qc in range(CPB):
                    if live(k, par, BG - 1) or qc == 0:
                        negate(CPB * (2 * k + par) + qc + 1, 1 - qc)

            steps(pool, step, BG, 2, BG - 2)

        @block.tensor
        def _(pe):
            def take(kind, u, j):
                number, which = slots.at(kind, u, j)
                need(pe, emptied, number - 1)
                return slot[which]

            def score_max(u, par, qc, j):
                h, t = j // TPC, j % TPC
                dst = take("max", u, j)
                tile = q[par][0:ROWS_SCORE, qc, h, t * P:(t + 1) * P]
                for c in range(CPB):
                    last = pe.matmul(dst[:, c * CH:(c + 1) * CH], tile, kk[par][0:ROWS_SCORE, c, h, :],
                                     start=True, stop=True)
                last.then_inc(filled, 1)

            def turn_max(u):
                pe.wait_ge(negated, u + 1)
                pe.transpose(take("maxT", u, 0)[0:2 * NMAX, 0:P],
                             maxrows[:, :, :].bitcast(F32).rearrange("p r j -> p (r j)"), ident[:, :])\
                    .then_inc(filled, 1)

            def turn_out(u):
                pe.wait_ge(o_done, u + 1)
                dst = take("out", u, 0)
                for t in range(TPC):
                    last = pe.transpose(dst[:, t * P:(t + 1) * P], o_sb[:, t * P:(t + 1) * P], ident[:, :])
                last.then_inc(filled, 1)

            def values(u, par, st):
                if st == 0:
                    need(pe, o_done, u)
                pe.wait_ge(exp_done, HG * (KT * u + st + 1))
                for h in range(HG):
                    last = pe.matmul(o_ps[h * VW:(h + 1) * VW, :], v[par][:, st, h, :], probs[st % NP_][:, h, :],
                                     start=(st == 0), stop=(st == KT - 1), tile_position=(0, h * VW))
                last.then_inc(pv_done, 1)

            def prologue():
                pe.wait_ge(rows_in[0], SELF_LOADS)
                for j in range(NMAX):
                    score_max(0, 0, 0, j)
                turn_max(0)
                for j in range(2 * LEAD):
                    score_max(1, 0, 1, j)

            prologue()

            def step(k, par):
                n = 2 * k + par
                more = live(k, par, BG - 1)
                k1, p1 = back(k, par, -1)
                for qc in range(CPB):
                    u = CPB * n + qc
                    next_par, next_qc = (par, 1) if qc == 0 else (1 - par, 0)
                    pe.wait_ge(max_in, 16 * (u + 1))
                    for st in range(KT):
                        for h in range(HG):
                            i = HG * st + h
                            need(pe, exp_done, NEXP * u + i + 1 - reuse(i, exp_bank))
                            pe.matmul(s_exp[exp_bank[i]][:, :], kk[par][0:ROWS, st // TPC, h, st % TPC * P:(st % TPC + 1) * P],
                                      q[par][0:ROWS, qc, h, :], start=True, stop=True).then_inc(s_done, 1)
                            if h in (0, 3):
                                j = 2 * (st + LEAD) + h // 3
                                if j < NMAX:
                                    if more or qc == 0:
                                        score_max(u + 1, next_par, next_qc, j)
                                elif more:
                                    if qc == 0 and j == NMAX:
                                        pe.wait_ge(rows_in[1 - par], SELF_LOADS * (k1 + 1))
                                    score_max(u + 2, 1 - par, qc, j - NMAX)
                            if h == 1:
                                if st > 0:
                                    values(u, par, st - 1)
                                elif not (isinstance(u, int) and u == 0):
                                    values(u - 1, par if qc else 1 - par, KT - 1)
                                if st == MAXT_STEP and (more or qc == 0):
                                    turn_max(u + 1)
                                if st == OUT_STEP and not (isinstance(u, int) and u == 0):
                                    turn_out(u - 1)

            steps(pe, step, BG, 2, BG - 2)
            values(NU - 1, 1, KT - 1)
            turn_out(NU - 1)

        @block.scalar
        def _(act):
            for par in range(2):
                act.wait_ge(shared.qkv_stored[par], 16 * QKV_STORES * NCH // 2)

            def step(k, par):
                n = 2 * k + par
                for qc in range(CPB):
                    u = CPB * n + qc
                    for st in range(KT):
                        need(act, pv_done, KT * u + st - NP_ + 1)
                        for h in range(HG):
                            act.wait_ge(s_done, HG * (KT * u + st) + h + 1)
                            act.activation(probs[st % NP_][:, h, :], s_exp[exp_bank[HG * st + h]][:, :], ACT.Exp, scale=SCALE)\
                                .then_inc(exp_done, 1)

            steps(act, step, BG, 2, BG - 2)

        @block.vector
        def _(dve):
            def item(kind, u, j):
                number, which = slots.at(kind, u, j)
                dve.wait_ge(filled, number + 1)
                return slot[which]

            def reduce(u, qc, j):
                dve.tensor_reduce(maxima[qc][:, j:j + 1], item("max", u, j)[:, :], AX_X, ALU.max).then_inc(emptied, 1)

            def take_max(u):
                need(dve, max_in, 16 * u)
                dve.tensor_copy(maxT[:, :], item("maxT", u, 0)[0:2 * NMAX, 0:P]).then_inc(emptied, 1)

            def take_out(u):
                dve.wait_ge(pv_done, KT * (u + 1))
                if not isinstance(u, int) or u > 0:
                    dve.wait_ge(filled, slots.at("out", u - 1, 0)[0] + 1)
                dve.tensor_copy(o_sb[:, :], o_ps[:, :]).then_inc(o_done, 1)

            def scale_out(u, qc, k_):
                if not isinstance(u, int) or u > 0:
                    dve.wait_ge(emptied, slots.at("out", u - 1, 0)[0] + 1)
                sums = item("out", u, 0)[:, 0:CH].rearrange("p (t h e) -> p t h e", t=TPC, h=HG)
                dve.reciprocal(inv[:, :, :], sums[:, :, :, HD]).then_inc(inv_done, 1)
                dve.wait_ge(inv_done, u + 1)
                need(dve, out_done[qc], 16 * k_)
                dve.tensor_tensor(o_out[qc][:, :, :, :], sums[:, :, :, 0:HD],
                                  inv.rearrange("p t (h e) -> p t h e", e=1).to_broadcast([P, TPC, HG, HD]),
                                  ALU.mult).then_inc(emptied, 1)

            for j in range(NMAX):
                reduce(0, 0, j)
            take_max(0)
            for j in range(2 * LEAD):
                reduce(1, 1, j)

            def step(k, par):
                n = 2 * k + par
                more = live(k, par, BG - 1)
                for qc in range(CPB):
                    u = CPB * n + qc
                    for st in range(KT):
                        for i in range(2):
                            j = 2 * (st + LEAD) + i
                            if j < NMAX:
                                if more or qc == 0:
                                    reduce(u + 1, 1 - qc, j)
                            elif more:
                                reduce(u + 2, qc, j - NMAX)
                            if i == 0 and st == 0 and not (isinstance(u, int) and u == 0):
                                take_out(u - 1)
                            if i == 0 and st == OUT_STEP and not (isinstance(u, int) and u == 0):
                                scale_out(u - 1, 1 - qc, (u - 1) // 2 if isinstance(u, int) else n - (1 - qc))
                            if i == 0 and st == MAXT_STEP and (more or qc == 0):
                                take_max(u + 1)

            steps(dve, step, BG, 2, BG - 2)
            take_out(NU - 1)
            scale_out(NU - 1, 1, BG - 1)


class Residual:

    def __init__(self, m, W, s, shared, x_dram, wo, row, gain):
        self.W, self.s, self.shared, self.x_dram, self.wo, self.row, self.gain = W, s, shared, x_dram, wo, row, gain
        self.att, self.x, self.badd, self.loaded = shared.att, shared.x, shared.badd, shared.residual_in[row]
        self.attT = m.sb("attT", [P, DC, CH])
        self.y = [m.sb(f"y{i}", [P, TPC, D]) for i in range(2)]
        self.stats, self.moments, self.rstd = m.sb("stats", [P, TPC + 1, 6]), m.sb("moments", [P, TPC, 2]), m.sb("rstd", [P, TPC])
        self.xhat = m.sb("xhat", [P, TPC, D])
        self.hT = [m.sb(f"hT{i}", [P, DC, CH]) for i in range(2)]
        self.turned = [m.ps(f"turned{c}", [P, CH]) for c in range(DC)]
        self.wo_ps = [m.ps(f"wo{i}", [P, 2 * D]) for i in range(TPC // 2)]
        (self.own, self.pool_own, self.attT_ps, self.attT_sb, self.wo_done, self.xb_done, self.y_done, self.stats_done,
         self.rstd_done, self.xhat_done, self.hT_ps, self.hT_sb) = (
            m.sem(n) for n in ("own", "pool_own", "attT_ps", "attT_sb", "wo_done", "xb_done", "y_done", "stats_done",
                               "rstd_done", "xhat_done", "hT_ps", "hT_sb"))

    def load(self, sp, k, par):
        n = 2 * k + par
        if isinstance(n, int) and n < 2:
            return
        sp.wait_ge(self.attT_ps, DC * (n - 1))
        sp.wait_ge(self.y_done, n - 1)
        self.shared.load_residual(sp, self.s, self.x_dram, self.row, k, par)

    def pool_add(self, pool, k, par):
        pool.wait_ge(self.loaded[par], RESIDUAL_LOADS * (k + 1))
        pool.tensor_tensor(self.x[par][:, :, :], self.x[par][:, :, :],
                           self.badd[par].rearrange("p (t d) -> p t d", t=1).to_broadcast([P, TPC, D]), ALU.add)\
            .then_inc(self.xb_done, 1)

    def pool_rstd(self, pool, k, par):
        n = 2 * k + par
        pool.wait_ge(self.stats_done, n + 1)
        need(pool, self.xhat_done, n)
        rstd_of(pool, self.moments, self.rstd, self.W["half"], self.pool_own, n + 1).then_inc(self.rstd_done, 1)

    def turn_att(self, pe, k, par):
        n = 2 * k + par
        pe.wait_ge(self.loaded[par], RESIDUAL_LOADS * (k + 1))
        need(pe, self.hT_sb, DC * (n - 1))
        turn(pe, self.turned, self.att[par], self.W["ident"], self.attT_ps)

    def turn_h(self, pe, k, par):
        n = 2 * k + par
        pe.wait_ge(self.xhat_done, n + 1)
        pe.wait_ge(self.attT_sb, DC * (min(n + 2, NCH) if isinstance(n, int) else n + 2))
        turn(pe, self.turned, self.xhat, self.W["ident"], self.hT_ps)

    def project(self, pe, k, par):
        n = 2 * k + par
        pe.wait_ge(self.attT_sb, DC * (n + 1))
        for t in range(TPC):
            if t % 2 == 0:
                need(pe, self.y_done, n)
            for c in range(DC):
                last = pe.matmul(self.wo_ps[t // 2][:, (t % 2) * D:(t % 2 + 1) * D],
                                 self.attT[:, c, t * P:(t + 1) * P], self.wo[:, c, :],
                                 start=(c == 0), stop=(c == DC - 1))
            if t % 2:
                last.then_inc(self.wo_done, 1)

    def take_att(self, act, k, par):
        n = 2 * k + par
        for c in range(DC):
            act.wait_ge(self.attT_ps, DC * n + c + 1)
            if c == 0:
                need(act, self.wo_done, 2 * n)
            act.activation(self.attT[:, c, :], self.turned[c][:, :], ACT.Copy).then_inc(self.attT_sb, 1)

    def take_h(self, act, k, par, used, count):
        n = 2 * k + par
        need(act, used, count)
        for c in range(DC):
            act.wait_ge(self.hT_ps, DC * n + c + 1)
            act.activation(self.hT[par][:, c, :], self.turned[c][:, :], ACT.Identity,
                           scale=self.W["col"][:, self.gain, c:c + 1],
                           bias=self.W["col"][:, self.gain + 1, c:c + 1]).then_inc(self.hT_sb, 1)

    def add_norm(self, dve, k, par, free):
        n = 2 * k + par
        dve.wait_ge(self.xb_done, n + 1)
        free(k, par)
        for i in range(TPC // 2):
            dve.wait_ge(self.wo_done, 2 * n + i + 1)
            last = dve.tensor_tensor(self.y[par][:, 2 * i:2 * i + 2, :],
                                     self.wo_ps[i].rearrange("p (t d) -> p t d", t=2),
                                     self.x[par][:, 2 * i:2 * i + 2, :], ALU.add)
        last.then_inc(self.y_done, 1)
        dve.wait_ge(self.y_done, n + 1)
        norm_stats(dve, self.y[par], self.stats, self.moments, self.own, n + 1).then_inc(self.stats_done, 1)
        dve.wait_ge(self.rstd_done, n + 1)
        need(dve, self.hT_ps, DC * n)
        normalize(dve, self.xhat, self.y[par], self.moments, self.rstd).then_inc(self.xhat_done, 1)


def chunk_view(x):
    return x.rearrange("b (c t p) d -> (b c) p t d", c=CPB, t=TPC)


def cross_q(nc, a, W, s, shared):
    col = W["col"]
    with ExitStack() as stack:
        m = Arena(nc, stack, "cq")
        r = Residual(m, W, s, shared, chunk_view(a["x"]), W["sa_wo"], 0, 2)
        full = [m.sb(f"full{i}", [P, DC, CH]) for i in range(2)]
        hi = [m.sb(f"hi{i}", [P, DC, CH], F32R) for i in range(2)]
        lo = [m.sb(f"lo{i}", [P, DC, CH], F32R) for i in range(2)]
        q_ps = [m.ps(f"q{i}", [P, CH]) for i in range(DC)]
        stored, q_done, hi_done, full_done, lo_done = (
            shared.cq_stored, m.sem("q_done"), m.sem("hi_done"), m.sem("full_done"), m.sem("lo_done"))
        y_stored = m.sems("y_stored", 2)
        block = stack.enter_context(nc.Block())

        @block.sync
        def _(sp):
            def step(k, par):
                n = 2 * k + par
                if live(k, par, NCH):
                    r.load(sp, k, par)
                k1, p1 = back(k, par, 1)
                if live(k1, p1, NCH):
                    n1 = 2 * k1 + p1
                    sp.wait_ge(r.y_done, n1 + 1)
                    sp.dma_start(s["x1"][n1], r.y[p1][:, :, :]).then_inc(y_stored[p1], 16)
                if isinstance(k, int) and n == NCH + 1:
                    for first in range(2):
                        sp.wait_ge(stored[first], CQ_STORES)
                    shared.load_cross(sp, s, 0, 0)
                k2, p2 = back(k, par, 3)
                if live(k2, p2, NCH):
                    n2 = 2 * k2 + p2
                    sp.wait_ge(hi_done, DC * (n2 + 1))
                    sp.wait_ge(lo_done, DC * (n2 + 1))
                    for part, src in enumerate((hi, lo)):
                        dst = s["cq"][part].rearrange("(b c g) r q t -> b q (g r) c t", b=B, c=DC)
                        sp.dma_start(dst[k2, p2], words(src[p2][:, :, :])).then_inc(stored[p2], 16)

            steps(sp, step, NCH + 3, 4, NCH)
            for par in range(2):
                sp.wait_ge(y_stored[par], 16 * NCH // 2)

        @block.gpsimd
        def _(pool):
            def step(k, par):
                if live(k, par, NCH):
                    r.pool_add(pool, k, par)
                k2, p2 = back(k, par, 2)
                if live(k2, p2, NCH):
                    n2 = 2 * k2 + p2
                    need(pool, stored[p2], CQ_STORES * k2)
                    for i in range(DC):
                        pool.wait_ge(hi_done, DC * n2 + i + 1)
                        pool.tensor_tensor(lo[p2][:, i, :], full[p2][:, i, :], hi[p2][:, i, :].bitcast(F32),
                                           ALU.subtract).then_inc(lo_done, 1)
                if live(k, par, NCH):
                    r.pool_rstd(pool, k, par)

            steps(pool, step, NCH + 2, 4, NCH)

        @block.tensor
        def _(pe):
            def step(k, par):
                k2, p2 = back(k, par, 2)
                for i in range(DC):
                    if live(k2, p2, NCH):
                        n2 = 2 * k2 + p2
                        pe.wait_ge(r.hT_sb, DC * (n2 + 1))
                        need(pe, full_done, DC * (n2 - 1) + i + 1)
                        for c in range(DC):
                            last = pe.matmul(q_ps[i][:, :], W["ca_wq"][:, c, i * P:(i + 1) * P], r.hT[p2][:, c, :],
                                             start=(c == 0), stop=(c == DC - 1))
                        last.then_inc(q_done, 1)
                    if i == 0 and live(k, par, NCH):
                        r.turn_att(pe, k, par)
                if live(k, par, NCH):
                    r.project(pe, k, par)
                k1, p1 = back(k, par, 1)
                if live(k1, p1, NCH):
                    r.turn_h(pe, k1, p1)

            steps(pe, step, NCH + 2, 4, NCH)

        @block.scalar
        def _(act):
            def step(k, par):
                if live(k, par, NCH):
                    r.take_att(act, k, par)
                k2, p2 = back(k, par, 2)
                if live(k2, p2, NCH):
                    n2 = 2 * k2 + p2
                    need(act, stored[p2], CQ_STORES * k2)
                    for i in range(DC):
                        act.wait_ge(full_done, DC * n2 + i + 1)
                        act.activation(hi[p2][:, i, :], full[p2][:, i, :], ACT.Copy).then_inc(hi_done, 1)
                k1, p1 = back(k, par, 1)
                if live(k1, p1, NCH):
                    r.take_h(act, k1, p1, q_done, DC * (2 * k1 + p1 - 1))

            steps(act, step, NCH + 2, 4, NCH)

        @block.vector
        def _(dve):
            def free(k, par):
                need(dve, y_stored[par], 16 * k)

            def step(k, par):
                k2, p2 = back(k, par, 2)
                if live(k2, p2, NCH):
                    n2 = 2 * k2 + p2
                    need(dve, lo_done, DC * (n2 - 1))
                    for i in range(DC):
                        dve.wait_ge(q_done, DC * n2 + i + 1)
                        dve.tensor_scalar(full[p2][:, i, :], q_ps[i][:, :], col[:, 9, i:i + 1], None,
                                          ALU.add).then_inc(full_done, 1)
                if live(k, par, NCH):
                    r.add_norm(dve, k, par, free)

            steps(dve, step, NCH + 2, 4, NCH)


def cross_attention(nc, a, W, s, shared):
    ident = W["ident"]
    UB = NG * CPB
    AHEAD = 3
    with ExitStack() as stack:
        m = Arena(nc, stack, "ca")
        q, k_rows, v, mask = shared.cq, shared.ck, shared.cv, shared.mask
        blocks, half_blocks = m.sb("blocks", [P, HG]), m.sb("half_blocks", [P, 2 * HG])
        kk = [m.sb(f"k{i}", [P, 2, HG, NKE], F32R) for i in range(NG)]
        probs = [m.sb(f"probs{i}", [P, TPC, HG, NK]) for i in range(2 * CPB)]
        maxima = [m.sb(f"maxima{i}", [P, TPC, HG]) for i in range(2)]
        probsT = [m.sb(f"probsT{i}", [P, HG, CH]) for i in range(2)]
        o_sb = m.sb("o_sb", [P, CH])
        inv = m.sb("inv", [P, TPC, HG])
        o_out = [m.sb(f"o_out{i}", [P, TPC, HG, HD]) for i in range(2)]
        s_ps = [m.ps(f"s{i}", [P, CH]) for i in range(TPC)]
        turned = [m.ps(f"turned{i}", [P, CH]) for i in range(2)]
        o_ps, oT = m.ps("o", [P, CH]), m.ps("oT", [P, CH])
        loads_in, out_done = shared.cross_in, m.sems("out_done", 2)
        zero, probsT_zero, own, blocks_sb, k_sb, scored, masked, reduced, centred, exp_done = (
            m.sem(n) for n in ("zero", "probsT_zero", "own", "blocks_sb", "k_sb", "scored", "masked", "reduced", "centred", "exp_done"))
        turned_done, probsT_done, pv_done, o_done, oT_done, inv_done, out_ready = (
            m.sem(n) for n in ("turned_done", "probsT_done", "pv_done", "o_done", "oT_done", "inv_done", "out_ready"))
        block = stack.enter_context(nc.Block())

        def batches(eng, step):
            step(0)
            with eng.Fori(1, B - 1) as b:
                step(b)
            step(B - 1)

        def there(b, unit):
            return not isinstance(b, int) or 0 <= b * UB + unit < NU

        @block.sync
        def _(sp):
            def store(b, unit):
                qc = unit % CPB
                sp.wait_ge(out_ready, UB * b + unit + 1)
                dst = s["attn"][NG * b + unit // CPB, qc]
                sp.dma_start(dst.rearrange("t p e -> p t e"), o_out[qc].rearrange("p t h e -> p t (h e)"))\
                    .then_inc(out_done[qc], 16)

            for g in (1, 2):
                shared.load_cross(sp, s, 0, g)
            for par in range(2):
                sp.wait_ge(shared.cq_stored[par], CQ_STORES * NCH // 2)

            def step(b):
                for unit in range(UB):
                    qc = unit % CPB
                    if qc == 0 and there(b, unit + 3 * CPB):
                        g = unit // CPB + 3
                        need(sp, pv_done, UB * b + unit)
                        shared.load_cross(sp, s, b + g // NG, g % NG)
                    if there(b, unit - 1):
                        store(b, unit - 1)
                    if isinstance(b, int) and b == B - 1 and unit // CPB == 2:
                        sp.wait_ge(out_done[qc], 16 * NG)
                        shared.load_residual(sp, s, s["x1"], 1, 0, qc)

            batches(sp, step)
            store(B - 1, UB - 1)
            for qc in range(CPB):
                sp.wait_ge(out_done[qc], 16 * BG)

        @block.gpsimd
        def _(pool):
            for g in range(NG):
                pool.memset(words(kk[g][:, :, :, NK:NKE]), 0.0).then_inc(zero, 1)
                pool.wait_ge(zero, g + 1)
            pool.wait_ge(blocks_sb, 1)

            def spread(b, g):
                pool.wait_ge(loads_in[g], CROSS_LOADS * (b + 1))
                need(pool, scored, TPC * CPB * (NG * b + g - NG + 1))
                for part in range(2):
                    pool.tensor_tensor(kk[g][:, part, :, 0:NK],
                                       k_rows[g][:, part, :].bitcast(F32).rearrange("p (h k) -> p h k", h=1)
                                       .to_broadcast([P, HG, NK]),
                                       blocks.rearrange("p (h k) -> p h k", k=1).to_broadcast([P, HG, NK]),
                                       ALU.mult).then_inc(k_sb, 1)

            def centre(b, unit):
                u, buf = UB * b + unit, unit % (2 * CPB)
                pool.wait_ge(reduced, u + 1)
                tile = probs[buf].rearrange("p t h k -> p (t h) k")
                pool.tensor_tensor(tile, tile, maxima[unit % 2].rearrange("p t (h k) -> p (t h) k", k=1)
                                   .to_broadcast([P, TPC * HG, NK]), ALU.subtract).then_inc(centred, 1)

            spread(0, 0)
            centre(0, 0)
            spread(0, 1)
            centre(0, 1)

            def step(b):
                for unit in range(UB):
                    if unit % CPB == 0 and there(b, unit + 4):
                        g = unit // CPB + 2
                        spread(b + g // NG, g % NG)
                    if there(b, unit + 2):
                        centre(b, unit + 2)

            batches(pool, step)

        @block.tensor
        def _(pe):
            def scores(b, unit, t):
                g, qc, u = unit // CPB % NG, unit % CPB, UB * b + unit
                if qc == 0 and t == 0:
                    pe.wait_ge(k_sb, 2 * (NG * b + unit // CPB + 1))
                need(pe, masked, TPC * (u - 1) + t + 1)
                for part in range(2):
                    last = pe.matmul(s_ps[t][:, 0:HG * NKE], q[g][:, qc, t * P:(t + 1) * P],
                                     kk[g][:, part, :, :].rearrange("p h k -> p (h k)"),
                                     start=(part == 0), stop=(part == 1))
                last.then_inc(scored, 1)

            def turn_probs(b, unit, h):
                u = UB * b + unit
                if h == 0:
                    pe.wait_ge(exp_done, u + 1)
                need(pe, probsT_done, HG * u + h - 1)
                for t in range(TPC):
                    last = pe.transpose(turned[h % 2][0:NK, t * P:(t + 1) * P],
                                        probs[unit % (2 * CPB)][:, t, h, :], ident[:, :])
                last.then_inc(turned_done, 1)

            def values(b, unit):
                g, qc, u = unit // CPB % NG, unit % CPB, UB * b + unit
                need(pe, o_done, u)
                pe.wait_ge(probsT_done, HG * (u + 1))
                for h in range(HG):
                    last = pe.matmul(o_ps[h * VW:(h + 1) * VW, :], v[g][:, h, :], probsT[qc][:, h, :],
                                     start=True, stop=True, tile_position=(0, h * VW))
                last.then_inc(pv_done, 1)

            def turn_out(b, unit):
                u = UB * b + unit
                pe.wait_ge(o_done, u + 1)
                need(pe, out_ready, u)
                for t in range(TPC):
                    last = pe.transpose(oT[:, t * P:(t + 1) * P], o_sb[:, t * P:(t + 1) * P], ident[:, :])
                last.then_inc(oT_done, 1)

            for unit in range(AHEAD):
                for t in range(TPC):
                    scores(0, unit, t)

            def step(b):
                for unit in range(UB):
                    for h in range(HG):
                        if there(b, unit + AHEAD):
                            scores(b, unit + AHEAD, h)
                        turn_probs(b, unit, h)
                        if h == 0 and there(b, unit - 1):
                            values(b, unit - 1)
                        if h == 3 and there(b, unit - 1):
                            turn_out(b, unit - 1)

            batches(pe, step)
            values(B - 1, UB - 1)
            turn_out(B - 1, UB - 1)

        @block.scalar
        def _(act):
            def exponentials(b, unit):
                u = UB * b + unit
                act.wait_ge(centred, u + 1)
                tile = probs[unit % (2 * CPB)].rearrange("p t h k -> p (t h k)")
                act.activation(tile, tile, ACT.Exp, scale=SCALE).then_inc(exp_done, 1)

            def take_out(b, unit):
                u = UB * b + unit
                act.wait_ge(pv_done, u + 1)
                need(act, oT_done, u)
                act.activation(o_sb[:, :], o_ps[:, :], ACT.Copy).then_inc(o_done, 1)

            act.wait_ge(probsT_zero, 2)
            exponentials(0, 0)

            def step(b):
                for unit in range(UB):
                    u = UB * b + unit
                    need(act, pv_done, u - 1)
                    for h in range(HG):
                        act.wait_ge(turned_done, HG * u + h + 1)
                        act.activation(probsT[unit % 2][0:NK, h, :], turned[h % 2][0:NK, :], ACT.Copy)\
                            .then_inc(probsT_done, 1)
                        if h == 1 and there(b, unit - 1):
                            take_out(b, unit - 1)
                        if h == 0 and there(b, unit + 1):
                            exponentials(b, unit + 1)

            batches(act, step)
            take_out(B - 1, UB - 1)

        @block.vector
        def _(dve):
            dve.tensor_reduce(half_blocks[:, :], ident.rearrange("p (x e) -> p x e", e=HD), AX_X, ALU.max).then_inc(own, 1)
            dve.wait_ge(own, 1)
            dve.tensor_tensor(blocks[:, :], half_blocks[:, 0:HG], half_blocks[:, HG:2 * HG], ALU.max).then_inc(blocks_sb, 1)

            for par in range(2):
                dve.wait_ge(shared.cq_stored[par], CQ_STORES * NCH // 2)
            for i in range(2):
                dve.memset(probsT[i][:, :, :], 0.0).then_inc(probsT_zero, 1)

            def add_mask(b, unit, t):
                g, u = unit // CPB % NG, UB * b + unit
                dve.wait_ge(scored, TPC * u + t + 1)
                if t == 0:
                    need(dve, turned_done, HG * (u - 2 * CPB + 1))
                dve.tensor_tensor(probs[unit % (2 * CPB)][:, t, :, :],
                                  s_ps[t][:, 0:HG * NKE].rearrange("p (h k) -> p h k", h=HG)[:, :, 0:NK],
                                  mask[g].rearrange("p (h k) -> p h k", h=1).to_broadcast([P, HG, NK]),
                                  ALU.add).then_inc(masked, 1)

            def reduce(b, unit):
                u = UB * b + unit
                dve.wait_ge(masked, TPC * (u + 1))
                need(dve, centred, u - 1)
                dve.tensor_reduce(maxima[unit % 2][:, :, :], probs[unit % (2 * CPB)][:, :, :, :], AX_X, ALU.max)\
                    .then_inc(reduced, 1)

            def scale_out(b, unit):
                u, qc = UB * b + unit, unit % CPB
                dve.wait_ge(oT_done, u + 1)
                need(dve, out_ready, u)
                sums = oT.rearrange("p (t h e) -> p t h e", t=TPC, h=HG)
                dve.reciprocal(inv[:, :, :], sums[:, :, :, HD]).then_inc(inv_done, 1)
                dve.wait_ge(inv_done, u + 1)
                need(dve, out_done[qc], 16 * (NG * b + unit // CPB))
                dve.tensor_tensor(o_out[qc][:, :, :, :], sums[:, :, :, 0:HD],
                                  inv.rearrange("p t (h e) -> p t h e", e=1).to_broadcast([P, TPC, HG, HD]),
                                  ALU.mult).then_inc(out_ready, 1)

            for unit in range(AHEAD):
                for t in range(TPC):
                    add_mask(0, unit, t)
                reduce(0, unit)

            def step(b):
                for unit in range(UB):
                    if there(b, unit + AHEAD):
                        for t in range(TPC):
                            add_mask(b, unit + AHEAD, t)
                        reduce(b, unit + AHEAD)
                    if there(b, unit - 1):
                        scale_out(b, unit - 1)

            batches(dve, step)
            scale_out(B - 1, UB - 1)


def mlp(nc, a, W, s, shared, out):
    with ExitStack() as stack:
        m = Arena(nc, stack, "mlp")
        r = Residual(m, W, s, shared, s["x1"], W["ca_wo"], 1, 4)
        row2 = [m.sb(f"row2_{i}", [P, D]) for i in range(2)]
        yb = [m.sb(f"yb{i}", [P, TPC, D]) for i in range(2)]
        hT_hi, hT_lo = ([m.sb(f"hT_{part}{i}", [P, DC, CH], F32R) for i in range(2)] for part in ("hi", "lo"))
        w1 = [shared.rows[0][:, part].rearrange("p (c h) t -> p c (h t)", c=DC) for part in range(2)]
        w2 = [shared.rows[1][:, part].rearrange("p h (x d) -> p (h x) d", d=D) for part in range(2)]
        hidden = [shared.rows[2 + part].rearrange("p c h t -> p (c h) t") for part in range(2)]
        gelu = [m.sb(f"gelu{i}", [P, CH]) for i in range(4)]
        res = [m.sb(f"res{i}", [P, TPC, D]) for i in range(2)]
        w1_ps = [m.ps(f"w1_{i}", [P, CH]) for i in range(2)]
        w2_ps = [m.ps(f"w2_{i}", [P, 2 * D]) for i in range(2)]
        row_in, stored = m.sems("row_in", 2), m.sems("stored", 2)
        w_hi, w_lo, hT_hi_done, hT_lo_done, gelu_done, hidden_lo_done = (
            m.sem(n) for n in ("w_hi", "w_lo", "hT_hi_done", "hT_lo_done", "gelu_done", "hidden_lo_done"))
        w1_done, hidden_done, w2_done, yb_done, res_done = (
            m.sem(n) for n in ("w1_done", "hidden_done", "w2_done", "yb_done", "res_done"))
        out_dram = chunk_view(out)
        block = stack.enter_context(nc.Block())

        @block.sync
        def _(sp):
            def step(k, par):
                if live(k, par, NCH):
                    r.load(sp, k, par)
                    need(sp, yb_done, 2 * k + par - 1)
                    sp.dma_start(row2[par][:, :], s["badd"][k][:, 2 * D:3 * D].to_broadcast([P, D]))\
                        .then_inc(row_in[par], 16)
                k2, p2 = back(k, par, 3)
                if live(k2, p2, NCH):
                    n2 = 2 * k2 + p2
                    sp.wait_ge(res_done, 2 * (n2 + 1))
                    sp.dma_start(out_dram[n2], res[p2][:, :, :]).then_inc(stored[p2], 16)

            steps(sp, step, NCH + 3, 4, NCH)
            for par in range(2):
                sp.wait_ge(stored[par], 16 * NCH // 2)

        @block.gpsimd
        def _(pool):
            def step(k, par):
                n = 2 * k + par
                r.pool_add(pool, k, par)
                r.pool_rstd(pool, k, par)
                pool.wait_ge(row_in[par], 16 * (k + 1))
                need(pool, res_done, 2 * (n - 1))
                pool.tensor_tensor(yb[par][:, :, :], r.y[par][:, :, :],
                                   row2[par].rearrange("p (t d) -> p t d", t=1).to_broadcast([P, TPC, D]),
                                   ALU.add).then_inc(yb_done, 1)

            steps(pool, step, NCH, 2, NCH)

        @block.tensor
        def _(pe):
            def step(k, par):
                if live(k, par, NCH):
                    r.turn_att(pe, k, par)
                k2, p2 = back(k, par, 2)
                if live(k2, p2, NCH):
                    up(2 * k2 + p2, p2)
                if live(k, par, NCH):
                    r.project(pe, k, par)
                k1, p1 = back(k, par, 1)
                if live(k1, p1, NCH):
                    r.turn_h(pe, k1, p1)
                if live(k2, p2, NCH):
                    down(2 * k2 + p2, p2)

            def up(n, par):
                if isinstance(n, int) and n == 0:
                    pe.wait_ge(w_lo, 1)
                pe.wait_ge(hT_lo_done, DC * (n + 1))
                for f in range(FC):
                    need(pe, gelu_done, FC * n + f - 1)
                    for c in range(DC):
                        for left, right in ((0, hT_hi), (0, hT_lo), (1, hT_hi)):
                            last = pe.matmul(w1_ps[f % 2][:, :], w1[left][:, c, f * P:(f + 1) * P], right[par][:, c, :],
                                             start=(c == 0 and right is hT_hi and left == 0),
                                             stop=(c == DC - 1 and left == 1))
                    last.then_inc(w1_done, 1)

            def down(n, par):
                if isinstance(n, int) and n == 0:
                    pe.wait_ge(w_lo, 2)
                pe.wait_ge(hidden_lo_done, FC * (n + 1))
                for t in range(TPC):
                    if t % 2 == 0:
                        need(pe, res_done, 2 * (n - 1) + t // 2 + 1)
                    for f in range(FC):
                        for i, (left, right) in enumerate(((0, 0), (0, 1), (1, 0))):
                            last = pe.matmul(w2_ps[t // 2][:, (t % 2) * D:(t % 2 + 1) * D],
                                             hidden[left][:, f, t * P:(t + 1) * P], w2[right][:, f, :],
                                             start=(f == 0 and i == 0), stop=(f == FC - 1 and i == 2))
                    if t % 2:
                        last.then_inc(w2_done, 1)

            steps(pe, step, NCH + 2, 4, NCH)

        @block.scalar
        def _(act):
            def weight_hi(parts, full):
                act.activation(parts[0][:, :, :], full[:, :, :], ACT.Copy).then_inc(w_hi, 1)

            def step(k, par):
                if live(k, par, NCH):
                    r.take_att(act, k, par)
                if isinstance(k, int) and k == 0:
                    weight_hi(*((w1, W["w1"]) if par == 0 else (w2, W["w2"])))
                k1, p1 = back(k, par, 2)
                if live(k1, p1, NCH):
                    n1 = 2 * k1 + p1
                    need(act, w2_done, 2 * n1)
                    for f in range(FC):
                        act.wait_ge(w1_done, FC * n1 + f + 1)
                        need(act, hidden_lo_done, FC * n1 + f - 3)
                        act.activation(gelu[f % 4][:, :], w1_ps[f % 2][:, :], ACT.Gelu,
                                       bias=W["b1"][:, f:f + 1]).then_inc(gelu_done, 1)
                        act.wait_ge(gelu_done, FC * n1 + f + 1)
                        act.activation(hidden[0][:, f, :], gelu[f % 4][:, :], ACT.Copy).then_inc(hidden_done, 1)
                kh, ph = back(k, par, 1)
                if live(kh, ph, NCH):
                    nh = 2 * kh + ph
                    r.take_h(act, kh, ph, hT_lo_done, DC * (nh - 1))
                    need(act, w1_done, FC * (nh - 1))
                    for c in range(DC):
                        act.wait_ge(r.hT_sb, DC * nh + c + 1)
                        act.activation(hT_hi[ph][:, c, :], r.hT[ph][:, c, :], ACT.Copy).then_inc(hT_hi_done, 1)

            steps(act, step, NCH + 2, 4, NCH)

        @block.vector
        def _(dve):
            def free(k, par):
                need(dve, yb_done, 2 * k + par - 1)

            def weight_lo(parts, full, which):
                dve.wait_ge(w_hi, which + 1)
                dve.tensor_tensor(parts[1][:, :, :], full[:, :, :], parts[0][:, :, :].bitcast(F32), ALU.subtract)\
                    .then_inc(w_lo, 1)

            def step(k, par):
                k1, p1 = back(k, par, 2)
                n1 = 2 * k1 + p1
                if live(k1, p1, NCH):
                    need(dve, w2_done, 2 * n1)
                    for f in range(FC):
                        dve.wait_ge(hidden_done, FC * n1 + f + 1)
                        dve.tensor_tensor(hidden[1][:, f, :], gelu[f % 4][:, :], hidden[0][:, f, :].bitcast(F32),
                                          ALU.subtract).then_inc(hidden_lo_done, 1)
                kh, ph = back(k, par, 1)
                if live(kh, ph, NCH):
                    nh = 2 * kh + ph
                    need(dve, w1_done, FC * (nh - 1))
                    for c in range(DC):
                        dve.wait_ge(hT_hi_done, DC * nh + c + 1)
                        dve.tensor_tensor(hT_lo[ph][:, c, :], r.hT[ph][:, c, :], hT_hi[ph][:, c, :].bitcast(F32),
                                          ALU.subtract).then_inc(hT_lo_done, 1)
                if live(k, par, NCH):
                    r.add_norm(dve, k, par, free)
                if isinstance(k, int) and k == 0:
                    weight_lo(*((w1, W["w1"]) if par == 0 else (w2, W["w2"])), par)
                if live(k1, p1, NCH):
                    dve.wait_ge(yb_done, n1 + 1)
                    need(dve, stored[p1], 16 * k1)
                    for i in range(TPC // 2):
                        dve.wait_ge(w2_done, 2 * n1 + i + 1)
                        dve.tensor_tensor(res[p1][:, 2 * i:2 * i + 2, :],
                                          w2_ps[i].rearrange("p (t d) -> p t d", t=2),
                                          yb[p1][:, 2 * i:2 * i + 2, :], ALU.add).then_inc(res_done, 1)

            steps(dve, step, NCH + 2, 4, NCH)


def build(nc, a, out):
    def scratch(name, shape, dt=F32):
        return nc.dram_tensor(name, shape, dt, kind="Internal").ap()

    qk = scratch("qk_parts", [2, 2, BG, GW, CPB, CH])
    s = {
        "qk": qk,
        "v": scratch("v_ones", [BG, P, KT, HG * VW]),
        "ck": scratch("ctx_k_parts", [2, BG * GW, NK]),
        "cv": scratch("ctx_v", [BG, NK, HG * VW]),
        "cmask": scratch("ctx_mask", [BG, 1, HG * NK]),
        "cq": scratch("cross_q_parts", [2, BG, GW, CPB, CH]),
        "badd": scratch("rows", [B, 1, 3 * D]),
        "attn": scratch("attn", [BG, CPB, TPC, P, GW]),
        "x1": scratch("x1", [NCH, P, TPC, D]),
    }
    with ExitStack() as stack:
        def sb(name, shape):
            return stack.enter_context(nc.sbuf_tensor(name, shape, F32))

        W = {n: sb(n, [P, DC, D]) for n in ("sa_wq", "sa_wk", "sa_wv", "sa_wo", "ca_wq", "ca_wo")}
        W |= {"w1": sb("w1", [P, DC, FF]), "w2": sb("w2", [P, FC, D]), "b1": sb("b1", [P, FC]),
              "col": sb("col", [P, 10, DC]), "ident": sb("ident", [P, P]), "half": sb("half", [P, 2, TPC])}
        shared = Shared(Arena(nc, stack, "shared"))
        setup(nc, a, W, s, shared)
        self_qkv(nc, a, W, s, shared)
        self_attention(nc, a, W, s, shared)
        cross_q(nc, a, W, s, shared)
        cross_attention(nc, a, W, s, shared)
        mlp(nc, a, W, s, shared, out)


_INS = {"x": "x", "cond_1024": "cond", "ctx_1024": "ctx", "mask_BxS2_ik0": "mask"}
_WEIGHTS = ["ln1_g", "ln1_b", "ln3_g", "ln3_b", "ln2_g", "ln2_b", "sa_wq", "sa_bq", "sa_wk", "sa_bk", "sa_wv", "sa_bv",
            "sa_wo", "sa_bo", "ca_wq", "ca_bq", "ca_wk", "ca_bk", "ca_wv", "ca_bv", "ca_wo", "ca_bo", "tp_w", "tp_b",
            "w1", "b1", "w2", "b2"]


def kernel(**inputs):
    import numpy as np
    import concourse.bacc as bacc
    from concourse.bass_utils import run_bass_kernel_spmd

    nc = bacc.Bacc("TRN2", target_bir_lowering=False, num_devices=1)
    arrays, args = {}, {}
    for name, short in (_INS | {f"L0_xcond_{w}": w for w in _WEIGHTS}).items():
        v = np.ascontiguousarray(inputs[name])
        arrays[f"in_{short}"] = v
        args[short] = nc.dram_tensor(f"in_{short}", v.shape, mybir.dt.from_np(v.dtype), kind="ExternalInput").ap()
    out = nc.dram_tensor("out", (B, T, D), F32, kind="ExternalOutput").ap()
    with nc.allow_non_contiguous_dma(reason="a few short vectors are loaded as columns"):
        build(nc, args, out)
    r = run_bass_kernel_spmd(nc, [arrays], core_ids=[0])
    return r.results[0]["out"]
```
